# Optimizing a Trainium2 kernel written in Bass

```python
import numpy as np
import jax
import jax.numpy as jnp

def _softmax(x, axis=-1):
    return jax.nn.softmax(x, axis=axis)

def _gelu(x):
    return jax.nn.gelu(x, approximate=True)

def _silu(x):
    return jax.nn.silu(x)

def _sigmoid(x):
    return jax.nn.sigmoid(x)

def _layernorm(x, axis=-1, eps=1e-05):
    m = jnp.mean(x, axis=axis, keepdims=True)
    v = jnp.var(x, axis=axis, keepdims=True)
    return (x - m) / jnp.sqrt(v + eps)

def _scatter_add(tgt, idx, src, axis=0):
    return tgt.at[idx].add(src)

def _segment_sum(src, seg, n):
    return jax.ops.segment_sum(src, seg, n)
kernel_name = 'mk_flamingo_gated_d1_seqx_r2_b7317b'

def setup_inputs(seed: int=0):
    np.random.seed(seed)
    _w = jnp.asarray

    def _rec_inputs():
        import jax
        import jax.numpy as jnp
        _rk = jax.random.key(seed)
        x = 7.22e-05 + 1 * jax.random.normal(jax.random.fold_in(_rk, 1), (16, 224, 512), jnp.float32)
        _lenS = 224 - jax.random.randint(jax.random.fold_in(_rk, 7), (16,), 0, max(1, 224 // 4) + 1, jnp.int32)
        _lenS2 = 750 - jax.random.randint(jax.random.fold_in(_rk, 8), (16,), 0, max(1, 750 // 4) + 1, jnp.int32)
        _ctx_1024P = jax.random.normal(jax.random.fold_in(_rk, 11), (16, 16, 512), jnp.float32)
        _ctx_1024c = jax.random.dirichlet(jax.random.fold_in(_rk, 511), 0.3 * jnp.ones((16,), jnp.float32), (16, 750))
        _ctx_1024t = jnp.einsum('bsk,bkd->bsd', _ctx_1024c, _ctx_1024P)
        _ctx_1024t = _ctx_1024t * jax.lax.rsqrt(jnp.mean(jnp.square(_ctx_1024t)) + 1e-12) * 0.953939
        ctx_1024 = 4.13588e-05 + 0.999923 * (_ctx_1024t + 0.3 * jax.random.normal(jax.random.fold_in(_rk, 611), (16, 750, 512), jnp.float32))
        _ctxb_2048x32P = jax.random.normal(jax.random.fold_in(_rk, 12), (16, 16, 32), jnp.float32)
        _ctxb_2048x32c = jax.random.dirichlet(jax.random.fold_in(_rk, 512), 0.3 * jnp.ones((16,), jnp.float32), (16, 750))
        _ctxb_2048x32t = jnp.einsum('bsk,bkd->bsd', _ctxb_2048x32c, _ctxb_2048x32P)
        _ctxb_2048x32t = _ctxb_2048x32t * jax.lax.rsqrt(jnp.mean(jnp.square(_ctxb_2048x32t)) + 1e-12) * 0.953939
        ctxb_2048x32 = 0.000843197 + 0.998132 * (_ctxb_2048x32t + 0.3 * jax.random.normal(jax.random.fold_in(_rk, 612), (16, 750, 32), jnp.float32))
        _g = jax.random.normal(jax.random.fold_in(_rk, 9001), (2, 1), jnp.float32)
        _g = jnp.sign(_g) * jnp.maximum(jnp.abs(_g), 1.0) + (_g == 0) * 1.0
        g_xattn = _g[0]
        g_ffn = _g[1]
        return (x, ctx_1024, ctxb_2048x32, g_xattn, g_ffn)
    x, ctx_1024, ctxb_2048x32, g_xattn, g_ffn = _rec_inputs()

    def _L0_xattn_setup():
        import jax, jax.numpy as jnp
        import numpy as np
        B, L, D, H, NF = (4, 1024, 512, 16, 32)
        THRESHOLD = 0.1
        key = jax.random.key(seed)
        ks = jax.random.split(key, 12)
        s = 1.0 / np.sqrt(D)
        return {'q_x': jax.random.normal(ks[0], (B, L, D), jnp.float32), 'k_x': jax.random.normal(ks[1], (B, L, D), jnp.float32), 'v_x': jax.random.normal(ks[2], (B, L, D), jnp.float32), 'energy_coeffs': jax.random.normal(ks[3], (B, L, NF), jnp.float32), 'Wq': jax.random.normal(ks[4], (D, D), jnp.float32) * s, 'bq': jnp.zeros((D,), jnp.float32), 'Wk': jax.random.normal(ks[5], (D, D), jnp.float32) * s, 'bk': jnp.zeros((D,), jnp.float32), 'Wv': jax.random.normal(ks[6], (D, D), jnp.float32) * s, 'bv': jnp.zeros((D,), jnp.float32), 'Wo': jax.random.normal(ks[7], (D, D), jnp.float32) * s, 'bo': jnp.zeros((D,), jnp.float32)}
    _L0_xattn_all = _L0_xattn_setup()
    _L0_xattn_in = {k: v for k, v in _L0_xattn_all.items() if k in ('Wq', 'bq', 'Wk', 'bk', 'Wv', 'bv', 'Wo', 'bo')}
    del _L0_xattn_all

    def _L0_ffn_setup():
        import jax, jax.numpy as jnp
        import numpy as np
        HIDDEN = 512
        N_ROUTED = 16
        N_SHARED = 2
        TOP_K = 2
        MID_R = HIDDEN // 4
        MID_S = HIDDEN // 2
        key = jax.random.key(seed)
        ks = jax.random.split(key, 8)
        s = 0.02
        return {'x': jax.random.normal(ks[0], (2, 512, HIDDEN), dtype=jnp.float32), 'router_w': jax.random.normal(ks[1], (HIDDEN, N_ROUTED), dtype=jnp.float32) * s, 'wg_r': jax.random.normal(ks[2], (N_ROUTED, HIDDEN, MID_R), dtype=jnp.float32) * s, 'wu_r': jax.random.normal(ks[3], (N_ROUTED, HIDDEN, MID_R), dtype=jnp.float32) * s, 'wd_r': jax.random.normal(ks[4], (N_ROUTED, MID_R, HIDDEN), dtype=jnp.float32) * s, 'wg_s': jax.random.normal(ks[5], (N_SHARED, HIDDEN, MID_S), dtype=jnp.float32) * s, 'wu_s': jax.random.normal(ks[6], (N_SHARED, HIDDEN, MID_S), dtype=jnp.float32) * s, 'wd_s': jax.random.normal(ks[7], (N_SHARED, MID_S, HIDDEN), dtype=jnp.float32) * s}
    _L0_ffn_all = _L0_ffn_setup()
    _L0_ffn_in = {k: v for k, v in _L0_ffn_all.items() if k in ('router_w', 'wg_r', 'wu_r', 'wd_r', 'wg_s', 'wu_s', 'wd_s')}
    del _L0_ffn_all
    return {'x': x, 'ctx_1024': ctx_1024, 'ctxb_2048x32': ctxb_2048x32, 'g_xattn': g_xattn, 'g_ffn': g_ffn, 'L0_xattn_Wq': _L0_xattn_in['Wq'], 'L0_xattn_bq': _L0_xattn_in['bq'], 'L0_xattn_Wk': _L0_xattn_in['Wk'], 'L0_xattn_bk': _L0_xattn_in['bk'], 'L0_xattn_Wv': _L0_xattn_in['Wv'], 'L0_xattn_bv': _L0_xattn_in['bv'], 'L0_xattn_Wo': _L0_xattn_in['Wo'], 'L0_xattn_bo': _L0_xattn_in['bo'], 'L0_ffn_router_w': _L0_ffn_in['router_w'], 'L0_ffn_wg_r': _L0_ffn_in['wg_r'], 'L0_ffn_wu_r': _L0_ffn_in['wu_r'], 'L0_ffn_wd_r': _L0_ffn_in['wd_r'], 'L0_ffn_wg_s': _L0_ffn_in['wg_s'], 'L0_ffn_wu_s': _L0_ffn_in['wu_s'], 'L0_ffn_wd_s': _L0_ffn_in['wd_s']}

def reference(x, ctx_1024, ctxb_2048x32, g_xattn, g_ffn, L0_xattn_Wq, L0_xattn_bq, L0_xattn_Wk, L0_xattn_bk, L0_xattn_Wv, L0_xattn_bv, L0_xattn_Wo, L0_xattn_bo, L0_ffn_router_w, L0_ffn_wg_r, L0_ffn_wu_r, L0_ffn_wd_r, L0_ffn_wg_s, L0_ffn_wu_s, L0_ffn_wd_s):
    import jax
    import jax.numpy as jnp

    def _L0_xattn_ref(q_x, k_x, v_x, energy_coeffs, Wq, bq, Wk, bk, Wv, bv, Wo, bo):
        import jax, jax.numpy as jnp
        import numpy as np
        B, L, D, H, NF = (4, 1024, 512, 16, 32)
        THRESHOLD = 0.1
        Bq, Lq, Dm = q_x.shape
        Dh = Dm // H
        Q = (q_x @ Wq + bq).reshape(Bq, Lq, H, Dh).transpose(0, 2, 1, 3)
        K = (k_x @ Wk + bk).reshape(Bq, -1, H, Dh).transpose(0, 2, 1, 3)
        V = (v_x @ Wv + bv).reshape(Bq, -1, H, Dh).transpose(0, 2, 1, 3)
        scores = jnp.einsum('bhqd,bhkd->bhqk', Q, K) / jnp.sqrt(jnp.float32(Dh))
        energy = jnp.abs(energy_coeffs).mean(axis=-1)
        energy = energy / (energy.max(axis=-1, keepdims=True) + 1e-08)
        gate = (energy > THRESHOLD).astype(scores.dtype) * 0.9 + 0.1
        scores = scores * gate[:, None, None, :]
        attn = jax.nn.softmax(scores, axis=-1)
        attn = jnp.nan_to_num(attn, nan=0.0)
        out = jnp.einsum('bhqk,bhkd->bhqd', attn, V)
        out = out.transpose(0, 2, 1, 3).reshape(Bq, Lq, Dm)
        return out @ Wo + bo

    def _L0_ffn_ref(x, router_w, wg_r, wu_r, wd_r, wg_s, wu_s, wd_s):
        import jax, jax.numpy as jnp
        import numpy as np
        HIDDEN = 512
        N_ROUTED = 16
        N_SHARED = 2
        TOP_K = 2
        MID_R = HIDDEN // 4
        MID_S = HIDDEN // 2
        orig_shape = x.shape
        flat = x.reshape(-1, orig_shape[-1])
        gs = jnp.einsum('td,ndm->tnm', flat, wg_s)
        us = jnp.einsum('td,ndm->tnm', flat, wu_s)
        out = jnp.einsum('tnm,nmd->td', jax.nn.silu(gs) * us, wd_s)
        logits = (flat @ router_w).astype(jnp.float32)
        probs = jax.nn.softmax(logits, axis=-1)
        weights, indices = jax.lax.top_k(probs, TOP_K)
        weights = weights / (weights.sum(axis=-1, keepdims=True) + 1e-09)
        weights = weights.astype(x.dtype)
        comb = jnp.sum(jax.nn.one_hot(indices, N_ROUTED, dtype=x.dtype) * weights[..., None], axis=1)
        g = jnp.einsum('td,edm->tem', flat, wg_r)
        u = jnp.einsum('td,edm->tem', flat, wu_r)
        h = jax.nn.silu(g) * u
        h = h * comb[:, :, None]
        out = out + jnp.einsum('tem,emd->td', h, wd_r)
        return out.reshape(orig_shape)
    x = x + jnp.tanh(g_xattn[0]) * _L0_xattn_ref(_layernorm(x, axis=-1), ctx_1024, ctx_1024, ctxb_2048x32, L0_xattn_Wq, L0_xattn_bq, L0_xattn_Wk, L0_xattn_bk, L0_xattn_Wv, L0_xattn_bv, L0_xattn_Wo, L0_xattn_bo)
    x = x + jnp.tanh(g_ffn[0]) * _L0_ffn_ref(_layernorm(x, axis=-1), L0_ffn_router_w, L0_ffn_wg_r, L0_ffn_wu_r, L0_ffn_wd_r, L0_ffn_wg_s, L0_ffn_wu_s, L0_ffn_wd_s)
    return x

_drawn_inputs = setup_inputs


def setup_inputs(seed=0):
    import zlib

    import numpy as np

    out = dict(_drawn_inputs(seed))
    spreads = {'L0_xattn_bq': (0.0, 0.523),
     'L0_xattn_bk': (0.0, 0.8),
     'L0_xattn_bv': (0.0, 0.1),
     'L0_xattn_bo': (0.0, 0.1)}
    factors = {'L0_ffn_router_w': 3.986, 'L0_ffn_wg_r': 3.818, 'L0_ffn_wu_r': 3.738, 'L0_ffn_wd_r': 3.738}
    for name, (base, spread) in spreads.items():
        noise = np.random.default_rng([zlib.crc32(name.encode()), seed]).standard_normal(out[name].shape)
        drawn = base * np.exp(spread * noise) if base else spread * noise
        out[name] = jnp.asarray(drawn.astype(out[name].dtype))
    for name, factor in factors.items():
        out[name] = (out[name] * factor).astype(out[name].dtype)
    return out
```

```python
from contextlib import ExitStack

import concourse.bass as bass
from concourse import mybir

F32 = mybir.dt.float32
F32R = mybir.dt.float32r
I32 = mybir.dt.int32
U32 = mybir.dt.uint32
ACT = mybir.ActivationFunctionType
ALU = mybir.AluOpType
AX = mybir.AxisListType

P = 128
B, L, D = 16, 224, 512
S, NF = 750, 32
H, DH = 16, 32
DC = D // P
HC = H // DC
QT, QW = 2, L // 2
KT, KW = 6, S // 6
T = B * L
EPS = 1e-5
THRESHOLD = 0.1
GATE_LOW = 0.1
SCORE_SCALE = float(DH) ** -0.5
HALF_N = (512, S - 512)
HALF_K = (376, S - 376)

XT0, XT1, Q0, Q1, K0, V0 = 0, 1, 2, 3, 4, 12
ITEMS = 18
SPLITS = 10


def attention_phase(nc, x, ctx_t, ctxb, g_xattn, wq, bq, wk, bk, wv, bv, wo, bo, x1):
    q_dram = nc.dram_tensor("q_parts", (B, DC, HC, 2, DH, L), F32, kind="Internal").ap()
    energy_dram = nc.dram_tensor("energy", (B, S), F32, kind="Internal").ap()
    gate_dram = nc.dram_tensor("gate", (B, S), F32, kind="Internal").ap()

    es = ExitStack()
    with es:
        def sb(name, shape, dt=F32):
            return es.enter_context(nc.sbuf_tensor(name, shape, dt))

        def ps(name, shape):
            return es.enter_context(nc.psum_tensor(name, shape, F32))

        def sem(name):
            return es.enter_context(nc.semaphore(name))

        wq_sb = sb("wq_sb", [P, DC, D])
        wo_sb = sb("wo_sb", [P, DC, D])
        wk_hi = sb("wk_hi", [P, DC, D], F32R)
        wk_lo = sb("wk_lo", [P, DC, D], F32R)
        wv_hi = sb("wv_hi", [P, DC, D], F32R)
        wv_lo = sb("wv_lo", [P, DC, D], F32R)
        ctx_raw = sb("ctx_raw", [P, 2, S])
        ctx_hi = sb("ctx_hi", [P, DC, S], F32R)
        ctx_lo = sb("ctx_lo", [P, DC, S], F32R)
        fresh = sb("fresh", [P, 2 * L])
        k_hi = sb("k_hi", [P, DC, S], F32R)
        k_lo = sb("k_lo", [P, DC, S], F32R)
        k_stack = sb("k_stack", [P, 2 * HC, S], F32R)
        q_hi = sb("q_hi", [P, DC, L], F32R)
        q_lo = sb("q_lo", [P, DC, L], F32R)
        q_stack = sb("q_stack", [P, 2 * HC, L], F32R)
        v_sb = sb("v_sb", [P, KT, D])
        probs = sb("probs", [P, 2, QT, S])
        probs_t = sb("probs_t", [P, HC, KT, L])
        x_in = sb("x_in", [QW, QT, D])
        x_res = sb("x_res", [QW, QT, D])
        xn_t = sb("xn_t", [P, DC, L])
        out_t = sb("out_t", [P, DC, L])
        rec_b = sb("rec_b", [P, L])
        rec = sb("rec", [QW, QT, HC])
        rec_x = sb("rec_x", [QW, QT, HC * DH])
        gate_b = sb("gate_b", [P, S])
        bo_t = sb("bo_t", [P, D])
        ident = sb("ident", [P, P])
        neg_max = sb("neg_max", [QW, 2, QT])
        row_sum = sb("row_sum", [QW, QT, H])
        bq_col = sb("bq_col", [P, DC])
        bk_col = sb("bk_col", [P, DC])
        bv_col = sb("bv_col", [P, DC])
        g_col = sb("g_col", [P, 1])
        tanh_g = sb("tanh_g", [P, 1])
        stats = sb("stats", [QW, QT, 6])
        moments = sb("moments", [QW, QT, 2])
        var_eps = sb("var_eps", [QW, QT])
        rstd0 = sb("rstd0", [QW, QT])
        rstd = sb("rstd", [QW, QT])
        newton = sb("newton", [QW, QT])
        minus_half = sb("minus_half", [P, QT])
        zero = sb("zero", [P, 1])
        e_max = sb("e_max", [B, 1])
        e_rec = sb("e_rec", [B, 1])
        token = sb("token", [P, 16])

        score = [ps(f"score{t}", [P, 1024]) for t in range(QT)]
        flip = [ps(f"flip{i}", [P, 512]) for i in range(2)]
        proj = ps("proj", [P, 512])
        pv = ps("pv", [P, 512])

        tabs_in = sem("tabs_in")
        ctxb_in = sem("ctxb_in")
        consts = sem("consts")
        w_hi = sem("w_hi")
        w_lo = sem("w_lo")
        energy_out = sem("energy_out")
        energy_in = sem("energy_in")
        gate_out = sem("gate_out")
        gate_ready = sem("gate_ready")
        tanh_ready = sem("tanh_ready")
        bvwo_done = sem("bvwo_done")
        bo_ready = sem("bo_ready")
        dve_chain = sem("dve_chain")
        raw_in = [sem(f"raw_in{r}") for r in range(2)]
        x_loaded = sem("x_loaded")
        gate_loaded = sem("gate_loaded")
        res_loaded = sem("res_loaded")
        x1_stored = sem("x1_stored")
        k_stacked = [sem(f"k_stacked{r}") for r in range(2)]
        q_stored = sem("q_stored")
        q_stacked = [sem(f"q_stacked{r}") for r in range(2)]
        ctx_hi_done = sem("ctx_hi_done")
        ctx_lo_done = sem("ctx_lo_done")
        var_ready = sem("var_ready")
        rstd0_ready = sem("rstd0_ready")
        xn_ready = sem("xn_ready")
        proj_done = sem("proj_done")
        proj_read = sem("proj_read")
        hi_done = sem("hi_done")
        lo_done = sem("lo_done")
        scored = [sem(f"scored{t}") for t in range(QT)]
        maxed = [sem(f"maxed{t}") for t in range(QT)]
        exped = [sem(f"exped{t}") for t in range(QT)]
        flipped = sem("flipped")
        copied_act = sem("copied_act")
        copied_dve = sem("copied_dve")
        rec_done = sem("rec_done")
        rec_x_done = sem("rec_x_done")
        pv_done = sem("pv_done")
        normed = sem("normed")
        out_done = sem("out_done")
        res_ready = sem("res_ready")
        res_done = sem("res_done")

        PRE = {"exped": 1, "flipped": 4, "pv_done": 1, "normed": 1, "rec_x_done": 1,
               "proj_read": 1, "lo_done": 1, "res_done": 2, "x1_stored": 16}
        K_SET, Q_SET = 16 * 4 * HC, 16 * 2

        def by_vector(h, p):
            return p == 1 and h % HC != HC - 1

        ACT_CHUNK, DVE_CHUNK = 3 * HC - (HC - 1), HC - 1

        def copied_before(h, p, vector):
            return sum(by_vector(i, j) == vector for i in range(h + 1) for j in range(3) if (i, j) <= (h, p))

        TABS = 16 * 9
        BATCH_LINKS = 6 + 2 * DC
        flat_t = probs_t[:, :, :, :].rearrange("p a b c -> p (a b c)")
        wv_tmp = probs[:, :, :, :].rearrange("p a b c -> p (a b c)")[:, 0:DC * D].rearrange("p (c n) -> p c n", c=DC)

        block = es.enter_context(nc.Block())

        @block.sync
        def _(sp):
            sp.dma_start(flat_t[0:B * KT, 0:KW * NF],
                         ctxb.rearrange("b (c t) f -> (b c) (t f)", c=KT)).then_inc(ctxb_in, 16)
            sp.dma_start(v_sb[:, 0:DC, :], wk.rearrange("(c p) n -> p c n", p=P)).then_inc(tabs_in, 16)

            def at_batch(first, each, n):
                value = first + each * n
                return value if isinstance(n, int) else sp.snap(sp.to_reg(value))

            def load_raw(n, d):
                sp.dma_start(ctx_raw[:, d % 2, :],
                             ctx_t[bass.ds(n, 1), :, d, :].rearrange("a p s -> p (a s)")).then_inc(raw_in[d % 2], 16)

            def load_x(n):
                sp.dma_start(x_in[:, :, :],
                             x[bass.ds(n, 1), :, :].rearrange("a (t p) d -> p (a t) d", p=QW)).then_inc(x_loaded, 16)

            def load_gate(n):
                sp.dma_start(gate_b[:, :], gate_dram[bass.ds(n, 1), :].broadcast_to([P, S])).then_inc(gate_loaded, 16)

            def store_q(n):
                sp.wait_ge(lo_done, PRE["lo_done"] + n * SPLITS + 2)
                for c in range(DC):
                    for part, q_sb in enumerate((q_hi, q_lo)):
                        sp.dma_start(q_dram[bass.ds(n, 1), c, :, part, :, :].rearrange("a j p q -> (a j) p q"),
                                     q_sb[:, c, :].bitcast(F32)).then_inc(q_stored, 16)

            def stack(n, c, heads_done=None):
                ring = c % 2
                split = at_batch(PRE["lo_done"] + 4 + 2 * c, SPLITS, n)
                stored = at_batch(16 * 2 * DC, 16 * 2 * DC, n)
                if heads_done is not None:
                    for t in range(QT):
                        sp.wait_ge(scored[t], heads_done)
                sp.wait_ge(lo_done, split)
                sp.wait_ge(q_stored, stored)
                for j in range(HC):
                    for row in range(4):
                        k_sb = k_hi if row < 2 else k_lo
                        sp.dma_start(k_stack[row * DH:(row + 1) * DH, ring * HC + j, :].bitcast(F32),
                                     k_sb[j * DH:(j + 1) * DH, c, :].bitcast(F32)).then_inc(k_stacked[ring], 16)
                for rep in range(2):
                    sp.dma_start(q_stack[rep * 64:(rep + 1) * 64, ring * HC:(ring + 1) * HC, :].bitcast(F32),
                                 q_dram[bass.ds(n, 1), c, :, :, :, :].rearrange("a j w p q -> (a w p) j q"))\
                        .then_inc(q_stacked[ring], 16)

            load_raw(0, 0)
            load_raw(0, 1)
            load_x(0)
            sp.dma_start(wv_tmp, wv.rearrange("(c p) n -> p c n", p=P)).then_inc(tabs_in, 16)
            sp.dma_start(wq_sb[:, :, :], wq.rearrange("(c p) n -> p c n", p=P)).then_inc(tabs_in, 16)
            sp.dma_start(wo_sb[:, :, :], wo.rearrange("(c p) n -> p c n", p=P)).then_inc(tabs_in, 16)
            sp.dma_start(bq_col[:, :], bq).then_inc(tabs_in, 16)
            sp.dma_start(bk_col[:, :], bk).then_inc(tabs_in, 16)
            sp.dma_start(bv_col[:, :], bv).then_inc(tabs_in, 16)
            sp.dma_start(bo_t[:, :], bo.rearrange("(a n) -> a n", a=1).broadcast_to([P, D])).then_inc(tabs_in, 16)
            sp.dma_start(g_col[:, :], g_xattn.rearrange("(a n) -> a n", a=1).broadcast_to([P, 1])).then_inc(tabs_in, 16)
            sp.wait_ge(dve_chain, 1)
            sp.dma_start(energy_dram.rearrange("b (c t) -> (b c) t", c=KT),
                         rec_b[0:B * KT, 0:KW]).then_inc(energy_out, 16)
            sp.wait_ge(energy_out, 16)
            sp.dma_start(gate_b[0:B, :], energy_dram).then_inc(energy_in, 16)
            for d in (2, 3):
                sp.wait_ge(ctx_lo_done, d - 1)
                load_raw(0, d)
            sp.wait_ge(gate_ready, 1)
            sp.dma_start(gate_dram, gate_b[0:B, :]).then_inc(gate_out, 16)
            sp.wait_ge(gate_out, 16)
            load_gate(0)
            store_q(0)
            stack(0, 0)
            stack(0, 1)

            def batch(b, last):
                n = b + 1
                if not last:
                    sp.wait_ge(proj_done, b * ITEMS + XT1 + 1)
                    load_x(n)
                    for d in (0, 1):
                        sp.wait_ge(ctx_lo_done, b * DC + d + 3)
                        load_raw(n, d)
                    sp.wait_ge(proj_read, PRE["proj_read"] + b * ITEMS + V0)
                    load_gate(n)
                sp.wait_ge(x1_stored, PRE["x1_stored"] + b * 16)
                sp.dma_start(x_res[:, :, :], x[bass.ds(b, 1), :, :].rearrange("a (t p) d -> p (a t) d", p=QW))\
                    .then_inc(res_loaded, 16)
                stack(b, 2, at_batch(HC, H, b))
                if not last:
                    for d in (2, 3):
                        sp.wait_ge(ctx_lo_done, n * DC + d - 1)
                        load_raw(n, d)
                stack(b, 3, at_batch(2 * HC, H, b))
                if not last:
                    store_q(n)
                    for c in range(2):
                        stack(n, c, at_batch((c + 3) * HC, H, b))
                sp.wait_ge(res_done, PRE["res_done"] + b * QT + QT)
                sp.dma_start(x1[bass.ds(b * L, L), :].rearrange("(t p) d -> p t d", p=QW), x_res[:, :, :])\
                    .then_inc(x1_stored, 16)

            with sp.Fori(0, B - 1) as b:
                batch(b, False)
            batch(B - 1, True)
            sp.wait_ge(x1_stored, PRE["x1_stored"] + B * 16)

        @block.gpsimd
        def _(pool):
            pool.memset(ident[:, :], 0.0).then_inc(consts, 1)
            pool.memset(minus_half[:, :], -0.5).then_inc(consts, 1)
            pool.memset(zero[:, :], 0.0).then_inc(consts, 1)
            pool.wait_ge(consts, 3)
            pool.affine_select(out=ident[:, :], in_=ident[:, :], compare_op=ALU.not_equal, fill=1.0,
                               base=0, pattern=[[-1, P]], channel_multiplier=1).then_inc(consts, 1)
            pool.wait_ge(consts, 4)

            def remainder(lo, full, hi):
                return nc.gpsimd.tensor_tensor(lo, full, hi.bitcast(F32), ALU.subtract)

            def norm_power(n):
                pool.wait_ge(var_ready, n + 1)
                nc.gpsimd.tensor_tensor(rstd0[:, :], var_eps[:, :], minus_half[0:QW, :], ALU.pow).then_inc(rstd0_ready, 1)

            def ctx_remainder(n, d):
                pool.wait_ge(ctx_hi_done, n * DC + d + 1)
                remainder(ctx_lo[:, d, :], ctx_raw[:, d % 2, :], ctx_hi[:, d, :]).then_inc(ctx_lo_done, 1)

            def split_remainder(n, i):
                pool.wait_ge(hi_done, n * SPLITS + i + 1)
                if i < 2:
                    remainder(q_lo[:, 2 * i:2 * i + 2, :].rearrange("p c q -> p (c q)"), fresh[:, :],
                              q_hi[:, 2 * i:2 * i + 2, :].rearrange("p c q -> p (c q)")).then_inc(lo_done, 1)
                else:
                    c, half = divmod(i - 2, 2)
                    at, w = half * HALF_K[0], HALF_K[half]
                    remainder(k_lo[:, c, at:at + w], fresh[:, 0:w], k_hi[:, c, at:at + w]).then_inc(lo_done, 1)

            def spread_reciprocals(b, c):
                pool.wait_ge(rec_done, b * DC + c + 1)
                pool.wait_ge(pv_done, PRE["pv_done"] + b * DC + c)
                nc.gpsimd.tensor_tensor(rec_x[:, :, :].rearrange("p t (h w) -> p (t h) w", w=DH),
                                        rec[:, :, :].rearrange("p t h -> p (t h)").unsqueeze(2).broadcast_to([QW, QT * HC, DH]),
                                        zero[0:QW, :].unsqueeze(2).broadcast_to([QW, QT * HC, DH]), ALU.add)\
                    .then_inc(rec_x_done, 1)

            pool.wait_ge(tabs_in, TABS)
            for i, (lo, tmp, hi) in enumerate(((wk_lo, v_sb[:, 0:DC, :], wk_hi), (wv_lo, wv_tmp, wv_hi))):
                pool.wait_ge(w_hi, i + 1)
                remainder(lo[:, :, :], tmp, hi[:, :, :]).then_inc(w_lo, 1)
            norm_power(0)
            for d in range(DC):
                ctx_remainder(0, d)
            for i in range(SPLITS):
                split_remainder(0, i)

            def batch(b, last):
                n = b + 1
                if not last:
                    norm_power(n)
                pool.wait_ge(res_loaded, b * 16 + 16)
                pool.wait_ge(bo_ready, 1)
                nc.gpsimd.tensor_tensor(x_res[:, :, :], x_res[:, :, :],
                                        bo_t[0:QW, :].unsqueeze(1).broadcast_to([QW, QT, D]), ALU.add).then_inc(res_ready, 1)
                spread_reciprocals(b, 0)
                if not last:
                    for d in range(DC):
                        ctx_remainder(n, d)
                    split_remainder(n, 0)
                    split_remainder(n, 1)
                spread_reciprocals(b, 1)
                if not last:
                    for i in range(2, 6):
                        split_remainder(n, i)
                spread_reciprocals(b, 2)
                if not last:
                    for i in range(6, SPLITS):
                        split_remainder(n, i)
                spread_reciprocals(b, 3)

            with pool.Fori(0, B - 1) as b:
                batch(b, False)
            batch(B - 1, True)

        @block.scalar
        def _(act):
            act.wait_ge(tabs_in, TABS)
            act.activation(tanh_g[:, :], g_col[:, :], ACT.Tanh).then_inc(tanh_ready, 1)

            def exponentials(b, h):
                for t in range(QT):
                    act.wait_ge(maxed[t], b * H + h + 1)
                    act.wait_ge(flipped, PRE["flipped"] + b * 3 * H + 3 * (h - 1))
                    act.activation(probs[0:QW, h % 2, t, :], score[t][0:QW, 0:S], ACT.Exp,
                                   bias=neg_max[:, h % 2, t:t + 1], accum_out=row_sum[:, t, h:h + 1]).then_inc(exped[t], 1)

            def copy_flipped(b, h):
                for p in range(3):
                    if not by_vector(h, p):
                        act.wait_ge(flipped, PRE["flipped"] + b * 3 * H + 3 * h + p + 1)
                        act.activation(probs_t[0:KW, h % HC, 2 * p:2 * p + 2, :].rearrange("k a q -> k (a q)"),
                                       flip[(3 * h + p) % 2][0:KW, 0:2 * L], ACT.Relu).then_inc(copied_act, 1)

            def copy_values(n, kt):
                act.wait_ge(proj_done, n * ITEMS + V0 + kt + 1)
                act.activation(v_sb[0:KW, kt, :], proj[0:KW, :], ACT.Copy).then_inc(proj_read, 1)

            def split_high(n, i, first):
                act.wait_ge(proj_read, PRE["proj_read"] + n * ITEMS + Q0 + i + 1)
                if i < 2:
                    if not first:
                        act.wait_ge(q_stored, n * 16 * 2 * DC)
                    act.activation(q_hi[:, 2 * i:2 * i + 2, :].rearrange("p c q -> p (c q)"), fresh[:, :], ACT.Copy)\
                        .then_inc(hi_done, 1)
                else:
                    c, half = divmod(i - 2, 2)
                    at, w = half * HALF_K[0], HALF_K[half]
                    if not first:
                        act.wait_ge(k_stacked[c % 2], K_SET * (2 * n + c // 2 - 1))
                    act.activation(k_hi[:, c, at:at + w], fresh[:, 0:w], ACT.Copy).then_inc(hi_done, 1)

            for i in range(SPLITS):
                split_high(0, i, True)
            copy_values(0, 0)
            copy_values(0, 1)

            def batch(b, last):
                n = b + 1
                for h in range(H):
                    exponentials(b, h)
                    if h < KT - 2:
                        copy_values(b, h + 2)
                    if not last and h >= 6:
                        split_high(n, h - 6, False)
                    if h:
                        copy_flipped(b, h - 1)
                copy_flipped(b, H - 1)
                if not last:
                    copy_values(n, 0)
                    copy_values(n, 1)

            with act.Fori(0, B - 1) as b:
                batch(b, False)
            batch(B - 1, True)

        @block.vector
        def _(dve):
            links = [0]

            def link(ins, base=0):
                links[0] += 1
                ins.then_inc(dve_chain, 1)
                dve.wait_ge(dve_chain, base + links[0])

            free = {"exped": exped, "flipped": [flipped], "pv_done": [pv_done], "normed": [normed],
                    "rec_x_done": [rec_x_done], "proj_read": [proj_read], "lo_done": [lo_done],
                    "res_done": [res_done], "x1_stored": [x1_stored]}
            given = [(s, PRE[name]) for name, sems in free.items() for s in sems]
            for i, (s, count) in enumerate(given):
                nc.vector.memset(token[:, i:i + 1], 0.0).then_inc(s, count)

            dve.wait_ge(ctxb_in, 16)
            link(nc.vector.tensor_reduce(rec_b[0:B * KT, 0:KW],
                                         flat_t[0:B * KT, 0:KW * NF].rearrange("p (t f) -> p t f", f=NF),
                                         axis=AX.X, op=ALU.add, apply_absolute_value=True))
            dve.wait_ge(tabs_in, TABS)
            nc.vector.tensor_copy(wk_hi[:, :, :], v_sb[:, 0:DC, :]).then_inc(w_hi, 1)
            nc.vector.tensor_copy(wv_hi[:, :, :], wv_tmp).then_inc(w_hi, 1)

            def norm_statistics(n, base):
                dve.wait_ge(x_loaded, n * 16 + 16)
                nc.vector.bn_stats(stats[:, 0, :], x_in[:, 0, :])
                link(nc.vector.bn_stats(stats[:, 1, :], x_in[:, 1, :]), base)
                nc.vector.memset(token[:, 15:16], 0.0)
                nc.vector.bn_aggr(moments[:, 0, :], stats[:, 0, :])
                link(nc.vector.bn_aggr(moments[:, 1, :], stats[:, 1, :]), base)
                nc.vector.tensor_scalar(var_eps[:, :], moments[:, :, 1], EPS, None, ALU.add).then_inc(var_ready, 1)

            def normalize(n, base):
                dve.wait_ge(rstd0_ready, n + 1)
                link(nc.vector.tensor_tensor(newton[:, :], rstd0[:, :], rstd0[:, :], ALU.mult), base)
                link(nc.vector.tensor_tensor(newton[:, :], newton[:, :], var_eps[:, :], ALU.mult), base)
                link(nc.vector.tensor_scalar(newton[:, :], newton[:, :], -0.5, 1.5, ALU.mult, ALU.add), base)
                link(nc.vector.tensor_tensor(rstd[:, :], rstd0[:, :], newton[:, :], ALU.mult), base)
                for t in range(QT):
                    nc.vector.tensor_scalar(x_in[:, t, :], x_in[:, t, :], moments[:, t, 0:1], rstd[:, t:t + 1],
                                            ALU.subtract, ALU.mult).then_inc(xn_ready, 1)

            def ctx_high(n, d, first):
                ring = d % 2
                dve.wait_ge(raw_in[ring], 16 * (2 * n + d // 2 + 1))
                if not first:
                    dve.wait_ge(proj_done, n * ITEMS)
                nc.vector.tensor_copy(ctx_hi[:, d, :], ctx_raw[:, ring, :]).then_inc(ctx_hi_done, 1)

            def copy_xt(n, t):
                dve.wait_ge(proj_done, n * ITEMS + XT0 + t + 1)
                nc.vector.tensor_copy(xn_t[:, :, t * QW:(t + 1) * QW],
                                      proj[:, 0:DC * QW].rearrange("p (c q) -> p c q", c=DC)).then_inc(proj_read, 1)

            def read_split(n, i):
                dve.wait_ge(proj_done, n * ITEMS + Q0 + i + 1)
                dve.wait_ge(lo_done, PRE["lo_done"] + n * SPLITS + i)
                if i < 2:
                    for k in range(2):
                        c = 2 * i + k
                        ins = nc.vector.tensor_scalar(fresh[:, k * L:(k + 1) * L], proj[:, k * L:(k + 1) * L],
                                                      bq_col[:, c:c + 1], None, ALU.add)
                    ins.then_inc(proj_read, 1)
                else:
                    c, half = divmod(i - 2, 2)
                    at, w = half * HALF_K[0], HALF_K[half]
                    if i == 2:
                        dve.wait_ge(gate_loaded, n * 16 + 16)
                    nc.vector.scalar_tensor_tensor(fresh[:, 0:w], proj[:, 0:w], bk_col[:, c:c + 1],
                                                   gate_b[:, at:at + w], ALU.add, ALU.mult).then_inc(proj_read, 1)

            def maxima(b, h):
                for t in range(QT):
                    dve.wait_ge(scored[t], b * H + h + 1)
                    nc.vector.tensor_reduce(neg_max[:, h % 2, t:t + 1], score[t][0:QW, 0:S], axis=AX.X, op=ALU.max,
                                            negate=True).then_inc(maxed[t], 1)

            def copy_flipped(b, h):
                for p in range(3):
                    if by_vector(h, p):
                        dve.wait_ge(flipped, PRE["flipped"] + b * 3 * H + 3 * h + p + 1)
                        nc.vector.tensor_scalar(probs_t[0:KW, h % HC, 2 * p:2 * p + 2, :].rearrange("k a q -> k (a q)"),
                                                flip[(3 * h + p) % 2][0:KW, 0:2 * L], 0.0, None, ALU.max)\
                            .then_inc(copied_dve, 1)

            def reciprocals(b, c, base):
                for t in range(QT):
                    dve.wait_ge(exped[t], PRE["exped"] + b * H + (c + 1) * HC)
                dve.wait_ge(rec_x_done, PRE["rec_x_done"] + b * DC + c)
                link(nc.vector.reciprocal(rec[:, :, :], row_sum[:, :, c * HC:(c + 1) * HC]), base)
                nc.vector.tensor_scalar(rec[:, :, :], rec[:, :, :], 0.0, None, ALU.max).then_inc(rec_done, 1)

            def normalize_output(b, c, base):
                dve.wait_ge(pv_done, PRE["pv_done"] + b * DC + c + 1)
                link(nc.vector.tensor_copy(rec_b[:, :], pv[:, L:2 * L]), base)
                nc.vector.tensor_tensor(out_t[:, c, :], pv[:, 0:L], rec_b[:, :], ALU.mult).then_inc(normed, 1)

            norm_statistics(0, 0)
            dve.wait_ge(energy_in, 16)
            link(nc.vector.tensor_reduce(e_max[:, :], gate_b[0:B, :], axis=AX.X, op=ALU.max))
            link(nc.vector.tensor_scalar(e_max[:, :], e_max[:, :], 1.0 / NF, 1e-8, ALU.mult, ALU.add))
            link(nc.vector.reciprocal(e_rec[:, :], e_max[:, :]))
            link(nc.vector.tensor_scalar(gate_b[0:B, :], gate_b[0:B, :], 1.0 / NF, e_rec[:, :], ALU.mult, ALU.mult))
            link(nc.vector.tensor_scalar(gate_b[0:B, :], gate_b[0:B, :], THRESHOLD, 1.0 - GATE_LOW, ALU.is_gt, ALU.mult))
            nc.vector.tensor_scalar(gate_b[0:B, :], gate_b[0:B, :], GATE_LOW, SCORE_SCALE, ALU.add, ALU.mult)\
                .then_inc(gate_ready, 1)
            normalize(0, 0)
            for d in range(DC):
                ctx_high(0, d, True)
            dve.wait_ge(bvwo_done, 1)
            dve.wait_ge(tanh_ready, 1)
            link(nc.vector.tensor_tensor(bo_t[:, :], pv[:, :], bo_t[:, :], ALU.add))
            nc.vector.tensor_scalar(bo_t[:, :], bo_t[:, :], tanh_g[:, :], None, ALU.mult).then_inc(bo_ready, 1)
            for t in range(QT):
                copy_xt(0, t)
            for i in range(SPLITS):
                read_split(0, i)
            setup_links = links[0]

            def batch(b, last):
                n = b + 1
                base = setup_links + b * BATCH_LINKS
                links[0] = 0
                for h in range(H):
                    maxima(b, h)
                    if h and h % HC == 0:
                        reciprocals(b, h // HC - 1, base)
                    if not last:
                        if h == 0:
                            norm_statistics(n, base)
                        if h == 2:
                            normalize(n, base)
                        if 4 <= h < 8:
                            ctx_high(n, h - 4, False)
                        if 4 <= h < 6:
                            copy_xt(n, h - 4)
                        if h >= 6:
                            read_split(n, h - 6)
                    if h > HC and h % HC == 1:
                        normalize_output(b, h // HC - 1, base)
                    if h:
                        copy_flipped(b, h - 1)
                reciprocals(b, DC - 1, base)
                copy_flipped(b, H - 1)
                normalize_output(b, DC - 1, base)
                dve.wait_ge(res_ready, b + 1)
                for t in range(QT):
                    dve.wait_ge(out_done, b * QT + t + 1)
                    nc.vector.scalar_tensor_tensor(x_res[:, t, :], flip[t][0:QW, :], tanh_g[0:QW, :], x_res[:, t, :],
                                                   ALU.mult, ALU.add).then_inc(res_done, 1)
                return links[0]

            with dve.Fori(0, B - 1) as b:
                assert batch(b, False) == BATCH_LINKS
            batch(B - 1, True)

        @block.tensor
        def _(pe):
            pe.wait_ge(consts, 4)
            pe.wait_ge(tabs_in, TABS)
            for c in range(DC):
                ins = nc.tensor.matmul(pv[:, :], bv_col[:, c:c + 1].broadcast_to([P, P]), wo_sb[:, c, :],
                                       start=(c == 0), stop=(c == DC - 1))
            ins.then_inc(bvwo_done, 1)

            def take_proj(n, i):
                pe.wait_ge(proj_read, PRE["proj_read"] + n * ITEMS + i)

            def transpose_x(n, t):
                take_proj(n, XT0 + t)
                pe.wait_ge(xn_ready, n * QT + t + 1)
                for c in range(DC):
                    ins = nc.tensor.transpose(proj[:, c * QW:(c + 1) * QW], x_in[:, t, c * P:(c + 1) * P],
                                              ident[0:QW, 0:QW])
                ins.then_inc(proj_done, 1)

            def project_q(n, i):
                take_proj(n, Q0 + i)
                for k in range(2):
                    c = 2 * i + k
                    for d in range(DC):
                        ins = nc.tensor.matmul(proj[:, k * L:(k + 1) * L], wq_sb[:, d, c * P:(c + 1) * P], xn_t[:, d, :],
                                               start=(d == 0), stop=(d == DC - 1))
                ins.then_inc(proj_done, 1)

            def project_k(n, i):
                c, half = divmod(i, 2)
                at, w = half * HALF_K[0], HALF_K[half]
                take_proj(n, K0 + i)
                if i == 0:
                    pe.wait_ge(ctx_lo_done, n * DC + DC)
                for d in range(DC):
                    for k, (wp, xp) in enumerate(((wk_hi, ctx_hi), (wk_hi, ctx_lo), (wk_lo, ctx_hi))):
                        ins = nc.tensor.matmul(proj[:, 0:w], wp[:, d, c * P:(c + 1) * P], xp[:, d, at:at + w],
                                               start=(d == 0 and k == 0), stop=(d == DC - 1 and k == 2))
                ins.then_inc(proj_done, 1)

            def project_v(n, kt):
                take_proj(n, V0 + kt)
                for d in range(DC):
                    for k, (xp, wp) in enumerate(((ctx_hi, wv_hi), (ctx_hi, wv_lo), (ctx_lo, wv_hi))):
                        ins = nc.tensor.matmul(proj[0:KW, :], xp[:, d, kt * KW:(kt + 1) * KW], wp[:, d, :],
                                               start=(d == 0 and k == 0), stop=(d == DC - 1 and k == 2))
                ins.then_inc(proj_done, 1)

            def scores(b, h):
                c = h // HC
                if h % HC == 0:
                    pe.wait_ge(k_stacked[c % 2], K_SET * (2 * b + c // 2 + 1))
                    pe.wait_ge(q_stacked[c % 2], Q_SET * (2 * b + c // 2 + 1))
                slot = h % (2 * HC)
                for t in range(QT):
                    pe.wait_ge(exped[t], PRE["exped"] + b * H + h)
                    at = 0
                    for w in HALF_N:
                        ins = nc.tensor.matmul(score[t][0:QW, at:at + w], q_stack[:, slot, t * QW:(t + 1) * QW],
                                               k_stack[:, slot, at:at + w], start=True, stop=True)
                        at += w
                    ins.then_inc(scored[t], 1)

            def wait_copied(b, h, p):
                vector = by_vector(h, p)
                done, each = (copied_dve, DVE_CHUNK) if vector else (copied_act, ACT_CHUNK)
                pe.wait_ge(done, b * DC * each + copied_before(h, p, vector))

            def flip_probs(b, h):
                for t in range(QT):
                    pe.wait_ge(exped[t], PRE["exped"] + b * H + h + 1)
                for p in range(3):
                    g = 3 * h + p
                    if g < 2:
                        pe.wait_ge(res_done, PRE["res_done"] + (b - 1) * QT + g + 1)
                    else:
                        wait_copied(b, (g - 2) // 3, (g - 2) % 3)
                    for k in range(2):
                        for t in range(QT):
                            kt = 2 * p + k
                            ins = nc.tensor.transpose(flip[g % 2][0:KW, k * L + t * QW:k * L + (t + 1) * QW],
                                                      probs[0:QW, h % 2, t, kt * KW:(kt + 1) * KW], ident[0:QW, 0:QW])
                    ins.then_inc(flipped, 1)

            def attend(b, c):
                pe.wait_ge(normed, PRE["normed"] + b * DC + c)
                pe.wait_ge(rec_x_done, PRE["rec_x_done"] + b * DC + c + 1)
                for t in range(QT):
                    nc.tensor.matmul(pv[:, L + t * QW:L + (t + 1) * QW], rec_x[:, t, :], ident[0:QW, 0:QW],
                                     start=True, stop=True)
                h = c * HC + HC - 1
                pe.wait_ge(copied_act, b * DC * ACT_CHUNK + copied_before(h, 2, False))
                pe.wait_ge(copied_dve, b * DC * DVE_CHUNK + copied_before(h, 2, True))
                for kt in range(KT):
                    for j in range(HC):
                        at = (c * HC + j) * DH
                        ins = nc.tensor.matmul(pv[j * DH:(j + 1) * DH, 0:L], v_sb[0:KW, kt, at:at + DH],
                                               probs_t[0:KW, j, kt, :], start=(kt == 0), stop=(kt == KT - 1))
                ins.then_inc(pv_done, 1)

            def project_out(b, t):
                pe.wait_ge(normed, PRE["normed"] + b * DC + DC)
                for c in range(DC):
                    ins = nc.tensor.matmul(flip[t][0:QW, :], out_t[:, c, t * QW:(t + 1) * QW], wo_sb[:, c, :],
                                           start=(c == 0), stop=(c == DC - 1))
                ins.then_inc(out_done, 1)

            for t in range(QT):
                transpose_x(0, t)
            for i in range(2):
                project_q(0, i)
            pe.wait_ge(w_lo, 2)
            for i in range(2 * DC):
                project_k(0, i)
            project_v(0, 0)
            project_v(0, 1)

            def batch(b, last):
                n = b + 1
                for h in range(H):
                    scores(b, h)
                    if h < KT - 2:
                        project_v(b, h + 2)
                    elif not last:
                        if h < 6:
                            transpose_x(n, h - 4)
                        elif h < 8:
                            project_q(n, h - 6)
                        else:
                            project_k(n, h - 8)
                    if h > HC and h % HC == 1:
                        attend(b, h // HC - 1)
                    if h:
                        flip_probs(b, h - 1)
                flip_probs(b, H - 1)
                attend(b, DC - 1)
                if not last:
                    project_v(n, 0)
                for t in range(QT):
                    project_out(b, t)
                if not last:
                    project_v(n, 1)

            with pe.Fori(0, B - 1) as b:
                batch(b, False)
            batch(B - 1, True)


E_R, TOP, MID = 16, 2, 128
MID_S = 512
TILES = T // P
GROUPS = 5
GW = 4 * MID


def experts_phase(nc, x1, g_ffn, router_w, w_gu, w_d, ws_gu, ws_d, out):
    es = ExitStack()
    with es:
        def sb(name, shape, dt=F32):
            return es.enter_context(nc.sbuf_tensor(name, shape, dt))

        def ps(name, shape):
            return es.enter_context(nc.psum_tensor(name, shape, F32))

        def sem(name):
            return es.enter_context(nc.semaphore(name))

        gu_sb = sb("gu_sb", [P, E_R, DC, 2 * MID])
        d_sb = sb("d_sb", [P, E_R, D])
        sgu_sb = sb("sgu_sb", [P, DC, 2 * MID_S])
        sd_sb = sb("sd_sb", [P, DC, D])
        rw_sb = sb("rw_sb", [P, DC, E_R])
        ident2 = sb("ident2", [P, P])
        minus_half2 = sb("minus_half2", [P, 1])
        iota_e = sb("iota_e", [P, E_R])
        g_col2 = sb("g_col2", [P, 1])
        tanh_g2 = sb("tanh_g2", [P, 1])
        xt = sb("xt", [P, D])
        xn = sb("xn", [P, D])
        xn_t2 = sb("xn_t2", [P, DC, P])
        stats2 = sb("stats2", [P, 6])
        moments2 = sb("moments2", [P, 2])
        var2 = sb("var2", [P, 1])
        r0 = sb("r0", [P, 1])
        r1 = sb("r1", [P, 1])
        nw = sb("nw", [P, 1])
        neg_top = sb("neg_top", [P, 1])
        pexp = sb("pexp", [P, E_R])
        psum_e = sb("psum_e", [P, 1])
        prec = sb("prec", [P, 1])
        top8 = sb("top8", [P, 8])
        top_at = sb("top_at", [P, 8], U32)
        top_f = sb("top_f", [P, 8])
        wsum = sb("wsum", [P, 1])
        top_w = sb("top_w", [P, TOP])
        pick = sb("pick", [P, TOP, E_R])
        comb = sb("comb", [P, E_R])
        act_g = sb("act_g", [P, 2, GW])
        hid = sb("hid", [P, 2, GW])
        hid_t = sb("hid_t", [P, 2, GW])
        token2 = sb("token2", [P, 4])

        gate_ps = [ps(f"gate_ps{i}", [P, GW]) for i in range(2)]
        up_ps = [ps(f"up_ps{i}", [P, GW]) for i in range(2)]
        turn = ps("turn", [P, 512])
        logit = ps("logit", [P, 512])
        y_ps = ps("y_ps", [P, D])

        w2_in = sem("w2_in")
        consts2 = sem("consts2")
        tanh2 = sem("tanh2")
        x1_in = sem("x1_in")
        chain2 = sem("chain2")
        var2_ready = sem("var2_ready")
        r0_ready = sem("r0_ready")
        xn2_ready = sem("xn2_ready")
        turned = sem("turned")
        xt_read = sem("xt_read")
        logits_done = sem("logits_done")
        top_ready = sem("top_ready")
        pexp_ready = sem("pexp_ready")
        gate_done = sem("gate_done")
        up_done = sem("up_done")
        silu_done = sem("silu_done")
        mult_done = sem("mult_done")
        hid_done = sem("hid_done")
        hid_t_done = sem("hid_t_done")
        y_done = sem("y_done")
        out_ready = sem("out_ready")
        out_stored = sem("out_stored")
        W2 = 16 * 6

        block = es.enter_context(nc.Block())

        @block.sync
        def _(sp):
            sp.dma_start(rw_sb[:, :, :], router_w.rearrange("(c p) e -> p c e", p=P)).then_inc(w2_in, 16)
            sp.dma_start(g_col2[:, :], g_ffn.rearrange("(a n) -> a n", a=1).broadcast_to([P, 1])).then_inc(w2_in, 16)
            sp.dma_start(gu_sb[:, :, :, :].rearrange("p e c m -> p (e c m)"), w_gu).then_inc(w2_in, 16)
            sp.dma_start(sgu_sb[:, :, :], ws_gu).then_inc(w2_in, 16)
            sp.dma_start(d_sb[:, :, :], w_d.rearrange("e m n -> m e n")).then_inc(w2_in, 16)
            sp.dma_start(sd_sb[:, :, :], ws_d.rearrange("(c p) n -> p c n", p=P)).then_inc(w2_in, 16)
            with sp.Fori(0, TILES) as t:
                sp.wait_ge(out_stored, t * 16 + 16)
                sp.dma_start(xt[:, :], x1[bass.ds(t * P, P), :]).then_inc(x1_in, 16)
                sp.wait_ge(out_ready, t + 1)
                sp.dma_start(out[bass.ds(t * P, P), :], xt[:, :]).then_inc(out_stored, 16)
            sp.wait_ge(out_stored, TILES * 16 + 16)

        @block.gpsimd
        def _(pool):
            pool.memset(ident2[:, :], 0.0).then_inc(consts2, 1)
            pool.memset(minus_half2[:, :], -0.5).then_inc(consts2, 1)
            pool.iota(iota_e[:, :], pattern=[[1, E_R]], base=0, channel_multiplier=0,
                      allow_small_or_imprecise_dtypes=True).then_inc(consts2, 1)
            pool.wait_ge(consts2, 3)
            pool.affine_select(out=ident2[:, :], in_=ident2[:, :], compare_op=ALU.not_equal, fill=1.0,
                               base=0, pattern=[[-1, P]], channel_multiplier=1).then_inc(consts2, 1)
            pool.wait_ge(consts2, 4)
            with pool.Fori(0, TILES) as t:
                pool.wait_ge(var2_ready, t + 1)
                nc.gpsimd.tensor_tensor(r0[:, :], var2[:, :], minus_half2[:, :], ALU.pow).then_inc(r0_ready, 1)

        @block.scalar
        def _(act):
            act.wait_ge(w2_in, W2)
            act.activation(tanh_g2[:, :], g_col2[:, :], ACT.Tanh).then_inc(tanh2, 1)
            with act.Fori(0, TILES) as t:
                act.wait_ge(top_ready, t + 1)
                act.activation(pexp[:, :], logit[:, 0:E_R], ACT.Exp, bias=neg_top[:, :], accum_out=psum_e[:, :])\
                    .then_inc(pexp_ready, 1)

                def copy_turned(q):
                    act.wait_ge(turned, t * (GROUPS + 1) + q + 2)
                    act.activation(hid_t[:, q % 2, :], turn[:, :], ACT.Copy).then_inc(hid_t_done, 1)

                for q in range(GROUPS):
                    act.wait_ge(gate_done, t * GROUPS + q + 1)
                    act.activation(act_g[:, q % 2, :], gate_ps[q % 2][:, :], ACT.Silu).then_inc(silu_done, 1)
                    if q:
                        copy_turned(q - 1)
                copy_turned(GROUPS - 1)

        @block.vector
        def _(dve):
            links = [0]

            def link(ins, base):
                links[0] += 1
                ins.then_inc(chain2, 1)
                dve.wait_ge(chain2, base + links[0])

            LINKS = 14
            nc.vector.memset(token2[:, 0:1], 0.0).then_inc(out_stored, 16)
            dve.wait_ge(tanh2, 1)
            dve.wait_ge(consts2, 4)
            with dve.Fori(0, TILES) as t:
                base = t * LINKS
                dve.wait_ge(x1_in, t * 16 + 16)
                link(nc.vector.bn_stats(stats2[:, :], xt[:, :]), base)
                nc.vector.memset(token2[:, 1:2], 0.0)
                link(nc.vector.bn_aggr(moments2[:, :], stats2[:, :]), base)
                nc.vector.tensor_scalar(var2[:, :], moments2[:, 1:2], EPS, None, ALU.add).then_inc(var2_ready, 1)
                dve.wait_ge(r0_ready, t + 1)
                link(nc.vector.tensor_tensor(nw[:, :], r0[:, :], r0[:, :], ALU.mult), base)
                link(nc.vector.tensor_tensor(nw[:, :], nw[:, :], var2[:, :], ALU.mult), base)
                link(nc.vector.tensor_scalar(nw[:, :], nw[:, :], -0.5, 1.5, ALU.mult, ALU.add), base)
                link(nc.vector.tensor_tensor(r1[:, :], r0[:, :], nw[:, :], ALU.mult), base)
                nc.vector.tensor_scalar(xn[:, :], xt[:, :], moments2[:, 0:1], r1[:, :], ALU.subtract, ALU.mult)\
                    .then_inc(xn2_ready, 1)
                dve.wait_ge(turned, t * (GROUPS + 1) + 1)
                nc.vector.tensor_copy(xn_t2[:, :, :].rearrange("p c q -> p (c q)"), turn[:, :]).then_inc(xt_read, 1)
                dve.wait_ge(logits_done, t + 1)
                nc.vector.tensor_reduce(neg_top[:, :], logit[:, 0:E_R], axis=AX.X, op=ALU.max, negate=True)\
                    .then_inc(top_ready, 1)
                dve.wait_ge(pexp_ready, t + 1)
                link(nc.vector.reciprocal(prec[:, :], psum_e[:, :]), base)
                link(nc.vector.tensor_scalar(pexp[:, :], pexp[:, :], prec[:, :], None, ALU.mult), base)
                nc.vector.memset(token2[:, 2:3], 0.0)
                link(nc.vector.max(top8[:, :], pexp[:, :]), base)
                nc.vector.memset(token2[:, 3:4], 0.0)
                nc.vector.max_index(top_at[:, :], top8[:, :], pexp[:, :])
                link(nc.vector.tensor_scalar(wsum[:, :], top8[:, 0:1], top8[:, 1:2], 1e-9, ALU.add, ALU.add), base)
                nc.vector.tensor_copy(top_f[:, :], top_at[:, :])
                link(nc.vector.reciprocal(prec[:, :], wsum[:, :]), base)
                link(nc.vector.tensor_scalar(top_w[:, :], top8[:, 0:TOP], prec[:, :], None, ALU.mult), base)
                for k in range(TOP):
                    ins = nc.vector.tensor_scalar(pick[:, k, :], iota_e[:, :], top_f[:, k:k + 1], top_w[:, k:k + 1],
                                                  ALU.is_equal, ALU.mult)
                link(ins, base)
                link(nc.vector.tensor_tensor(comb[:, :], pick[:, 0, :], pick[:, 1, :], ALU.add), base)
                for q in range(GROUPS):
                    i = t * GROUPS + q
                    dve.wait_ge(up_done, i + 1)
                    dve.wait_ge(silu_done, i + 1)
                    ins = nc.vector.tensor_tensor(hid[:, q % 2, :], act_g[:, q % 2, :], up_ps[q % 2][:, :], ALU.mult)
                    if q < 4:
                        ins.then_inc(mult_done, 1)
                        dve.wait_ge(mult_done, t * 4 + q + 1)
                        ins = nc.vector.tensor_tensor(
                            hid[:, q % 2, :].rearrange("p (e m) -> p e m", m=MID),
                            hid[:, q % 2, :].rearrange("p (e m) -> p e m", m=MID),
                            comb[:, 4 * q:4 * q + 4].unsqueeze(2).broadcast_to([P, 4, MID]), ALU.mult)
                    ins.then_inc(hid_done, 1)
                dve.wait_ge(y_done, t + 1)
                nc.vector.scalar_tensor_tensor(xt[:, :], y_ps[:, :], tanh_g2[:, :], xt[:, :], ALU.mult, ALU.add)\
                    .then_inc(out_ready, 1)
                assert links[0] == LINKS

        @block.tensor
        def _(pe):
            pe.wait_ge(consts2, 4)
            pe.wait_ge(w2_in, W2)
            with pe.Fori(0, TILES) as t:
                pe.wait_ge(xn2_ready, t + 1)
                for c in range(DC):
                    ins = nc.tensor.transpose(turn[:, c * P:(c + 1) * P], xn[:, c * P:(c + 1) * P], ident2[:, :])
                ins.then_inc(turned, 1)
                pe.wait_ge(xt_read, t + 1)
                for c in range(DC):
                    ins = nc.tensor.matmul(logit[:, 0:E_R], xn_t2[:, c, :], rw_sb[:, c, :], start=(c == 0), stop=(c == DC - 1))
                ins.then_inc(logits_done, 1)

                def gate_up(q):
                    for half, (bank, done) in enumerate(((gate_ps, gate_done), (up_ps, up_done))):
                        for c in range(DC):
                            if q < 4:
                                rhs = gu_sb[:, 4 * q:4 * q + 4, c, half * MID:(half + 1) * MID]
                            else:
                                rhs = sgu_sb[:, c, half * MID_S:(half + 1) * MID_S]
                            ins = nc.tensor.matmul(bank[q % 2][:, :], xn_t2[:, c, :], rhs,
                                                   start=(c == 0), stop=(c == DC - 1))
                        ins.then_inc(done, 1)

                def down(q):
                    i = t * GROUPS + q
                    pe.wait_ge(hid_done, i + 1)
                    for k in range(4):
                        ins = nc.tensor.transpose(turn[:, k * P:(k + 1) * P], hid[:, q % 2, k * P:(k + 1) * P], ident2[:, :])
                    ins.then_inc(turned, 1)
                    pe.wait_ge(hid_t_done, i + 1)
                    for k in range(4):
                        rhs = d_sb[:, 4 * q + k, :] if q < 4 else sd_sb[:, k, :]
                        ins = nc.tensor.matmul(y_ps[:, :], hid_t[:, q % 2, k * P:(k + 1) * P], rhs,
                                               start=(q == 0 and k == 0), stop=(q == GROUPS - 1 and k == 3))
                    if q == GROUPS - 1:
                        ins.then_inc(y_done, 1)

                gate_up(0)
                for q in range(1, GROUPS):
                    gate_up(q)
                    down(q - 1)
                down(GROUPS - 1)


def kernel(**inputs):
    import numpy as np
    import concourse.bacc as bacc
    from concourse.bass_utils import run_bass_kernel_spmd as run

    a = {k: np.asarray(v) for k, v in inputs.items()}
    laid = {
        "x": a["x"],
        "ctx_t": a["ctx_1024"].transpose(0, 2, 1).reshape(B, DC, P, S).transpose(0, 2, 1, 3),
        "ctxb": a["ctxb_2048x32"],
        "g_xattn": a["g_xattn"],
        "wq": a["L0_xattn_Wq"], "bq": a["L0_xattn_bq"].reshape(DC, P).T,
        "wk": a["L0_xattn_Wk"], "bk": a["L0_xattn_bk"].reshape(DC, P).T,
        "wv": a["L0_xattn_Wv"], "bv": a["L0_xattn_bv"].reshape(DC, P).T,
        "wo": a["L0_xattn_Wo"], "bo": a["L0_xattn_bo"],
        "g_ffn": a["g_ffn"],
        "router_w": a["L0_ffn_router_w"],
        "w_gu": np.concatenate([a["L0_ffn_wg_r"], a["L0_ffn_wu_r"]], axis=2)
        .reshape(E_R, DC, P, 2 * MID).transpose(2, 0, 1, 3).reshape(P, -1),
        "w_d": a["L0_ffn_wd_r"],
        "ws_gu": np.stack([a["L0_ffn_wg_s"], a["L0_ffn_wu_s"]]).transpose(2, 0, 1, 3)
        .reshape(DC, P, 2 * MID_S).transpose(1, 0, 2),
        "ws_d": a["L0_ffn_wd_s"].reshape(MID_S, D),
    }
    nc = bacc.Bacc("TRN2", target_bir_lowering=False, num_devices=1)
    arrays, dram = {}, {}
    for name, value in laid.items():
        arrays[f"in_{name}"] = np.ascontiguousarray(value)
        dram[name] = nc.dram_tensor(f"in_{name}", value.shape, mybir.dt.from_np(value.dtype), kind="ExternalInput").ap()
    out = nc.dram_tensor("out", (T, D), F32, kind="ExternalOutput").ap()
    program(nc, out=out, **dram)
    result = run(nc, [arrays], core_ids=[0])
    return result.results[0]["out"].reshape(B, L, D)


def program(nc, x, ctx_t, ctxb, g_xattn, wq, bq, wk, bk, wv, bv, wo, bo,
            g_ffn, router_w, w_gu, w_d, ws_gu, ws_d, out):
    x1 = nc.dram_tensor("x1", (T, D), F32, kind="Internal").ap()
    attention_phase(nc, x, ctx_t, ctxb, g_xattn, wq, bq, wk, bk, wv, bv, wo, bo, x1)
    experts_phase(nc, x1, g_ffn, router_w, w_gu, w_d, ws_gu, ws_d, out)
```

```python
from contextlib import ExitStack

import concourse.bass as bass
from concourse import mybir

F32 = mybir.dt.float32
F32R = mybir.dt.float32r
I32 = mybir.dt.int32
U32 = mybir.dt.uint32
ACT = mybir.ActivationFunctionType
ALU = mybir.AluOpType
AX = mybir.AxisListType

P = 128
B, L, D = 16, 224, 512
S, NF = 750, 32
H, DH = 16, 32
DC = D // P
HC = H // DC
QT, QW = 2, L // 2
KT, KW = 6, S // 6
T = B * L
EPS = 1e-5
THRESHOLD = 0.1
GATE_LOW = 0.1
SCORE_SCALE = float(DH) ** -0.5
HALF_N = (512, S - 512)
HALF_K = (376, S - 376)

XT0, XT1, Q0, Q1, K0, V0 = 0, 1, 2, 3, 4, 12
ITEMS = 18
SPLITS = 10
ATTEND_HEADS = (5, 9, 13)
VALUE_HEADS = (0, 1, 2, 3, 4)
XT_HEAD = 5
SPLIT_HEADS = (6, 7, 8, 10, 11, 12, 13, 14, 15)


def attention_phase(nc, x, ctx_t, ctxb, g_xattn, wq, bq, wk, bk, wv, bv, wo, bo, x1):
    q_dram = nc.dram_tensor("q_parts", (B, DC, HC, 2, DH, L), F32, kind="Internal").ap()
    energy_dram = nc.dram_tensor("energy", (B, S), F32, kind="Internal").ap()
    gate_dram = nc.dram_tensor("gate", (B, S), F32, kind="Internal").ap()

    es = ExitStack()
    with es:
        def sb(name, shape, dt=F32):
            return es.enter_context(nc.sbuf_tensor(name, shape, dt))

        def ps(name, shape):
            return es.enter_context(nc.psum_tensor(name, shape, F32))

        def sem(name):
            return es.enter_context(nc.semaphore(name))

        wq_sb = sb("wq_sb", [P, DC, D])
        wo_sb = sb("wo_sb", [P, DC, D])
        wk_hi = sb("wk_hi", [P, DC, D], F32R)
        wk_lo = sb("wk_lo", [P, DC, D], F32R)
        wv_hi = sb("wv_hi", [P, DC, D], F32R)
        wv_lo = sb("wv_lo", [P, DC, D], F32R)
        ctx_raw = sb("ctx_raw", [P, 2, S])
        ctx_hi = sb("ctx_hi", [P, DC, S], F32R)
        ctx_lo = sb("ctx_lo", [P, DC, S], F32R)
        fresh = sb("fresh", [P, 2 * L])
        k_hi = sb("k_hi", [P, DC, S], F32R)
        k_lo = sb("k_lo", [P, DC, S], F32R)
        k_stack = sb("k_stack", [P, 2 * HC, S], F32R)
        q_hi = sb("q_hi", [P, DC, L], F32R)
        q_lo = sb("q_lo", [P, DC, L], F32R)
        q_stack = sb("q_stack", [P, 2 * HC, L], F32R)
        v_sb = sb("v_sb", [P, KT, D])
        probs = sb("probs", [P, 2, QT, S])
        probs_t = sb("probs_t", [P, HC, KT, L])
        x_in = sb("x_in", [QW, QT, D])
        x_res = sb("x_res", [QW, QT, D])
        xn_t = sb("xn_t", [P, DC, L])
        out_t = sb("out_t", [P, DC, L])
        rec_b = sb("rec_b", [P, L])
        rec = sb("rec", [QW, QT, HC])
        rec_x = sb("rec_x", [QW, QT, HC * DH])
        gate_b = sb("gate_b", [P, S])
        bo_t = sb("bo_t", [P, D])
        ident = sb("ident", [P, P])
        neg_max = sb("neg_max", [QW, 2, QT])
        row_sum = sb("row_sum", [QW, QT, H])
        bq_col = sb("bq_col", [P, DC])
        bk_col = sb("bk_col", [P, DC])
        bv_col = sb("bv_col", [P, DC])
        g_col = sb("g_col", [P, 1])
        tanh_g = sb("tanh_g", [P, 1])
        stats = sb("stats", [QW, QT, 6])
        moments = sb("moments", [QW, QT, 2])
        var_eps = sb("var_eps", [QW, QT])
        rstd0 = sb("rstd0", [QW, QT])
        rstd = sb("rstd", [QW, QT])
        newton = sb("newton", [QW, QT])
        minus_half = sb("minus_half", [P, QT])
        zero = sb("zero", [P, 1])
        e_max = sb("e_max", [B, 1])
        e_rec = sb("e_rec", [B, 1])
        token = sb("token", [P, 16])

        score = [ps(f"score{t}", [P, 1024]) for t in range(QT)]
        flip = [ps(f"flip{i}", [P, 512]) for i in range(2)]
        proj = ps("proj", [P, 512])
        pv = ps("pv", [P, 512])

        tabs_in = sem("tabs_in")
        ctxb_in = sem("ctxb_in")
        consts = sem("consts")
        w_hi = sem("w_hi")
        w_lo = sem("w_lo")
        energy_out = sem("energy_out")
        energy_in = sem("energy_in")
        gate_out = sem("gate_out")
        gate_ready = sem("gate_ready")
        tanh_ready = sem("tanh_ready")
        bvwo_done = sem("bvwo_done")
        bo_ready = sem("bo_ready")
        dve_chain = sem("dve_chain")
        raw_in = [sem(f"raw_in{r}") for r in range(2)]
        x_loaded = sem("x_loaded")
        gate_loaded = sem("gate_loaded")
        res_loaded = sem("res_loaded")
        x1_stored = sem("x1_stored")
        k_stacked = [sem(f"k_stacked{r}") for r in range(2)]
        q_stored = sem("q_stored")
        q_stacked = [sem(f"q_stacked{r}") for r in range(2)]
        ctx_hi_done = sem("ctx_hi_done")
        ctx_lo_done = sem("ctx_lo_done")
        var_ready = sem("var_ready")
        rstd0_ready = sem("rstd0_ready")
        xn_ready = sem("xn_ready")
        proj_done = sem("proj_done")
        proj_read = sem("proj_read")
        hi_done = sem("hi_done")
        lo_done = sem("lo_done")
        scored = [sem(f"scored{t}") for t in range(QT)]
        maxed = [sem(f"maxed{t}") for t in range(QT)]
        exped = [sem(f"exped{t}") for t in range(QT)]
        flipped = sem("flipped")
        copied_act = sem("copied_act")
        copied_dve = sem("copied_dve")
        rec_done = sem("rec_done")
        rec_x_done = sem("rec_x_done")
        pv_done = sem("pv_done")
        normed = sem("normed")
        out_done = sem("out_done")
        res_ready = sem("res_ready")
        res_done = sem("res_done")

        PRE = {"exped": 1, "flipped": 4, "pv_done": 1, "normed": 1, "rec_x_done": 1,
               "proj_read": 1, "lo_done": 1, "res_done": 2, "x1_stored": 16}
        K_SET, Q_SET = 16 * 4 * HC, 16 * 2

        def by_vector(h, p):
            return p == 1

        ACT_CHUNK, DVE_CHUNK = 2 * HC, HC

        def copied_before(h, p, vector):
            return sum(by_vector(i, j) == vector for i in range(h + 1) for j in range(3) if (i, j) <= (h, p))

        TABS = 16 * 9
        BATCH_LINKS = 6 + 2 * DC
        flat_t = probs_t[:, :, :, :].rearrange("p a b c -> p (a b c)")
        wv_tmp = probs[:, :, :, :].rearrange("p a b c -> p (a b c)")[:, 0:DC * D].rearrange("p (c n) -> p c n", c=DC)

        block = es.enter_context(nc.Block())

        @block.sync
        def _(sp):
            sp.dma_start(flat_t[0:B * KT, 0:KW * NF],
                         ctxb.rearrange("b (c t) f -> (b c) (t f)", c=KT)).then_inc(ctxb_in, 16)
            sp.dma_start(v_sb[:, 0:DC, :], wk.rearrange("(c p) n -> p c n", p=P)).then_inc(tabs_in, 16)

            def at_batch(first, each, n):
                value = first + each * n
                return value if isinstance(n, int) else sp.snap(sp.to_reg(value))

            def load_raw(n, d):
                sp.dma_start(ctx_raw[:, d % 2, :],
                             ctx_t[bass.ds(n, 1), :, d, :].rearrange("a p s -> p (a s)")).then_inc(raw_in[d % 2], 16)

            def load_x(n):
                sp.dma_start(x_in[:, :, :],
                             x[bass.ds(n, 1), :, :].rearrange("a (t p) d -> p (a t) d", p=QW)).then_inc(x_loaded, 16)

            def load_gate(n):
                sp.dma_start(gate_b[:, :], gate_dram[bass.ds(n, 1), :].broadcast_to([P, S])).then_inc(gate_loaded, 16)

            def store_q(n):
                sp.wait_ge(lo_done, PRE["lo_done"] + n * SPLITS + 2)
                for c in range(DC):
                    for part, q_sb in enumerate((q_hi, q_lo)):
                        sp.dma_start(q_dram[bass.ds(n, 1), c, :, part, :, :].rearrange("a j p q -> (a j) p q"),
                                     q_sb[:, c, :].bitcast(F32)).then_inc(q_stored, 16)

            def stack(n, c, heads_done=None):
                ring = c % 2
                split = at_batch(PRE["lo_done"] + 4 + 2 * c, SPLITS, n)
                stored = at_batch(16 * 2 * DC, 16 * 2 * DC, n)
                if heads_done is not None:
                    for t in range(QT):
                        sp.wait_ge(scored[t], heads_done)
                sp.wait_ge(lo_done, split)
                sp.wait_ge(q_stored, stored)
                for j in range(HC):
                    for row in range(4):
                        k_sb = k_hi if row < 2 else k_lo
                        sp.dma_start(k_stack[row * DH:(row + 1) * DH, ring * HC + j, :].bitcast(F32),
                                     k_sb[j * DH:(j + 1) * DH, c, :].bitcast(F32)).then_inc(k_stacked[ring], 16)
                for rep in range(2):
                    sp.dma_start(q_stack[rep * 64:(rep + 1) * 64, ring * HC:(ring + 1) * HC, :].bitcast(F32),
                                 q_dram[bass.ds(n, 1), c, :, :, :, :].rearrange("a j w p q -> (a w p) j q"))\
                        .then_inc(q_stacked[ring], 16)

            load_raw(0, 0)
            load_raw(0, 1)
            load_x(0)
            sp.dma_start(wv_tmp, wv.rearrange("(c p) n -> p c n", p=P)).then_inc(tabs_in, 16)
            sp.dma_start(wq_sb[:, :, :], wq.rearrange("(c p) n -> p c n", p=P)).then_inc(tabs_in, 16)
            sp.dma_start(wo_sb[:, :, :], wo.rearrange("(c p) n -> p c n", p=P)).then_inc(tabs_in, 16)
            sp.dma_start(bq_col[:, :], bq).then_inc(tabs_in, 16)
            sp.dma_start(bk_col[:, :], bk).then_inc(tabs_in, 16)
            sp.dma_start(bv_col[:, :], bv).then_inc(tabs_in, 16)
            sp.dma_start(bo_t[:, :], bo.rearrange("(a n) -> a n", a=1).broadcast_to([P, D])).then_inc(tabs_in, 16)
            sp.dma_start(g_col[:, :], g_xattn.rearrange("(a n) -> a n", a=1).broadcast_to([P, 1])).then_inc(tabs_in, 16)
            sp.wait_ge(dve_chain, 1)
            sp.dma_start(energy_dram.rearrange("b (c t) -> (b c) t", c=KT),
                         rec_b[0:B * KT, 0:KW]).then_inc(energy_out, 16)
            sp.wait_ge(energy_out, 16)
            sp.dma_start(gate_b[0:B, :], energy_dram).then_inc(energy_in, 16)
            for d in (2, 3):
                sp.wait_ge(ctx_lo_done, d - 1)
                load_raw(0, d)
            sp.wait_ge(gate_ready, 1)
            sp.dma_start(gate_dram, gate_b[0:B, :]).then_inc(gate_out, 16)
            sp.wait_ge(gate_out, 16)
            load_gate(0)
            store_q(0)
            stack(0, 0)
            stack(0, 1)

            def batch(b, last):
                n = b + 1
                if not last:
                    sp.wait_ge(proj_done, b * ITEMS + XT1 + 1)
                    load_x(n)
                    for d in (0, 1):
                        sp.wait_ge(ctx_lo_done, b * DC + d + 3)
                        load_raw(n, d)
                    sp.wait_ge(proj_read, PRE["proj_read"] + b * ITEMS + V0)
                    load_gate(n)
                sp.wait_ge(x1_stored, PRE["x1_stored"] + b * 16)
                sp.dma_start(x_res[:, :, :], x[bass.ds(b, 1), :, :].rearrange("a (t p) d -> p (a t) d", p=QW))\
                    .then_inc(res_loaded, 16)
                stack(b, 2, at_batch(HC, H, b))
                if not last:
                    for d in (2, 3):
                        sp.wait_ge(ctx_lo_done, n * DC + d - 1)
                        load_raw(n, d)
                stack(b, 3, at_batch(2 * HC, H, b))
                if not last:
                    store_q(n)
                    for c in range(2):
                        stack(n, c, at_batch((c + 3) * HC, H, b))
                sp.wait_ge(res_done, PRE["res_done"] + b * QT + QT)
                sp.dma_start(x1[bass.ds(b * L, L), :].rearrange("(t p) d -> p t d", p=QW), x_res[:, :, :])\
                    .then_inc(x1_stored, 16)

            with sp.Fori(0, B - 1) as b:
                batch(b, False)
            batch(B - 1, True)
            sp.wait_ge(x1_stored, PRE["x1_stored"] + B * 16)

        @block.gpsimd
        def _(pool):
            pool.memset(ident[:, :], 0.0).then_inc(consts, 1)
            pool.memset(minus_half[:, :], -0.5).then_inc(consts, 1)
            pool.memset(zero[:, :], 0.0).then_inc(consts, 1)
            pool.wait_ge(consts, 3)
            pool.affine_select(out=ident[:, :], in_=ident[:, :], compare_op=ALU.not_equal, fill=1.0,
                               base=0, pattern=[[-1, P]], channel_multiplier=1).then_inc(consts, 1)
            pool.wait_ge(consts, 4)

            def remainder(lo, full, hi):
                return nc.gpsimd.tensor_tensor(lo, full, hi.bitcast(F32), ALU.subtract)

            def norm_power(n):
                pool.wait_ge(var_ready, n + 1)
                nc.gpsimd.tensor_tensor(rstd0[:, :], var_eps[:, :], minus_half[0:QW, :], ALU.pow).then_inc(rstd0_ready, 1)

            def ctx_remainder(n, d):
                pool.wait_ge(ctx_hi_done, n * DC + d + 1)
                remainder(ctx_lo[:, d, :], ctx_raw[:, d % 2, :], ctx_hi[:, d, :]).then_inc(ctx_lo_done, 1)

            def split_remainder(n, i):
                pool.wait_ge(hi_done, n * SPLITS + i + 1)
                if i < 2:
                    remainder(q_lo[:, 2 * i:2 * i + 2, :].rearrange("p c q -> p (c q)"), fresh[:, :],
                              q_hi[:, 2 * i:2 * i + 2, :].rearrange("p c q -> p (c q)")).then_inc(lo_done, 1)
                else:
                    c, half = divmod(i - 2, 2)
                    at, w = half * HALF_K[0], HALF_K[half]
                    remainder(k_lo[:, c, at:at + w], fresh[:, 0:w], k_hi[:, c, at:at + w]).then_inc(lo_done, 1)

            def spread_reciprocals(b, c):
                pool.wait_ge(rec_done, b * DC + c + 1)
                pool.wait_ge(pv_done, PRE["pv_done"] + b * DC + c)
                nc.gpsimd.tensor_tensor(rec_x[:, :, :].rearrange("p t (h w) -> p (t h) w", w=DH),
                                        rec[:, :, :].rearrange("p t h -> p (t h)").unsqueeze(2).broadcast_to([QW, QT * HC, DH]),
                                        zero[0:QW, :].unsqueeze(2).broadcast_to([QW, QT * HC, DH]), ALU.add)\
                    .then_inc(rec_x_done, 1)

            pool.wait_ge(tabs_in, TABS)
            for i, (lo, tmp, hi) in enumerate(((wk_lo, v_sb[:, 0:DC, :], wk_hi), (wv_lo, wv_tmp, wv_hi))):
                pool.wait_ge(w_hi, i + 1)
                remainder(lo[:, :, :], tmp, hi[:, :, :]).then_inc(w_lo, 1)
            norm_power(0)
            for d in range(DC):
                ctx_remainder(0, d)
            for i in range(SPLITS):
                split_remainder(0, i)

            def batch(b, last):
                n = b + 1
                if not last:
                    norm_power(n)
                pool.wait_ge(res_loaded, b * 16 + 16)
                pool.wait_ge(bo_ready, 1)
                nc.gpsimd.tensor_tensor(x_res[:, :, :], x_res[:, :, :],
                                        bo_t[0:QW, :].unsqueeze(1).broadcast_to([QW, QT, D]), ALU.add).then_inc(res_ready, 1)
                spread_reciprocals(b, 0)
                if not last:
                    for d in range(DC):
                        ctx_remainder(n, d)
                    split_remainder(n, 0)
                    split_remainder(n, 1)
                spread_reciprocals(b, 1)
                if not last:
                    for i in range(2, 5):
                        split_remainder(n, i)
                spread_reciprocals(b, 2)
                if not last:
                    for i in range(5, SPLITS - 1):
                        split_remainder(n, i)
                spread_reciprocals(b, 3)
                if not last:
                    split_remainder(n, SPLITS - 1)

            with pool.Fori(0, B - 1) as b:
                batch(b, False)
            batch(B - 1, True)

        @block.scalar
        def _(act):
            act.wait_ge(tabs_in, TABS)
            act.activation(tanh_g[:, :], g_col[:, :], ACT.Tanh).then_inc(tanh_ready, 1)

            def exponentials(b, h):
                for t in range(QT):
                    act.wait_ge(maxed[t], b * H + h + 1)
                    act.wait_ge(flipped, PRE["flipped"] + b * 3 * H + 3 * (h - 1))
                    act.activation(probs[0:QW, h % 2, t, :], score[t][0:QW, 0:S], ACT.Exp,
                                   bias=neg_max[:, h % 2, t:t + 1], accum_out=row_sum[:, t, h:h + 1]).then_inc(exped[t], 1)

            def copy_flipped(b, h, pieces=range(3)):
                for p in pieces:
                    if not by_vector(h, p):
                        act.wait_ge(flipped, PRE["flipped"] + b * 3 * H + 3 * h + p + 1)
                        act.activation(probs_t[0:KW, h % HC, 2 * p:2 * p + 2, :].rearrange("k a q -> k (a q)"),
                                       flip[(3 * h + p) % 2][0:KW, 0:2 * L], ACT.Relu).then_inc(copied_act, 1)

            def copy_values(n, kt):
                act.wait_ge(proj_done, n * ITEMS + V0 + kt + 1)
                act.activation(v_sb[0:KW, kt, :], proj[0:KW, :], ACT.Copy).then_inc(proj_read, 1)

            def split_high(n, i, first):
                act.wait_ge(proj_read, PRE["proj_read"] + n * ITEMS + Q0 + i + 1)
                if i < 2:
                    if not first:
                        act.wait_ge(q_stored, n * 16 * 2 * DC)
                    act.activation(q_hi[:, 2 * i:2 * i + 2, :].rearrange("p c q -> p (c q)"), fresh[:, :], ACT.Copy)\
                        .then_inc(hi_done, 1)
                else:
                    c, half = divmod(i - 2, 2)
                    at, w = half * HALF_K[0], HALF_K[half]
                    if not first:
                        act.wait_ge(k_stacked[c % 2], K_SET * (2 * n + c // 2 - 1))
                    act.activation(k_hi[:, c, at:at + w], fresh[:, 0:w], ACT.Copy).then_inc(hi_done, 1)

            for i in range(SPLITS):
                split_high(0, i, True)
            copy_values(0, 0)
            exponentials(0, 0)

            def batch(b, last):
                n = b + 1
                for h in range(H):
                    if h in ATTEND_HEADS:
                        exponentials(b, h)
                        copy_flipped(b, h - 1)
                    elif h:
                        copy_flipped(b, h - 1, (0, 1))
                        exponentials(b, h)
                        copy_flipped(b, h - 1, (2,))
                    if h in VALUE_HEADS:
                        copy_values(b, h + 1)
                    if not last and h in SPLIT_HEADS:
                        split_high(n, SPLIT_HEADS.index(h), False)
                copy_flipped(b, H - 1)
                if not last:
                    split_high(n, SPLITS - 1, False)
                    exponentials(n, 0)
                    copy_values(n, 0)

            with act.Fori(0, B - 1) as b:
                batch(b, False)
            batch(B - 1, True)

        @block.vector
        def _(dve):
            links = [0]

            def link(ins, base=0):
                links[0] += 1
                ins.then_inc(dve_chain, 1)
                dve.wait_ge(dve_chain, base + links[0])

            free = {"exped": exped, "flipped": [flipped], "pv_done": [pv_done], "normed": [normed],
                    "rec_x_done": [rec_x_done], "proj_read": [proj_read], "lo_done": [lo_done],
                    "res_done": [res_done], "x1_stored": [x1_stored]}
            given = [(s, PRE[name]) for name, sems in free.items() for s in sems]
            for i, (s, count) in enumerate(given):
                nc.vector.memset(token[:, i:i + 1], 0.0).then_inc(s, count)

            dve.wait_ge(ctxb_in, 16)
            link(nc.vector.tensor_reduce(rec_b[0:B * KT, 0:KW],
                                         flat_t[0:B * KT, 0:KW * NF].rearrange("p (t f) -> p t f", f=NF),
                                         axis=AX.X, op=ALU.add, apply_absolute_value=True))
            dve.wait_ge(tabs_in, TABS)
            nc.vector.tensor_copy(wk_hi[:, :, :], v_sb[:, 0:DC, :]).then_inc(w_hi, 1)
            nc.vector.tensor_copy(wv_hi[:, :, :], wv_tmp).then_inc(w_hi, 1)

            def norm_statistics(n, base):
                dve.wait_ge(x_loaded, n * 16 + 16)
                nc.vector.bn_stats(stats[:, 0, :], x_in[:, 0, :])
                link(nc.vector.bn_stats(stats[:, 1, :], x_in[:, 1, :]), base)
                nc.vector.memset(token[:, 15:16], 0.0)
                nc.vector.bn_aggr(moments[:, 0, :], stats[:, 0, :])
                link(nc.vector.bn_aggr(moments[:, 1, :], stats[:, 1, :]), base)
                nc.vector.tensor_scalar(var_eps[:, :], moments[:, :, 1], EPS, None, ALU.add).then_inc(var_ready, 1)

            def normalize(n, base):
                dve.wait_ge(rstd0_ready, n + 1)
                link(nc.vector.tensor_tensor(newton[:, :], rstd0[:, :], rstd0[:, :], ALU.mult), base)
                link(nc.vector.tensor_tensor(newton[:, :], newton[:, :], var_eps[:, :], ALU.mult), base)
                link(nc.vector.tensor_scalar(newton[:, :], newton[:, :], -0.5, 1.5, ALU.mult, ALU.add), base)
                link(nc.vector.tensor_tensor(rstd[:, :], rstd0[:, :], newton[:, :], ALU.mult), base)
                for t in range(QT):
                    nc.vector.tensor_scalar(x_in[:, t, :], x_in[:, t, :], moments[:, t, 0:1], rstd[:, t:t + 1],
                                            ALU.subtract, ALU.mult).then_inc(xn_ready, 1)

            def ctx_high(n, d, first):
                ring = d % 2
                dve.wait_ge(raw_in[ring], 16 * (2 * n + d // 2 + 1))
                if not first:
                    dve.wait_ge(proj_done, n * ITEMS)
                nc.vector.tensor_copy(ctx_hi[:, d, :], ctx_raw[:, ring, :]).then_inc(ctx_hi_done, 1)

            def copy_xt(n, t):
                dve.wait_ge(proj_done, n * ITEMS + XT0 + t + 1)
                nc.vector.tensor_copy(xn_t[:, :, t * QW:(t + 1) * QW],
                                      proj[:, 0:DC * QW].rearrange("p (c q) -> p c q", c=DC)).then_inc(proj_read, 1)

            def read_split(n, i):
                dve.wait_ge(proj_done, n * ITEMS + Q0 + i + 1)
                dve.wait_ge(lo_done, PRE["lo_done"] + n * SPLITS + i)
                if i < 2:
                    for k in range(2):
                        c = 2 * i + k
                        ins = nc.vector.tensor_scalar(fresh[:, k * L:(k + 1) * L], proj[:, k * L:(k + 1) * L],
                                                      bq_col[:, c:c + 1], None, ALU.add)
                    ins.then_inc(proj_read, 1)
                else:
                    c, half = divmod(i - 2, 2)
                    at, w = half * HALF_K[0], HALF_K[half]
                    if i == 2:
                        dve.wait_ge(gate_loaded, n * 16 + 16)
                    nc.vector.scalar_tensor_tensor(fresh[:, 0:w], proj[:, 0:w], bk_col[:, c:c + 1],
                                                   gate_b[:, at:at + w], ALU.add, ALU.mult).then_inc(proj_read, 1)

            def maxima(b, h):
                for t in range(QT):
                    dve.wait_ge(scored[t], b * H + h + 1)
                    nc.vector.tensor_reduce(neg_max[:, h % 2, t:t + 1], score[t][0:QW, 0:S], axis=AX.X, op=ALU.max,
                                            negate=True).then_inc(maxed[t], 1)

            def copy_flipped(b, h):
                for p in range(3):
                    if by_vector(h, p):
                        dve.wait_ge(flipped, PRE["flipped"] + b * 3 * H + 3 * h + p + 1)
                        nc.vector.tensor_scalar(probs_t[0:KW, h % HC, 2 * p:2 * p + 2, :].rearrange("k a q -> k (a q)"),
                                                flip[(3 * h + p) % 2][0:KW, 0:2 * L], 0.0, None, ALU.max)\
                            .then_inc(copied_dve, 1)

            def reciprocals(b, c, base):
                for t in range(QT):
                    dve.wait_ge(exped[t], PRE["exped"] + b * H + (c + 1) * HC)
                dve.wait_ge(rec_x_done, PRE["rec_x_done"] + b * DC + c)
                link(nc.vector.reciprocal(rec[:, :, :], row_sum[:, :, c * HC:(c + 1) * HC]), base)
                nc.vector.tensor_scalar(rec[:, :, :], rec[:, :, :], 0.0, None, ALU.max).then_inc(rec_done, 1)

            def normalize_output(b, c, base):
                dve.wait_ge(pv_done, PRE["pv_done"] + b * DC + c + 1)
                link(nc.vector.tensor_copy(rec_b[:, :], pv[:, L:2 * L]), base)
                nc.vector.tensor_tensor(out_t[:, c, :], pv[:, 0:L], rec_b[:, :], ALU.mult).then_inc(normed, 1)

            norm_statistics(0, 0)
            dve.wait_ge(energy_in, 16)
            link(nc.vector.tensor_reduce(e_max[:, :], gate_b[0:B, :], axis=AX.X, op=ALU.max))
            link(nc.vector.tensor_scalar(e_max[:, :], e_max[:, :], 1.0 / NF, 1e-8, ALU.mult, ALU.add))
            link(nc.vector.reciprocal(e_rec[:, :], e_max[:, :]))
            link(nc.vector.tensor_scalar(gate_b[0:B, :], gate_b[0:B, :], 1.0 / NF, e_rec[:, :], ALU.mult, ALU.mult))
            link(nc.vector.tensor_scalar(gate_b[0:B, :], gate_b[0:B, :], THRESHOLD, 1.0 - GATE_LOW, ALU.is_gt, ALU.mult))
            nc.vector.tensor_scalar(gate_b[0:B, :], gate_b[0:B, :], GATE_LOW, SCORE_SCALE, ALU.add, ALU.mult)\
                .then_inc(gate_ready, 1)
            normalize(0, 0)
            for d in range(DC):
                ctx_high(0, d, True)
            dve.wait_ge(bvwo_done, 1)
            dve.wait_ge(tanh_ready, 1)
            link(nc.vector.tensor_tensor(bo_t[:, :], pv[:, :], bo_t[:, :], ALU.add))
            nc.vector.tensor_scalar(bo_t[:, :], bo_t[:, :], tanh_g[:, :], None, ALU.mult).then_inc(bo_ready, 1)
            for t in range(QT):
                copy_xt(0, t)
            for i in range(SPLITS):
                read_split(0, i)
            maxima(0, 0)
            setup_links = links[0]

            def batch(b, last):
                n = b + 1
                base = setup_links + b * BATCH_LINKS
                links[0] = 0
                for h in range(H):
                    if h and h % HC == 0:
                        reciprocals(b, h // HC - 1, base)
                    if h:
                        maxima(b, h)
                    if h in ATTEND_HEADS:
                        normalize_output(b, ATTEND_HEADS.index(h), base)
                    if h == XT_HEAD and not last:
                        copy_xt(n, 0)
                    if h:
                        copy_flipped(b, h - 1)
                    if not last:
                        if h == 2:
                            norm_statistics(n, base)
                        if h == 3:
                            normalize(n, base)
                        if h == XT_HEAD:
                            copy_xt(n, 1)
                            ctx_high(n, 0, False)
                            ctx_high(n, 1, False)
                        if h == XT_HEAD + 1:
                            ctx_high(n, 2, False)
                        if h == XT_HEAD + 2:
                            ctx_high(n, 3, False)
                        if h in SPLIT_HEADS:
                            read_split(n, SPLIT_HEADS.index(h))
                reciprocals(b, DC - 1, base)
                copy_flipped(b, H - 1)
                if not last:
                    read_split(n, SPLITS - 1)
                normalize_output(b, DC - 1, base)
                if not last:
                    maxima(n, 0)
                dve.wait_ge(res_ready, b + 1)
                for t in range(QT):
                    dve.wait_ge(out_done, b * QT + t + 1)
                    nc.vector.scalar_tensor_tensor(x_res[:, t, :], flip[t][0:QW, :], tanh_g[0:QW, :], x_res[:, t, :],
                                                   ALU.mult, ALU.add).then_inc(res_done, 1)
                return links[0]

            with dve.Fori(0, B - 1) as b:
                assert batch(b, False) == BATCH_LINKS
            batch(B - 1, True)

        @block.tensor
        def _(pe):
            pe.wait_ge(consts, 4)
            pe.wait_ge(tabs_in, TABS)
            for c in range(DC):
                ins = nc.tensor.matmul(pv[:, :], bv_col[:, c:c + 1].broadcast_to([P, P]), wo_sb[:, c, :],
                                       start=(c == 0), stop=(c == DC - 1))
            ins.then_inc(bvwo_done, 1)

            def take_proj(n, i):
                pe.wait_ge(proj_read, PRE["proj_read"] + n * ITEMS + i)

            def transpose_x(n, t):
                take_proj(n, XT0 + t)
                pe.wait_ge(xn_ready, n * QT + t + 1)
                for c in range(DC):
                    ins = nc.tensor.transpose(proj[:, c * QW:(c + 1) * QW], x_in[:, t, c * P:(c + 1) * P],
                                              ident[0:QW, 0:QW])
                ins.then_inc(proj_done, 1)

            def project_q(n, i):
                take_proj(n, Q0 + i)
                for k in range(2):
                    c = 2 * i + k
                    for d in range(DC):
                        ins = nc.tensor.matmul(proj[:, k * L:(k + 1) * L], wq_sb[:, d, c * P:(c + 1) * P], xn_t[:, d, :],
                                               start=(d == 0), stop=(d == DC - 1))
                ins.then_inc(proj_done, 1)

            def project_k(n, i):
                c, half = divmod(i, 2)
                at, w = half * HALF_K[0], HALF_K[half]
                take_proj(n, K0 + i)
                if i == 0:
                    pe.wait_ge(ctx_lo_done, n * DC + DC)
                for d in range(DC):
                    for k, (wp, xp) in enumerate(((wk_hi, ctx_hi), (wk_hi, ctx_lo), (wk_lo, ctx_hi))):
                        ins = nc.tensor.matmul(proj[:, 0:w], wp[:, d, c * P:(c + 1) * P], xp[:, d, at:at + w],
                                               start=(d == 0 and k == 0), stop=(d == DC - 1 and k == 2))
                ins.then_inc(proj_done, 1)

            def split_item(n, i):
                if i < 2:
                    project_q(n, i)
                else:
                    project_k(n, i - 2)

            def project_v(n, kt):
                take_proj(n, V0 + kt)
                for d in range(DC):
                    for k, (xp, wp) in enumerate(((ctx_hi, wv_hi), (ctx_hi, wv_lo), (ctx_lo, wv_hi))):
                        ins = nc.tensor.matmul(proj[0:KW, :], xp[:, d, kt * KW:(kt + 1) * KW], wp[:, d, :],
                                               start=(d == 0 and k == 0), stop=(d == DC - 1 and k == 2))
                ins.then_inc(proj_done, 1)

            def scores(b, h):
                c = h // HC
                if h % HC == 0:
                    pe.wait_ge(k_stacked[c % 2], K_SET * (2 * b + c // 2 + 1))
                    pe.wait_ge(q_stacked[c % 2], Q_SET * (2 * b + c // 2 + 1))
                slot = h % (2 * HC)
                for t in range(QT):
                    pe.wait_ge(exped[t], PRE["exped"] + b * H + h)
                    at = 0
                    for w in HALF_N:
                        ins = nc.tensor.matmul(score[t][0:QW, at:at + w], q_stack[:, slot, t * QW:(t + 1) * QW],
                                               k_stack[:, slot, at:at + w], start=True, stop=True)
                        at += w
                    ins.then_inc(scored[t], 1)

            def wait_copied(b, h, p):
                vector = by_vector(h, p)
                done, each = (copied_dve, DVE_CHUNK) if vector else (copied_act, ACT_CHUNK)
                pe.wait_ge(done, b * DC * each + copied_before(h, p, vector))

            def flip_probs(b, h, pieces):
                if pieces[0] == 0:
                    for t in range(QT):
                        pe.wait_ge(exped[t], PRE["exped"] + b * H + h + 1)
                for p in pieces:
                    g = 3 * h + p
                    if g < 2:
                        pe.wait_ge(res_done, PRE["res_done"] + (b - 1) * QT + g + 1)
                    else:
                        wait_copied(b, (g - 2) // 3, (g - 2) % 3)
                    for k in range(2):
                        for t in range(QT):
                            kt = 2 * p + k
                            ins = nc.tensor.transpose(flip[g % 2][0:KW, k * L + t * QW:k * L + (t + 1) * QW],
                                                      probs[0:QW, h % 2, t, kt * KW:(kt + 1) * KW], ident[0:QW, 0:QW])
                    ins.then_inc(flipped, 1)

            def attend(b, c):
                pe.wait_ge(normed, PRE["normed"] + b * DC + c)
                pe.wait_ge(rec_x_done, PRE["rec_x_done"] + b * DC + c + 1)
                for t in range(QT):
                    nc.tensor.matmul(pv[:, L + t * QW:L + (t + 1) * QW], rec_x[:, t, :], ident[0:QW, 0:QW],
                                     start=True, stop=True)
                if c == 0:
                    pe.wait_ge(proj_read, PRE["proj_read"] + b * ITEMS + ITEMS)
                h = c * HC + HC - 1
                pe.wait_ge(copied_act, b * DC * ACT_CHUNK + copied_before(h, 2, False))
                pe.wait_ge(copied_dve, b * DC * DVE_CHUNK + copied_before(h, 2, True))
                for kt in range(KT):
                    for j in range(HC):
                        at = (c * HC + j) * DH
                        ins = nc.tensor.matmul(pv[j * DH:(j + 1) * DH, 0:L], v_sb[0:KW, kt, at:at + DH],
                                               probs_t[0:KW, j, kt, :], start=(kt == 0), stop=(kt == KT - 1))
                ins.then_inc(pv_done, 1)

            def project_out(b, t):
                pe.wait_ge(normed, PRE["normed"] + b * DC + DC)
                for c in range(DC):
                    ins = nc.tensor.matmul(flip[t][0:QW, :], out_t[:, c, t * QW:(t + 1) * QW], wo_sb[:, c, :],
                                           start=(c == 0), stop=(c == DC - 1))
                ins.then_inc(out_done, 1)

            for t in range(QT):
                transpose_x(0, t)
            for i in range(2):
                project_q(0, i)
            pe.wait_ge(w_lo, 2)
            for i in range(2 * DC):
                project_k(0, i)
            project_v(0, 0)
            scores(0, 0)

            def batch(b, last):
                n = b + 1
                for h in range(H):
                    if h:
                        scores(b, h)
                        if h in ATTEND_HEADS:
                            attend(b, ATTEND_HEADS.index(h))
                        if h == XT_HEAD and not last:
                            transpose_x(n, 0)
                        flip_probs(b, h - 1, (0, 1))
                    if h in VALUE_HEADS:
                        project_v(b, h + 1)
                    elif not last:
                        if h == XT_HEAD:
                            transpose_x(n, 1)
                        elif h in SPLIT_HEADS:
                            split_item(n, SPLIT_HEADS.index(h))
                    if h:
                        flip_probs(b, h - 1, (2,))
                flip_probs(b, H - 1, (0,))
                if not last:
                    split_item(n, SPLITS - 1)
                flip_probs(b, H - 1, (1, 2))
                attend(b, DC - 1)
                if not last:
                    scores(n, 0)
                    project_v(n, 0)
                for t in range(QT):
                    project_out(b, t)

            with pe.Fori(0, B - 1) as b:
                batch(b, False)
            batch(B - 1, True)


E_R, TOP, MID = 16, 2, 128
MID_S = 512
GATE_UP = 2 * MID
NTK = B * QT
GT = 4
GROUPS, GTOK = NTK // GT, GT * QW
SLOT_TILES = TOP * T // P + E_R
ASTEP = 4
MAX_TILES = T // P


def experts_phase(nc, x1, g_ffn, router_w, w_gu, w_d, ws_gu, ws_d, out):
    xn_rows = nc.dram_tensor("xn_rows", (T, D), F32, kind="Internal").ap()
    xn_cols = nc.dram_tensor("xn_cols", (GROUPS, P, DC, GTOK), F32, kind="Internal").ap()
    y_slots = nc.dram_tensor("y_slots", (SLOT_TILES * P, D), F32, kind="Internal").ap()

    outer = ExitStack()
    with outer:
        def sb(name, shape, dt=F32):
            return outer.enter_context(nc.sbuf_tensor(name, shape, dt))

        shared = {
            "gu_hi": sb("sgu_hi", [P, DC, 2 * MID_S], F32R), "gu_lo": sb("sgu_lo", [P, DC, 2 * MID_S], F32R),
            "d_hi": sb("sd_hi", [P, DC, D], F32R), "d_lo": sb("sd_lo", [P, DC, D], F32R),
        }
        tanh_g2 = sb("tanh_g2", [P, 1])
        weight = sb("weight", [QW, TOP, NTK])
        slot_i = sb("slot_i", [QW, TOP, NTK], I32)
        inner = ExitStack()
        with inner:
            def sbi(name, shape, dt=F32):
                return inner.enter_context(nc.sbuf_tensor(name, shape, dt))

            gu_sb = sbi("gu_sb", [P, E_R, DC, GATE_UP])
            d_sb = sbi("d_sb", [P, E_R, D])
            ident2 = sbi("ident2", [P, P])
            slot_token = sbi("slot_token", [P, SLOT_TILES], I32)
            tile_expert = sbi("tile_expert", [P, SLOT_TILES], I32)
            prev_expert = sbi("prev_expert", [P, SLOT_TILES], I32)
            routed_in = inner.enter_context(nc.semaphore("routed_in"))
            with nc.psum_tensor("logit", [P, NTK * E_R], F32) as logit:
                normalize_tokens(nc, x1, g_ffn, router_w, w_gu, w_d, ws_gu, ws_d, xn_rows, xn_cols,
                                 shared, tanh_g2, gu_sb, d_sb, ident2, routed_in, logit)
                assign_slots(nc, tanh_g2, weight, slot_i, slot_token, tile_expert, prev_expert, logit)
            routed_experts(nc, xn_rows, y_slots, gu_sb, d_sb, ident2, slot_token, tile_expert, prev_expert, routed_in)
        shared_and_combine(nc, x1, xn_cols, y_slots, shared, tanh_g2, weight, slot_i, out)


def normalize_tokens(nc, x1, g_ffn, router_w, w_gu, w_d, ws_gu, ws_d, xn_rows, xn_cols,
                     shared, tanh_g2, gu_sb, d_sb, ident2, routed_in, logit):
    es = ExitStack()
    with es:
        def sb(name, shape, dt=F32):
            return es.enter_context(nc.sbuf_tensor(name, shape, dt))

        def sem(name):
            return es.enter_context(nc.semaphore(name))

        rw_sb = sb("rw_sb", [P, DC, E_R])
        g_col2 = sb("g_col2", [P, 1])
        sgu_raw = sb("sgu_raw", [P, DC, 2 * MID_S])
        sd_raw = sb("sd_raw", [P, DC, D])
        rows = sb("rows", [QW, 2, GT, D])
        cols = sb("cols", [P, 2, DC, GTOK])
        minus_half2 = sb("minus_half2", [P, GT])
        stats2 = sb("stats2", [QW, GT, 6])
        moments2 = sb("moments2", [QW, GT, 2])
        var2 = sb("var2", [QW, GT])
        r0 = sb("r0", [QW, GT])
        r1 = sb("r1", [QW, GT])
        nw = sb("nw", [QW, GT])
        token2 = sb("token2", [P, 4])
        turn = [es.enter_context(nc.psum_tensor(f"turn{t}", [P, 512], F32)) for t in range(GT)]

        small_in = sem("small_in")
        shared_in = sem("shared_in")
        shared_hi = sem("shared_hi")
        consts2 = sem("consts2")
        tanh2 = sem("tanh2")
        x1_in = [sem(f"x1_in{r}") for r in range(2)]
        chain2 = sem("chain2")
        var2_ready = sem("var2_ready")
        r0_ready = sem("r0_ready")
        xn2_ready = sem("xn2_ready")
        turned = sem("turned")
        cols_ready = sem("cols_ready")
        rows_stored = [sem(f"rows_stored{r}") for r in range(2)]
        cols_stored = [sem(f"cols_stored{r}") for r in range(2)]
        split_done = sem("split_done")

        block = es.enter_context(nc.Block())
        PAIRS = GROUPS // 2

        @block.sync
        def _(sp):
            def load(g, r):
                sp.dma_start(rows[:, r, :, :], x1[bass.ds(g * GTOK, GTOK), :].rearrange("(t p) d -> p t d", p=QW))\
                    .then_inc(x1_in[r], 16)

            sp.dma_start(rw_sb[:, :, :], router_w.rearrange("(c p) e -> p c e", p=P)).then_inc(small_in, 16)
            sp.dma_start(g_col2[:, :], g_ffn.rearrange("(a n) -> a n", a=1).broadcast_to([P, 1])).then_inc(small_in, 16)
            for r in range(2):
                load(r, r)

            def pair(i, last):
                for r in range(2):
                    g = 2 * i + r
                    sp.wait_ge(xn2_ready, GT * g + GT)
                    sp.dma_start(xn_rows[bass.ds(g * GTOK, GTOK), :].rearrange("(t p) d -> p t d", p=QW), rows[:, r, :, :])\
                        .then_inc(rows_stored[r], 16)
                    sp.wait_ge(cols_ready, GT * g + GT)
                    sp.dma_start(xn_cols[bass.ds(g, 1), :, :, :].rearrange("a p c q -> p (a c) q"), cols[:, r, :, :])\
                        .then_inc(cols_stored[r], 16)
                    if not last:
                        sp.wait_ge(rows_stored[r], 16 * i + 16)
                        load(g + 2, r)

            with sp.Fori(0, PAIRS - 1) as i:
                pair(i, False)
            pair(PAIRS - 1, True)
            for r in range(2):
                sp.wait_ge(rows_stored[r], 16 * PAIRS)
                sp.wait_ge(cols_stored[r], 16 * PAIRS + 16)

        @block.gpsimd
        def _(pool):
            pool.memset(ident2[:, :], 0.0).then_inc(consts2, 1)
            pool.memset(minus_half2[:, :], -0.5).then_inc(consts2, 1)
            pool.wait_ge(consts2, 2)
            pool.affine_select(out=ident2[:, :], in_=ident2[:, :], compare_op=ALU.not_equal, fill=1.0,
                               base=0, pattern=[[-1, P]], channel_multiplier=1).then_inc(consts2, 1)
            pool.wait_ge(consts2, 3)
            with pool.Fori(0, GROUPS) as g:
                pool.wait_ge(var2_ready, g + 1)
                nc.gpsimd.tensor_tensor(r0[:, :], var2[:, :], minus_half2[0:QW, :], ALU.pow).then_inc(r0_ready, 1)

        @block.scalar
        def _(act):
            act.dma_start(sgu_raw[:, :, :], ws_gu).then_inc(shared_in, 16)
            act.dma_start(sd_raw[:, :, :], ws_d.rearrange("(c p) n -> p c n", p=P)).then_inc(shared_in, 16)
            act.dma_start(gu_sb[:, :, :, :].rearrange("p e c m -> p (e c m)"), w_gu).then_inc(routed_in, 16)
            act.dma_start(d_sb[:, :, :], w_d.rearrange("e m n -> m e n")).then_inc(routed_in, 16)
            act.wait_ge(small_in, 32)
            act.activation(tanh_g2[:, :], g_col2[:, :], ACT.Tanh).then_inc(tanh2, 1)
            with act.Fori(0, PAIRS) as i:
                for r in range(2):
                    for t in range(GT):
                        act.wait_ge(turned, (2 * i + r) * GT + t + 1)
                        if t == 0:
                            act.wait_ge(cols_stored[r], 16 * i + 16)
                        act.activation(cols[:, r, :, t * QW:(t + 1) * QW],
                                       turn[t][:, 0:DC * QW].rearrange("p (c q) -> p c q", c=DC), ACT.Copy)\
                            .then_inc(cols_ready, 1)
            act.wait_ge(shared_in, 32)
            act.activation(shared["gu_hi"][:, :, :], sgu_raw[:, :, :], ACT.Copy).then_inc(shared_hi, 1)
            act.activation(shared["d_hi"][:, :, :], sd_raw[:, :, :], ACT.Copy).then_inc(shared_hi, 1)

        @block.vector
        def _(dve):
            links = [0]

            def link(ins, base):
                links[0] += 1
                ins.then_inc(chain2, 1)
                dve.wait_ge(chain2, base + links[0])

            LINKS = 12
            for r in range(2):
                nc.vector.memset(token2[:, r:r + 1], 0.0).then_inc(cols_stored[r], 16)
            dve.wait_ge(consts2, 3)
            with dve.Fori(0, PAIRS) as i:
                base = i * LINKS
                for r in range(2):
                    dve.wait_ge(x1_in[r], i * 16 + 16)
                    for t in range(GT):
                        ins = nc.vector.bn_stats(stats2[:, t, :], rows[:, r, t, :])
                    link(ins, base)
                    nc.vector.memset(token2[:, 2:3], 0.0)
                    for t in range(GT):
                        ins = nc.vector.bn_aggr(moments2[:, t, :], stats2[:, t, :])
                    link(ins, base)
                    nc.vector.tensor_scalar(var2[:, :], moments2[:, :, 1], EPS, None, ALU.add).then_inc(var2_ready, 1)
                    dve.wait_ge(r0_ready, 2 * i + r + 1)
                    link(nc.vector.tensor_tensor(nw[:, :], r0[:, :], r0[:, :], ALU.mult), base)
                    link(nc.vector.tensor_tensor(nw[:, :], nw[:, :], var2[:, :], ALU.mult), base)
                    link(nc.vector.tensor_scalar(nw[:, :], nw[:, :], -0.5, 1.5, ALU.mult, ALU.add), base)
                    link(nc.vector.tensor_tensor(r1[:, :], r0[:, :], nw[:, :], ALU.mult), base)
                    for t in range(GT):
                        nc.vector.tensor_scalar(rows[:, r, t, :], rows[:, r, t, :], moments2[:, t, 0:1], r1[:, t:t + 1],
                                                ALU.subtract, ALU.mult).then_inc(xn2_ready, 1)
                assert links[0] == LINKS
            for n, (lo, raw, hi) in enumerate(((shared["gu_lo"], sgu_raw, shared["gu_hi"]),
                                               (shared["d_lo"], sd_raw, shared["d_hi"]))):
                dve.wait_ge(shared_hi, n + 1)
                nc.vector.tensor_tensor(lo[:, :, :], raw[:, :, :], hi[:, :, :].bitcast(F32), ALU.subtract)\
                    .then_inc(split_done, 1)
            dve.wait_ge(split_done, 2)

        @block.tensor
        def _(pe):
            pe.wait_ge(consts2, 3)
            pe.wait_ge(small_in, 32)

            def tile(i, r, t, first):
                q = (2 * i + r) * GT + t
                pe.wait_ge(xn2_ready, q + 1)
                if not (first and r == 0):
                    pe.wait_ge(cols_ready, q - GT + 1)
                for c in range(DC):
                    ins = nc.tensor.transpose(turn[t][:, c * QW:(c + 1) * QW], rows[:, r, t, c * P:(c + 1) * P],
                                              ident2[0:QW, 0:QW])
                ins.then_inc(turned, 1)
                pe.wait_ge(cols_ready, q + 1)
                for c in range(DC):
                    nc.tensor.matmul(logit[0:QW, bass.ds(q * E_R, E_R)], cols[:, r, c, t * QW:(t + 1) * QW],
                                     rw_sb[:, c, :], start=(c == 0), stop=(c == DC - 1))

            for r in range(2):
                for t in range(GT):
                    tile(0, r, t, True)
            with pe.Fori(1, PAIRS) as i:
                for r in range(2):
                    for t in range(GT):
                        tile(i, r, t, False)


def assign_slots(nc, tanh_g2, weight, slot_i, slot_token, tile_expert, prev_expert, logit):
    es = ExitStack()
    with es:
        def sb(name, shape, dt=F32):
            return es.enter_context(nc.sbuf_tensor(name, shape, dt))

        def sem(name):
            return es.enter_context(nc.semaphore(name))

        PAD_T, PAD_E = NTK // 2, E_R // 2
        CHUNK = 16
        CHUNKS = TOP * NTK // CHUNK
        before = sb("before", [QW, P])
        ones = sb("ones", [QW, P])
        rev = sb("rev", [QW, E_R])
        slot_iota = sb("slot_iota", [QW, P])
        tile_iota = sb("tile_iota", [P, SLOT_TILES])
        fill = sb("fill", [P, MAX_TILES])
        token_id = sb("token_id", [QW, TOP, NTK])
        probs2 = sb("probs2", [QW, NTK, E_R])
        key = sb("key", [QW, NTK, E_R])
        picked = sb("picked", [QW, TOP, NTK, E_R])
        any_pick = sb("any_pick", [QW, NTK, E_R])
        slot_e = sb("slot_e", [QW, NTK, E_R])
        top = sb("top", [QW, NTK])
        denom = sb("denom", [QW, NTK])
        top_p = sb("top_p", [QW, TOP, NTK])
        run_t = [sb(f"run_t{i}", [P, PAD_T + NTK, E_R]) for i in range(2)]
        run_e = [sb(f"run_e{i}", [P, PAD_E + E_R]) for i in range(2)]
        full = sb("full", [P, E_R, MAX_TILES])
        passed = sb("passed", [P, SLOT_TILES, E_R])
        expert_f = sb("expert_f", [P, SLOT_TILES])
        slot_f = sb("slot_f", [QW, TOP, NTK])
        part_i = sb("part_i", [QW, 2, TOP, NTK], I32)
        part_f = sb("part_f", [QW, 2, TOP, NTK])
        row_hot = sb("row_hot", [QW, 2, CHUNK, P])
        tile_hot = sb("tile_hot", [QW, 2, CHUNK, SLOT_TILES])
        counts = es.enter_context(nc.psum_tensor("counts", [P, NTK * E_R], F32))
        earlier = es.enter_context(nc.psum_tensor("earlier", [P, NTK * E_R], F32))
        table = es.enter_context(nc.psum_tensor("table", [P, 512], F32))

        consts3 = sem("consts3")
        chain3 = sem("chain3")
        shifted = sem("shifted")
        exped2 = sem("exped2")
        picks_ready = sem("picks_ready")
        counted = sem("counted")
        hot_ready = sem("hot_ready")
        hot_used = sem("hot_used")
        CONSTS = 12

        block = es.enter_context(nc.Block())

        @block.gpsimd
        def _(pool):
            def iota(dst, pattern, base=0, step=0):
                pool.iota(dst, pattern=pattern, base=base, channel_multiplier=step,
                          allow_small_or_imprecise_dtypes=True).then_inc(consts3, 1)

            pool.memset(ones[:, :], 1.0).then_inc(consts3, 1)
            pool.memset(before[:, :], 1.0).then_inc(consts3, 1)
            iota(rev[:, :], [[-1, E_R]], base=E_R)
            iota(slot_iota[:, :], [[1, P]])
            iota(tile_iota[:, :], [[1, SLOT_TILES]])
            iota(fill[:, :], [[P, MAX_TILES]])
            iota(token_id[:, :, :], [[0, TOP], [QW, NTK]], step=1)
            for i in range(2):
                pool.memset(run_t[i][:, 0:PAD_T, :], 0.0).then_inc(consts3, 1)
            for i in range(2):
                pool.memset(run_e[i][:, 0:PAD_E], 0.0).then_inc(consts3, 1)
            pool.wait_ge(consts3, CONSTS - 1)
            pool.affine_select(out=before[:, :], in_=before[:, :], compare_op=ALU.is_gt, fill=0.0,
                               base=0, pattern=[[1, P]], channel_multiplier=-1).then_inc(consts3, 1)

        @block.scalar
        def _(act):
            act.wait_ge(shifted, 1)
            act.activation(probs2[:, :, :], probs2[:, :, :], ACT.Exp).then_inc(exped2, 1)

        @block.vector
        def _(dve):
            links = [0]

            def link(ins):
                links[0] += 1
                ins.then_inc(chain3, 1)
                dve.wait_ge(chain3, links[0])

            def by_expert(ap):
                return ap.unsqueeze(2).broadcast_to([QW, NTK, E_R])

            def by_token(ap):
                return ap.unsqueeze(1).broadcast_to([QW, NTK, E_R])

            logits = logit[0:QW, :].rearrange("p (t e) -> p t e", e=E_R)
            dve.wait_ge(consts3, CONSTS)
            link(nc.vector.tensor_reduce(top[:, :], logits, axis=AX.X, op=ALU.max))
            nc.vector.tensor_tensor(probs2[:, :, :], logits, by_expert(top[:, :]), ALU.subtract).then_inc(shifted, 1)
            dve.wait_ge(exped2, 1)
            link(nc.vector.tensor_reduce(top[:, :], probs2[:, :, :], axis=AX.X, op=ALU.add))
            link(nc.vector.reciprocal(denom[:, :], top[:, :]))
            link(nc.vector.tensor_tensor(probs2[:, :, :], probs2[:, :, :], by_expert(denom[:, :]), ALU.mult))
            for k in range(TOP):
                link(nc.vector.tensor_reduce(top_p[:, k, :], probs2[:, :, :], axis=AX.X, op=ALU.max))
                link(nc.vector.tensor_tensor(key[:, :, :], probs2[:, :, :], by_expert(top_p[:, k, :]), ALU.is_equal))
                link(nc.vector.tensor_tensor(key[:, :, :], key[:, :, :], by_token(rev[:, :]), ALU.mult))
                link(nc.vector.tensor_reduce(top[:, :], key[:, :, :], axis=AX.X, op=ALU.max))
                link(nc.vector.tensor_tensor(picked[:, k, :, :], by_token(rev[:, :]), by_expert(top[:, :]), ALU.is_equal))
                if k == 0:
                    link(nc.vector.scalar_tensor_tensor(probs2[:, :, :], picked[:, 0, :, :], -2.0, probs2[:, :, :],
                                                        ALU.mult, ALU.add))
            nc.vector.tensor_tensor(any_pick[:, :, :], picked[:, 0, :, :], picked[:, 1, :, :], ALU.add)\
                .then_inc(picks_ready, 1)
            link(nc.vector.tensor_tensor(denom[:, :], top_p[:, 0, :], top_p[:, 1, :], ALU.add))
            link(nc.vector.tensor_scalar(denom[:, :], denom[:, :], 1e-9, None, ALU.add))
            link(nc.vector.reciprocal(denom[:, :], denom[:, :]))
            link(nc.vector.tensor_tensor(weight[:, :, :], top_p[:, :, :],
                                         denom[:, :].unsqueeze(1).broadcast_to([QW, TOP, NTK]), ALU.mult))
            link(nc.vector.tensor_scalar(weight[:, :, :], weight[:, :, :], tanh_g2[0:QW, :], None, ALU.mult))

            dve.wait_ge(counted, 1)
            link(nc.vector.tensor_copy(run_t[0][:, PAD_T:, :], counts[:, :].rearrange("p (t e) -> p t e", e=E_R)))
            at, shift = 0, 1
            while shift < NTK:
                link(nc.vector.tensor_tensor(run_t[1 - at][:, PAD_T:, :], run_t[at][:, PAD_T:, :],
                                             run_t[at][:, PAD_T - shift:PAD_T + NTK - shift, :], ALU.add))
                at, shift = 1 - at, 2 * shift
            tiles_before = run_t[at][0:QW, PAD_T - 1:PAD_T + NTK - 1, :]
            count = run_t[at][:, PAD_T + NTK - 1, :]
            link(nc.vector.tensor_tensor(full[:, :, :], count.unsqueeze(2).broadcast_to([P, E_R, MAX_TILES]),
                                         fill[:, :].unsqueeze(1).broadcast_to([P, E_R, MAX_TILES]), ALU.is_gt))
            link(nc.vector.tensor_reduce(run_e[0][:, PAD_E:], full[:, :, :], axis=AX.X, op=ALU.add))
            at, shift = 0, 1
            while shift < E_R:
                link(nc.vector.tensor_tensor(run_e[1 - at][:, PAD_E:], run_e[at][:, PAD_E:],
                                             run_e[at][:, PAD_E - shift:PAD_E + E_R - shift], ALU.add))
                at, shift = 1 - at, 2 * shift
            ends = run_e[at][:, PAD_E:]
            starts = run_e[at][0:QW, PAD_E - 1:PAD_E + E_R - 1]

            dve.wait_ge(counted, 2)
            link(nc.vector.tensor_tensor(slot_e[:, :, :], earlier[0:QW, :].rearrange("p (t e) -> p t e", e=E_R),
                                         tiles_before, ALU.add))
            link(nc.vector.scalar_tensor_tensor(slot_e[:, :, :], by_token(starts), float(P), slot_e[:, :, :],
                                                ALU.mult, ALU.add))
            for k in range(TOP):
                link(nc.vector.tensor_tensor(key[:, :, :], picked[:, k, :, :], slot_e[:, :, :], ALU.mult))
                link(nc.vector.tensor_reduce(slot_f[:, k, :], key[:, :, :], axis=AX.X, op=ALU.add))
            link(nc.vector.tensor_copy(slot_i[:, :, :], slot_f[:, :, :]))
            nc.vector.tensor_scalar(part_i[:, 0, :, :], slot_i[:, :, :], P - 1, None, ALU.bitwise_and)
            link(nc.vector.tensor_scalar(part_i[:, 1, :, :], slot_i[:, :, :], P.bit_length() - 1, None,
                                         ALU.logical_shift_right))
            link(nc.vector.tensor_copy(part_f[:, :, :, :], part_i[:, :, :, :]))

            for n in range(CHUNKS):
                ring = n % 2
                k, t = divmod(n * CHUNK, NTK)
                if n >= 2:
                    dve.wait_ge(hot_used, n - 1)

                def against(ap, width):
                    return ap.unsqueeze(2).broadcast_to([QW, CHUNK, width])

                nc.vector.tensor_tensor(row_hot[:, ring, :, :], slot_iota[:, :].unsqueeze(1).broadcast_to([QW, CHUNK, P]),
                                        against(part_f[:, 0, k, t:t + CHUNK], P), ALU.is_equal).then_inc(hot_ready, 1)
                link(nc.vector.tensor_tensor(tile_hot[:, ring, :, :],
                                             tile_iota[0:QW, :].unsqueeze(1).broadcast_to([QW, CHUNK, SLOT_TILES]),
                                             against(part_f[:, 1, k, t:t + CHUNK], SLOT_TILES), ALU.is_equal))
                nc.vector.tensor_tensor(tile_hot[:, ring, :, :], tile_hot[:, ring, :, :],
                                        against(token_id[:, k, t:t + CHUNK], SLOT_TILES), ALU.mult).then_inc(hot_ready, 1)

            link(nc.vector.tensor_tensor(passed[:, :, :], ends.unsqueeze(1).broadcast_to([P, SLOT_TILES, E_R]),
                                         tile_iota[:, :].unsqueeze(2).broadcast_to([P, SLOT_TILES, E_R]), ALU.is_le))
            link(nc.vector.tensor_reduce(expert_f[:, :], passed[:, :, :], axis=AX.X, op=ALU.add))
            link(nc.vector.tensor_scalar(expert_f[:, :], expert_f[:, :], float(E_R - 1), None, ALU.min))
            nc.vector.memset(prev_expert[:, 0:1], 0)
            nc.vector.tensor_copy(prev_expert[:, 1:], expert_f[:, 0:SLOT_TILES - 1])
            link(nc.vector.tensor_copy(tile_expert[:, :], expert_f[:, :]))
            dve.wait_ge(hot_used, CHUNKS)
            link(nc.vector.tensor_copy(slot_token[:, :], table[:, 0:SLOT_TILES]))

        @block.tensor
        def _(pe):
            pe.wait_ge(consts3, CONSTS)
            pe.wait_ge(picks_ready, 1)
            flat = any_pick[:, :, :].rearrange("p t e -> p (t e)")
            nc.tensor.matmul(counts[:, :], ones[:, :], flat, start=True, stop=True).then_inc(counted, 1)
            nc.tensor.matmul(earlier[:, :], before[:, :], flat, start=True, stop=True).then_inc(counted, 1)
            for n in range(CHUNKS):
                pe.wait_ge(hot_ready, 2 * n + 2)
                for a in range(CHUNK):
                    ins = nc.tensor.matmul(table[:, 0:SLOT_TILES], row_hot[:, n % 2, a, :], tile_hot[:, n % 2, a, :],
                                           start=(n == 0 and a == 0), stop=(n == CHUNKS - 1 and a == CHUNK - 1))
                ins.then_inc(hot_used, 1)


def routed_experts(nc, xn_rows, y_slots, gu_sb, d_sb, ident2, slot_token, tile_expert, prev_expert, routed_in):
    es = ExitStack()
    with es:
        def sb(name, shape, dt=F32):
            return es.enter_context(nc.sbuf_tensor(name, shape, dt))

        def ps(name):
            return es.enter_context(nc.psum_tensor(name, [P, 512], F32))

        def sem(name):
            return es.enter_context(nc.semaphore(name))

        STEPS = SLOT_TILES // ASTEP
        gather_at = sb("gather_at", [P, ASTEP], I32)
        xg = sb("xg", [P, ASTEP, D])
        xg_t = sb("xg_t", [P, 2, DC, P])
        silu_g = sb("silu_g", [P, 2, MID])
        hid2 = sb("hid2", [P, 2, MID])
        hid_t2 = sb("hid_t2", [P, 2, P])
        y_sb = sb("y_sb", [P, ASTEP, D])
        spare = sb("spare", [P, 8])
        gu_ps = [ps(f"gu_ps{i}") for i in range(2)]
        turn_x = [ps(f"turn_x{i}") for i in range(2)]
        turn_h = ps("turn_h")
        y_bank = [ps(f"y_bank{i}") for i in range(2)]

        spare_set = sem("spare_set")
        index_ready = sem("index_ready")
        gathered = [sem(f"gathered{k}") for k in range(ASTEP)]
        x_turned = sem("x_turned")
        xg_t_ready = sem("xg_t_ready")
        gu_done = sem("gu_done")
        silu2_done = sem("silu2_done")
        hid2_done = sem("hid2_done")
        h_turned = sem("h_turned")
        hid_t_ready = sem("hid_t_ready")
        y_done2 = sem("y_done2")
        y_copied = sem("y_copied")
        y_stored = [sem(f"y_stored{k}") for k in range(ASTEP)]

        block = es.enter_context(nc.Block())

        def loop(engine, step):
            step(0, True, False)
            with engine.Fori(1, STEPS - 1) as i:
                step(i, False, False)
            step(STEPS - 1, False, True)

        @block.gpsimd
        def _(pool):
            pool.memset(spare[:, :], 0.0).then_inc(spare_set, 1)
            pool.wait_ge(spare_set, 1)

            def take_waits(n):
                nc.gpsimd.tensor_tensor(spare[:, n:n + 1], spare[:, 7:8], spare[:, 7:8], ALU.add).then_inc(spare_set, 1)

            def step(i, first, last):
                if not first:
                    for k in range(ASTEP):
                        pool.wait_ge(gathered[k], 16 * i)
                    pool.wait_ge(spare_set, 1 + (i - 1) * (ASTEP + 2))
                    take_waits(ASTEP)
                nc.gpsimd.tensor_copy(gather_at[:, :], slot_token[:, bass.ds(i * ASTEP, ASTEP)]).then_inc(index_ready, 1)
                pool.wait_ge(index_ready, i + 1)
                if not first:
                    take_waits(ASTEP + 1)
                for k in range(ASTEP):
                    if not first:
                        pool.wait_ge(x_turned, (i - 1) * ASTEP + k + 1)
                        take_waits(k)
                    nc.gpsimd.indirect_dma_start(xg[:, k, :], None, xn_rows,
                                                 bass.IndirectOffsetOnAxis(ap=gather_at[:, k:k + 1], axis=0))\
                        .then_inc(gathered[k], 16)

            step(0, True, False)
            with pool.Fori(1, STEPS) as i:
                step(i, False, False)

        @block.sync
        def _(sp):
            with sp.Fori(0, STEPS) as i:
                for k in range(ASTEP):
                    sp.wait_ge(y_copied, i * ASTEP + k + 1)
                    sp.dma_start(y_slots[bass.ds((i * ASTEP + k) * P, P), :], y_sb[:, k, :]).then_inc(y_stored[k], 16)
            for k in range(ASTEP):
                sp.wait_ge(y_stored[k], 16 * STEPS)

        @block.scalar
        def _(act):
            def copy_y(q, k, i, first):
                act.wait_ge(y_done2, q + 1)
                if not first:
                    act.wait_ge(y_stored[k], 16 * i)
                act.activation(y_sb[:, k, :], y_bank[k % 2][:, :], ACT.Copy).then_inc(y_copied, 1)

            def step(i, first, last):
                for k in range(ASTEP):
                    q = i * ASTEP + k
                    act.wait_ge(gu_done, q + 1)
                    if not (first and k < 2):
                        act.wait_ge(hid2_done, q - 1)
                    act.activation(silu_g[:, k % 2, :], gu_ps[k % 2][:, 0:MID], ACT.Silu).then_inc(silu2_done, 1)
                    if k:
                        copy_y(q - 1, k - 1, i, first)
                    elif not first:
                        copy_y(q - 1, ASTEP - 1, i - 1, isinstance(i, int) and i == 1)
                if last:
                    copy_y(SLOT_TILES - 1, ASTEP - 1, i, False)

            step(0, True, False)
            step(1, False, False)
            with act.Fori(2, STEPS - 1) as i:
                step(i, False, False)
            step(STEPS - 1, False, True)

        @block.vector
        def _(dve):
            def copy_x(q, k, early):
                dve.wait_ge(x_turned, q + 1)
                if not early:
                    dve.wait_ge(gu_done, q - 1)
                nc.vector.tensor_copy(xg_t[:, k % 2, :, :].rearrange("p c q -> p (c q)"), turn_x[k % 2][:, :])\
                    .then_inc(xg_t_ready, 1)

            def copy_h(q, k, early):
                dve.wait_ge(h_turned, q + 1)
                if not early:
                    dve.wait_ge(y_done2, q - 1)
                nc.vector.tensor_copy(hid_t2[:, k % 2, :], turn_h[:, 0:P]).then_inc(hid_t_ready, 1)

            def step(i, first, last):
                for k in range(ASTEP):
                    q = i * ASTEP + k
                    if not (first and k == 0):
                        copy_h(q - 1, (k - 1) % 2, first and k < 3)
                    if not (last and k == ASTEP - 1):
                        copy_x(q + 1, k + 1, first and k < 1)
                    dve.wait_ge(silu2_done, q + 1)
                    if not (first and k < 2):
                        dve.wait_ge(h_turned, q - 1)
                    nc.vector.tensor_tensor(hid2[:, k % 2, :], silu_g[:, k % 2, :], gu_ps[k % 2][:, MID:GATE_UP], ALU.mult)\
                        .then_inc(hid2_done, 1)

            copy_x(0, 0, True)
            loop(dve, step)
            copy_h(SLOT_TILES - 1, ASTEP - 1, False)

        @block.tensor
        def _(pe):
            def turn(q, k, i, early):
                pe.wait_ge(gathered[k], 16 * i + 16)
                if not early:
                    pe.wait_ge(xg_t_ready, q - 1)
                for c in range(DC):
                    ins = nc.tensor.transpose(turn_x[k % 2][:, c * P:(c + 1) * P], xg[:, k, c * P:(c + 1) * P], ident2[:, :])
                ins.then_inc(x_turned, 1)

            def turn_hidden(q, k, early):
                pe.wait_ge(hid2_done, q + 1)
                if not early:
                    pe.wait_ge(hid_t_ready, q)
                nc.tensor.transpose(turn_h[:, 0:P], hid2[:, k % 2, :], ident2[:, :]).then_inc(h_turned, 1)

            def gate_up(q, k, expert, chunks):
                for c in chunks:
                    ins = nc.tensor.matmul(gu_ps[k % 2][:, 0:GATE_UP], xg_t[:, k % 2, c, :],
                                           gu_sb[:, bass.ds(expert, 1), c, :].rearrange("p a m -> p (a m)"),
                                           start=(c == 0), stop=(c == DC - 1))
                if c == DC - 1:
                    ins.then_inc(gu_done, 1)

            def down(q, k, expert, early):
                pe.wait_ge(hid_t_ready, q + 1)
                if not early:
                    pe.wait_ge(y_copied, q - 1)
                nc.tensor.matmul(y_bank[k % 2][:, :], hid_t2[:, k % 2, :],
                                 d_sb[:, bass.ds(expert, 1), :].rearrange("p a n -> p (a n)"),
                                 start=True, stop=True).then_inc(y_done2, 1)

            def expert_of(table, q):
                return pe.value_load(table[0:1, bass.ds(q, 1)], min_val=0, max_val=E_R - 1)

            def step(i, first, last):
                experts = [expert_of(prev_expert, i * ASTEP)] + [expert_of(tile_expert, i * ASTEP + k) for k in range(ASTEP)]
                for k in range(ASTEP):
                    q = i * ASTEP + k
                    pe.wait_ge(xg_t_ready, q + 1)
                    if not (first and k < 2):
                        pe.wait_ge(hid2_done, q - 1)
                    gate_up(q, k, experts[k + 1], (0, 1))
                    if not (first and k == 0):
                        turn_hidden(q - 1, (k - 1) % ASTEP, first and k == 1)
                    gate_up(q, k, experts[k + 1], (2, 3))
                    if k < ASTEP - 1:
                        turn(q + 1, k + 1, i, first and k == 0)
                    elif not last:
                        turn(q + 1, 0, i + 1, False)
                    if not (first and k == 0):
                        down(q - 1, (k - 1) % ASTEP, experts[k], first and k < 3)
                if last:
                    turn_hidden(SLOT_TILES - 1, ASTEP - 1, False)
                    down(SLOT_TILES - 1, ASTEP - 1, experts[ASTEP], False)

            pe.wait_ge(routed_in, 32)
            turn(0, 0, 0, True)
            loop(pe, step)


def shared_and_combine(nc, x1, xn_cols, y_slots, shared, tanh_g2, weight, slot_i, out):
    es = ExitStack()
    with es:
        def sb(name, shape, dt=F32):
            return es.enter_context(nc.sbuf_tensor(name, shape, dt))

        def ps(name):
            return es.enter_context(nc.psum_tensor(name, [P, 512], F32))

        def sem(name):
            return es.enter_context(nc.semaphore(name))

        SC = MID_S // P
        xc = sb("xc", [P, DC, GTOK])
        xc_hi = sb("xc_hi", [P, DC, GTOK], F32R)
        xc_lo = sb("xc_lo", [P, DC, GTOK], F32R)
        silu_s = sb("silu_s", [P, 2, GTOK])
        hid_s = sb("hid_s", [P, 2, GTOK])
        hid_hi = sb("hid_hi", [P, SC, GTOK], F32R)
        hid_lo = sb("hid_lo", [P, SC, GTOK], F32R)
        total = sb("total", [QW, GT, D])
        routed = sb("routed", [QW, GT, TOP, D])
        gather_at2 = sb("gather_at2", [QW, TOP, GT], I32)
        spare2 = sb("spare2", [P, 8])
        free2 = sb("free2", [P, 4])
        gate_bank = [ps(f"gate_bank{i}") for i in range(2)]
        up_bank = [ps(f"up_bank{i}") for i in range(2)]
        down_bank = [ps(f"down_bank{t}") for t in range(GT)]

        xc_in = sem("xc_in")
        xc_ready = sem("xc_ready")
        chain4 = sem("chain4")
        gate_done2 = sem("gate_done2")
        up_done2 = sem("up_done2")
        silu_done3 = sem("silu_done3")
        hid_done3 = sem("hid_done3")
        parts_ready = sem("parts_ready")
        down_done = sem("down_done")
        total_in = sem("total_in")
        spare_set2 = sem("spare_set2")
        index_ready2 = sem("index_ready2")
        routed_got = [sem(f"routed_got{t}") for t in range(GT)]
        bank_read = sem("bank_read")
        combined = sem("combined")
        out_stored = sem("out_stored")
        PRE4 = {"hid_done3": 2, "down_done": 1, "bank_read": GT, "combined": 1}

        block = es.enter_context(nc.Block())

        def loop(engine, step):
            with engine.Fori(0, GROUPS - 1) as g:
                step(g, False)
            step(GROUPS - 1, True)

        @block.sync
        def _(sp):
            def load_cols(g):
                sp.dma_start(xc[:, :, :], xn_cols[bass.ds(g, 1), :, :, :].rearrange("a p c q -> p (a c) q")).then_inc(xc_in, 16)

            def load_total(g):
                sp.dma_start(total[:, :, :], x1[bass.ds(g * GTOK, GTOK), :].rearrange("(t p) d -> p t d", p=QW))\
                    .then_inc(total_in, 16)

            load_cols(0)
            load_total(0)

            def step(g, last):
                if not last:
                    sp.wait_ge(xc_ready, g + 1)
                    load_cols(g + 1)
                for t in range(GT):
                    sp.wait_ge(combined, PRE4["combined"] + GT * g + t + 1)
                    sp.dma_start(out[bass.ds(g * GTOK + t * QW, QW), :], total[:, t, :]).then_inc(out_stored, 16)
                if not last:
                    sp.wait_ge(out_stored, 16 * (GT * g + GT))
                    load_total(g + 1)

            loop(sp, step)
            sp.wait_ge(out_stored, 16 * GT * GROUPS)

        @block.gpsimd
        def _(pool):
            pool.memset(spare2[:, :], 0.0).then_inc(spare_set2, 1)
            pool.wait_ge(spare_set2, 1)

            def take_waits(n):
                nc.gpsimd.tensor_tensor(spare2[:, n:n + 1], spare2[:, 7:8], spare2[:, 7:8], ALU.add).then_inc(spare_set2, 1)

            def step(g, first):
                if not first:
                    for t in range(GT):
                        pool.wait_ge(routed_got[t], 32 * g)
                    pool.wait_ge(spare_set2, 1 + (g - 1) * (GT + 2))
                    take_waits(GT)
                nc.gpsimd.tensor_copy(gather_at2[:, :, :], slot_i[:, :, bass.ds(g * GT, GT)]).then_inc(index_ready2, 1)
                pool.wait_ge(index_ready2, g + 1)
                if not first:
                    take_waits(GT + 1)
                for t in range(GT):
                    if not first:
                        pool.wait_ge(combined, PRE4["combined"] + GT * (g - 1) + t + 1)
                        take_waits(t)
                    for k in range(TOP):
                        nc.gpsimd.indirect_dma_start(routed[:, t, k, :], None, y_slots,
                                                     bass.IndirectOffsetOnAxis(ap=gather_at2[:, k, t:t + 1], axis=0))\
                            .then_inc(routed_got[t], 16)

            step(0, True)
            with pool.Fori(1, GROUPS) as g:
                step(g, False)

        @block.scalar
        def _(act):
            def step(g, last):
                for j in range(SC):
                    act.wait_ge(gate_done2, SC * g + j + 1)
                    act.wait_ge(hid_done3, PRE4["hid_done3"] + SC * g + j - 1)
                    act.activation(silu_s[:, j % 2, :], gate_bank[j % 2][:, 0:GTOK], ACT.Silu).then_inc(silu_done3, 1)

            loop(act, step)

        @block.vector
        def _(dve):
            links = [0]

            def link(ins, base):
                links[0] += 1
                ins.then_inc(chain4, 1)
                dve.wait_ge(chain4, base + links[0])

            for n, (s, name) in enumerate(((hid_done3, "hid_done3"), (down_done, "down_done"), (bank_read, "bank_read"),
                                           (combined, "combined"))):
                nc.vector.memset(free2[:, n:n + 1], 0.0).then_inc(s, PRE4[name])

            def split_cols(n, base):
                dve.wait_ge(xc_in, 16 * n + 16)
                link(nc.vector.tensor_copy(xc_hi[:, :, :], xc[:, :, :]), base)
                nc.vector.tensor_tensor(xc_lo[:, :, :], xc[:, :, :], xc_hi[:, :, :].bitcast(F32), ALU.subtract)\
                    .then_inc(xc_ready, 1)

            split_cols(0, 0)
            FIRST, LINKS = links[0], SC + 1 + 2 * GT

            def step(g, last):
                base = FIRST + g * LINKS
                links[0] = 0
                for j in range(SC):
                    dve.wait_ge(silu_done3, SC * g + j + 1)
                    dve.wait_ge(up_done2, SC * g + j + 1)
                    nc.vector.tensor_tensor(hid_s[:, j % 2, :], silu_s[:, j % 2, :], up_bank[j % 2][:, 0:GTOK], ALU.mult)\
                        .then_inc(hid_done3, 1)
                    dve.wait_ge(hid_done3, PRE4["hid_done3"] + SC * g + j + 1)
                    dve.wait_ge(down_done, PRE4["down_done"] + GT * g)
                    link(nc.vector.tensor_copy(hid_hi[:, j, :], hid_s[:, j % 2, :]), base)
                    nc.vector.tensor_tensor(hid_lo[:, j, :], hid_s[:, j % 2, :], hid_hi[:, j, :].bitcast(F32), ALU.subtract)\
                        .then_inc(parts_ready, 1)
                if not last:
                    split_cols(g + 1, base)
                for t in range(GT):
                    if t == 0:
                        dve.wait_ge(total_in, 16 * g + 16)
                    dve.wait_ge(down_done, PRE4["down_done"] + GT * g + t + 1)
                    nc.vector.scalar_tensor_tensor(total[:, t, :], down_bank[t][0:QW, :], tanh_g2[0:QW, :], total[:, t, :],
                                                   ALU.mult, ALU.add).then_inc(bank_read, 1)
                    dve.wait_ge(bank_read, PRE4["bank_read"] + GT * g + t + 1)
                    dve.wait_ge(routed_got[t], 32 * g + 32)
                    for k in range(TOP):
                        ins = nc.vector.scalar_tensor_tensor(total[:, t, :], routed[:, t, k, :],
                                                             weight[:, k, bass.ds(g * GT + t, 1)], total[:, t, :],
                                                             ALU.mult, ALU.add)
                        if k < TOP - 1:
                            link(ins, base)
                    ins.then_inc(combined, 1)
                return links[0]

            LINKS = SC + 1 + GT
            with dve.Fori(0, GROUPS - 1) as g:
                assert step(g, False) == LINKS
            step(GROUPS - 1, True)

        @block.tensor
        def _(pe):
            def step(g, last):
                pe.wait_ge(xc_ready, g + 1)
                for j in range(SC):
                    pe.wait_ge(hid_done3, PRE4["hid_done3"] + SC * g + j - 1)
                    for bank, done, at in ((gate_bank, gate_done2, j * P), (up_bank, up_done2, MID_S + j * P)):
                        for d in range(DC):
                            for n, (wp, xp) in enumerate(((shared["gu_hi"], xc_hi), (shared["gu_hi"], xc_lo),
                                                          (shared["gu_lo"], xc_hi))):
                                ins = nc.tensor.matmul(bank[j % 2][:, 0:GTOK], wp[:, d, at:at + P], xp[:, d, :],
                                                       start=(d == 0 and n == 0), stop=(d == DC - 1 and n == 2))
                        ins.then_inc(done, 1)
                for j in range(SC):
                    pe.wait_ge(parts_ready, SC * g + j + 1)
                    for t in range(GT):
                        if j == 0:
                            pe.wait_ge(bank_read, PRE4["bank_read"] + GT * (g - 1) + t + 1)
                        for n, (hp, wp) in enumerate(((hid_hi, "d_hi"), (hid_hi, "d_lo"), (hid_lo, "d_hi"))):
                            ins = nc.tensor.matmul(down_bank[t][0:QW, :], hp[:, j, t * QW:(t + 1) * QW], shared[wp][:, j, :],
                                                   start=(j == 0 and n == 0), stop=(j == SC - 1 and n == 2))
                        if j == SC - 1:
                            ins.then_inc(down_done, 1)

            loop(pe, step)


def kernel(**inputs):
    import numpy as np
    import concourse.bacc as bacc
    from concourse.bass_utils import run_bass_kernel_spmd as run

    a = {k: np.asarray(v) for k, v in inputs.items()}
    laid = {
        "x": a["x"],
        "ctx_t": a["ctx_1024"].transpose(0, 2, 1).reshape(B, DC, P, S).transpose(0, 2, 1, 3),
        "ctxb": a["ctxb_2048x32"],
        "g_xattn": a["g_xattn"],
        "wq": a["L0_xattn_Wq"], "bq": a["L0_xattn_bq"].reshape(DC, P).T,
        "wk": a["L0_xattn_Wk"], "bk": a["L0_xattn_bk"].reshape(DC, P).T,
        "wv": a["L0_xattn_Wv"], "bv": a["L0_xattn_bv"].reshape(DC, P).T,
        "wo": a["L0_xattn_Wo"], "bo": a["L0_xattn_bo"],
        "g_ffn": a["g_ffn"],
        "router_w": a["L0_ffn_router_w"],
        "w_gu": np.concatenate([a["L0_ffn_wg_r"], a["L0_ffn_wu_r"]], axis=2)
        .reshape(E_R, DC, P, 2 * MID).transpose(2, 0, 1, 3).reshape(P, -1),
        "w_d": a["L0_ffn_wd_r"],
        "ws_gu": np.stack([a["L0_ffn_wg_s"], a["L0_ffn_wu_s"]]).transpose(2, 0, 1, 3)
        .reshape(DC, P, 2 * MID_S).transpose(1, 0, 2),
        "ws_d": a["L0_ffn_wd_s"].reshape(MID_S, D),
    }
    nc = bacc.Bacc("TRN2", target_bir_lowering=False, num_devices=1)
    arrays, dram = {}, {}
    for name, value in laid.items():
        arrays[f"in_{name}"] = np.ascontiguousarray(value)
        dram[name] = nc.dram_tensor(f"in_{name}", value.shape, mybir.dt.from_np(value.dtype), kind="ExternalInput").ap()
    out = nc.dram_tensor("out", (T, D), F32, kind="ExternalOutput").ap()
    program(nc, out=out, **dram)
    result = run(nc, [arrays], core_ids=[0])
    return result.results[0]["out"].reshape(B, L, D)


def program(nc, x, ctx_t, ctxb, g_xattn, wq, bq, wk, bk, wv, bv, wo, bo,
            g_ffn, router_w, w_gu, w_d, ws_gu, ws_d, out):
    x1 = nc.dram_tensor("x1", (T, D), F32, kind="Internal").ap()
    attention_phase(nc, x, ctx_t, ctxb, g_xattn, wq, bq, wk, bk, wv, bv, wo, bo, x1)
    experts_phase(nc, x1, g_ffn, router_w, w_gu, w_d, ws_gu, ws_d, out)
```

```python
from contextlib import ExitStack

import concourse.bass as bass
from concourse import mybir

F32 = mybir.dt.float32
F32R = mybir.dt.float32r
BF16 = mybir.dt.bfloat16
I32 = mybir.dt.int32
U32 = mybir.dt.uint32
ACT = mybir.ActivationFunctionType
ALU = mybir.AluOpType
AX = mybir.AxisListType

P = 128
B, L, D = 16, 224, 512
S, NF = 750, 32
H, DH = 16, 32
DC = D // P
HC = H // DC
QT, QW = 2, L // 2
KT, KW = 6, S // 6
T = B * L
EPS = 1e-5
THRESHOLD = 0.1
GATE_LOW = 0.1
SCORE_SCALE = float(DH) ** -0.5
HALF_N = (512, S - 512)
HALF_K = (376, S - 376)

E_R = 16

XT0, XT1, Q0, Q1, K0 = 0, 1, 2, 3, 4
VALUES = (12, 13, 14, 15, 17, 19)
YT, LOGITS = (16, 18), 20
ITEMS = 21


def item(n, i):
    if isinstance(n, int) and n == 0:
        return i - sum(j < i for j in (*YT, LOGITS))
    return n * ITEMS + i - 3


SPLITS = 10
RESULT_HEADS = (2, 3)
LOGIT_HEAD = 4
ATTEND_HEADS = (5, 9, 13)
VALUE_HEADS = (0, 1, 2, 3, 4)
XT_HEAD = 5
SPLIT_HEADS = (6, 7, 8, 10, 11, 12, 13, 14, 15)


def attention_phase(nc, x, ctx_t, ctxb, g_xattn, wq, bq, wk, bk, wv, bv, wo, bo, router_w,
                    x1, xn_rows, xn_cols, logits):
    q_dram = nc.dram_tensor("q_parts", (B, DC, HC, 2, DH, L), F32, kind="Internal").ap()
    energy_dram = nc.dram_tensor("energy", (B, S), F32, kind="Internal").ap()
    gate_dram = nc.dram_tensor("gate", (B, S), F32, kind="Internal").ap()

    es = ExitStack()
    with es:
        def sb(name, shape, dt=F32):
            return es.enter_context(nc.sbuf_tensor(name, shape, dt))

        def ps(name, shape):
            return es.enter_context(nc.psum_tensor(name, shape, F32))

        def sem(name):
            return es.enter_context(nc.semaphore(name))

        wq_sb = sb("wq_sb", [P, DC, D])
        wo_sb = sb("wo_sb", [P, DC, D])
        wk_hi = sb("wk_hi", [P, DC, D], F32R)
        wk_lo = sb("wk_lo", [P, DC, D], F32R)
        wv_hi = sb("wv_hi", [P, DC, D], F32R)
        wv_lo = sb("wv_lo", [P, DC, D], F32R)
        ctx_raw = sb("ctx_raw", [P, 2, S])
        ctx_hi = sb("ctx_hi", [P, DC, S], F32R)
        ctx_lo = sb("ctx_lo", [P, DC, S], F32R)
        fresh = sb("fresh", [P, 2 * L])
        k_hi = sb("k_hi", [P, DC, S], F32R)
        k_lo = sb("k_lo", [P, DC, S], F32R)
        k_stack = sb("k_stack", [P, 2 * HC, S], F32R)
        q_hi = sb("q_hi", [P, DC, L], F32R)
        q_lo = sb("q_lo", [P, DC, L], F32R)
        q_stack = sb("q_stack", [P, 2 * HC, L], F32R)
        v_sb = sb("v_sb", [P, KT, D])
        probs = sb("probs", [P, 2, QT, S])
        probs_t = sb("probs_t", [P, HC, KT, L])
        x_in = sb("x_in", [QW, QT, D])
        x_res = sb("x_res", [QW, QT, D])
        xn_t = sb("xn_t", [P, DC, L])
        out_t = sb("out_t", [P, DC, L])
        rw_sb = sb("rw_sb", [P, DC, E_R])
        logit_sb = sb("logit_sb", [QW, QT, E_R])
        rec = sb("rec", [QW, QT, HC])
        rec_x = sb("rec_x", [QW, QT, HC * DH])
        gate_b = sb("gate_b", [P, S])
        bo_t = sb("bo_t", [P, D])
        ident = sb("ident", [P, P])
        neg_max = sb("neg_max", [QW, 2, QT])
        row_sum = sb("row_sum", [QW, QT, H])
        bq_col = sb("bq_col", [P, DC])
        bk_col = sb("bk_col", [P, DC])
        bv_col = sb("bv_col", [P, DC])
        g_col = sb("g_col", [P, 1])
        tanh_g = sb("tanh_g", [P, 1])
        stats = sb("stats", [QW, QT, 6])
        moments = sb("moments", [QW, QT, 2])
        var_eps = sb("var_eps", [QW, QT])
        rstd0 = sb("rstd0", [QW, QT])
        rstd = sb("rstd", [QW, QT])
        newton = sb("newton", [QW, QT])
        minus_half = sb("minus_half", [P, QT])
        zero = sb("zero", [P, 1])
        e_max = sb("e_max", [B, 1])
        e_rec = sb("e_rec", [B, 1])
        token = sb("token", [P, 16])

        score = [ps(f"score{t}", [P, 1024]) for t in range(QT)]
        flip = [ps(f"flip{i}", [P, 512]) for i in range(2)]
        proj = ps("proj", [P, 512])
        pv = ps("pv", [P, 512])

        wk_in = sem("wk_in")
        wv_in = sem("wv_in")
        wq_in = sem("wq_in")
        bias_in = sem("bias_in")
        tabs_in = sem("tabs_in")
        energy_summed = sem("energy_summed")
        ctxb_in = sem("ctxb_in")
        consts = sem("consts")
        w_hi = sem("w_hi")
        w_lo = sem("w_lo")
        energy_out = sem("energy_out")
        energy_in = sem("energy_in")
        gate_out = sem("gate_out")
        gate_ready = sem("gate_ready")
        tanh_ready = sem("tanh_ready")
        bvwo_done = sem("bvwo_done")
        bo_ready = sem("bo_ready")
        dve_chain = sem("dve_chain")
        raw_in = [sem(f"raw_in{r}") for r in range(2)]
        x_loaded = sem("x_loaded")
        gate_loaded = sem("gate_loaded")
        res_loaded = sem("res_loaded")
        x1_stored = sem("x1_stored")
        xn2_ready = sem("xn2_ready")
        rows_stored = sem("rows_stored")
        cols_stored = sem("cols_stored")
        logits_stored = sem("logits_stored")
        k_stacked = [sem(f"k_stacked{r}") for r in range(2)]
        q_stored = sem("q_stored")
        q_stacked = [sem(f"q_stacked{r}") for r in range(2)]
        ctx_hi_done = sem("ctx_hi_done")
        ctx_lo_done = sem("ctx_lo_done")
        var_ready = sem("var_ready")
        rstd0_ready = sem("rstd0_ready")
        xn_ready = sem("xn_ready")
        proj_done = sem("proj_done")
        proj_read = sem("proj_read")
        hi_done = sem("hi_done")
        lo_done = sem("lo_done")
        scored = [sem(f"scored{t}") for t in range(QT)]
        maxed = [sem(f"maxed{t}") for t in range(QT)]
        exped = [sem(f"exped{t}") for t in range(QT)]
        flipped = sem("flipped")
        copied_act = sem("copied_act")
        copied_dve = sem("copied_dve")
        rec_done = sem("rec_done")
        rec_x_done = sem("rec_x_done")
        pv_done = sem("pv_done")
        normed = sem("normed")
        out_done = sem("out_done")
        res_ready = sem("res_ready")
        res_done = sem("res_done")

        PRE = {"exped": 1, "flipped": 4, "pv_done": 1, "normed": 1, "rec_x_done": 1,
               "proj_read": 1, "lo_done": 1, "res_done": 2, "x1_stored": 16, "logits_stored": 16}
        K_SET, Q_SET = 16 * 4 * HC, 16 * 2

        def by_vector(h, p):
            return p == 1

        ACT_CHUNK, DVE_CHUNK = 2 * HC, HC

        def copied_before(h, p, vector):
            return sum(by_vector(i, j) == vector for i in range(h + 1) for j in range(3) if (i, j) <= (h, p))

        TABS = 16 * 5
        NORM_LINKS = 6
        BATCH_LINKS = 2 * NORM_LINKS + 2 * DC
        flat_t = probs_t[:, :, :, :].rearrange("p a b c -> p (a b c)")
        wv_tmp = probs[:, :, :, :].rearrange("p a b c -> p (a b c)")[:, 0:DC * D].rearrange("p (c n) -> p c n", c=DC)

        def load_raw(queue, n, d):
            queue.dma_start(ctx_raw[:, d % 2, :],
                            ctx_t[bass.ds(n, 1), :, d, :].rearrange("a p s -> p (a s)")).then_inc(raw_in[d % 2], 16)

        block = es.enter_context(nc.Block())

        @block.sync
        def _(sp):
            def in_register(value):
                return value if isinstance(value, int) else sp.snap(sp.to_reg(value))

            def at_batch(first, each, n):
                return in_register(first + each * n)

            def load_x(n):
                sp.dma_start(x_in[:, :, :],
                             x[bass.ds(n, 1), :, :].rearrange("a (t p) d -> p (a t) d", p=QW)).then_inc(x_loaded, 16)

            def load_gate(n):
                sp.dma_start(gate_b[:, :], gate_dram[bass.ds(n, 1), :].broadcast_to([P, S])).then_inc(gate_loaded, 16)

            def store_q(n):
                sp.wait_ge(lo_done, PRE["lo_done"] + n * SPLITS + 2)
                for c in range(DC):
                    for part, q_sb in enumerate((q_hi, q_lo)):
                        sp.dma_start(q_dram[bass.ds(n, 1), c, :, part, :, :].rearrange("a j p q -> (a j) p q"),
                                     q_sb[:, c, :].bitcast(F32)).then_inc(q_stored, 16)

            def store_rows(m):
                sp.wait_ge(xn2_ready, m * QT + QT)
                sp.dma_start(xn_rows[bass.ds(m * L, L), :].rearrange("(t p) d -> p t d", p=QW), x_res[:, :, :])\
                    .then_inc(rows_stored, 16)

            def store_logits(m, logits_read):
                sp.wait_ge(proj_read, logits_read)
                sp.dma_start(logits[:, bass.ds(m * QT, QT), :], logit_sb[:, :, :]).then_inc(logits_stored, 16)

            def stack(n, c, heads_done=None):
                ring = c % 2
                split = at_batch(PRE["lo_done"] + 4 + 2 * c, SPLITS, n)
                stored = at_batch(16 * 2 * DC, 16 * 2 * DC, n)
                if heads_done is not None:
                    for t in range(QT):
                        sp.wait_ge(scored[t], heads_done)
                sp.wait_ge(lo_done, split)
                sp.wait_ge(q_stored, stored)
                for j in range(HC):
                    for row in range(4):
                        k_sb = k_hi if row < 2 else k_lo
                        sp.dma_start(k_stack[row * DH:(row + 1) * DH, ring * HC + j, :].bitcast(F32),
                                     k_sb[j * DH:(j + 1) * DH, c, :].bitcast(F32)).then_inc(k_stacked[ring], 16)
                for rep in range(2):
                    sp.dma_start(q_stack[rep * 64:(rep + 1) * 64, ring * HC:(ring + 1) * HC, :].bitcast(F32),
                                 q_dram[bass.ds(n, 1), c, :, :, :, :].rearrange("a j w p q -> (a w p) j q"))\
                        .then_inc(q_stacked[ring], 16)

            load_x(0)
            sp.dma_start(flat_t[0:B * KT, 0:KW * NF],
                         ctxb.rearrange("b (c t) f -> (b c) (t f)", c=KT)).then_inc(ctxb_in, 16)
            sp.dma_start(v_sb[:, 0:DC, :], wk.rearrange("(c p) n -> p c n", p=P)).then_inc(wk_in, 16)
            load_raw(sp, 0, 0)
            load_raw(sp, 0, 1)
            sp.dma_start(wq_sb[:, :, :], wq.rearrange("(c p) n -> p c n", p=P)).then_inc(wq_in, 16)
            sp.wait_ge(energy_summed, 1)
            sp.dma_start(energy_dram.rearrange("b (c t) -> (b c) t", c=KT),
                         out_t[0:B * KT, 0, 0:KW]).then_inc(energy_out, 16)
            sp.dma_start(bq_col[:, :], bq).then_inc(bias_in, 16)
            sp.dma_start(bk_col[:, :], bk).then_inc(bias_in, 16)
            sp.dma_start(bv_col[:, :], bv).then_inc(tabs_in, 16)
            sp.dma_start(g_col[:, :], g_xattn.rearrange("(a n) -> a n", a=1).broadcast_to([P, 1])).then_inc(tabs_in, 16)
            for d in (2, 3):
                sp.wait_ge(ctx_lo_done, d - 1)
                load_raw(sp, 0, d)
            sp.dma_start(bo_t[:, :], bo.rearrange("(a n) -> a n", a=1).broadcast_to([P, D])).then_inc(tabs_in, 16)
            sp.dma_start(rw_sb[:, :, :], router_w.rearrange("(c p) e -> p c e", p=P)).then_inc(tabs_in, 16)
            sp.dma_start(wo_sb[:, :, :], wo.rearrange("(c p) n -> p c n", p=P)).then_inc(tabs_in, 16)
            sp.dma_start(wv_tmp, wv.rearrange("(c p) n -> p c n", p=P)).then_inc(wv_in, 16)
            store_q(0)
            stack(0, 0)
            stack(0, 1)

            def batch(b, first, last):
                n = b + 1
                if not last:
                    sp.wait_ge(proj_done, item(b, XT1) + 1)
                    load_x(n)
                    for d in (0, 1):
                        sp.wait_ge(ctx_lo_done, b * DC + d + 3)
                        load_raw(sp, n, d)
                    sp.wait_ge(proj_read, PRE["proj_read"] + item(b, VALUES[0]))
                    load_gate(n)
                if not first:
                    store_rows(b - 1)
                stack(b, 2, at_batch(HC, H, b))
                if not first:
                    left, turned = in_register(b * 16), in_register(item(b, YT[1]) + 1)
                    sp.wait_ge(rows_stored, left)
                    sp.wait_ge(proj_done, turned)
                sp.dma_start(x_res[:, :, :], x[bass.ds(b, 1), :, :].rearrange("a (t p) d -> p (a t) d", p=QW))\
                    .then_inc(res_loaded, 16)
                if not first:
                    store_logits(b - 1, PRE["proj_read"] + item(b, LOGITS) + 1)
                if not last:
                    for d in (2, 3):
                        sp.wait_ge(ctx_lo_done, n * DC + d - 1)
                        load_raw(sp, n, d)
                stack(b, 3, at_batch(2 * HC, H, b))
                if not last:
                    store_q(n)
                    for c in range(2):
                        stack(n, c, at_batch((c + 3) * HC, H, b))
                sp.wait_ge(res_done, PRE["res_done"] + b * QT + QT)
                sp.dma_start(x1[bass.ds(b * L, L), :].rearrange("(t p) d -> p t d", p=QW), x_res[:, :, :])\
                    .then_inc(x1_stored, 16)

            batch(0, True, False)
            with sp.Fori(1, B - 1) as b:
                batch(b, False, False)
            batch(B - 1, False, True)
            done = PRE["proj_read"] + item(B, 0)
            store_rows(B - 1)
            store_logits(B - 1, done + QT + 1)
            sp.wait_ge(x1_stored, PRE["x1_stored"] + B * 16)
            sp.wait_ge(rows_stored, B * 16)
            sp.wait_ge(cols_stored, B * 16)
            sp.wait_ge(logits_stored, PRE["logits_stored"] + B * 16)

        @block.gpsimd
        def _(pool):
            pool.memset(ident[:, :], 0.0).then_inc(consts, 1)
            pool.memset(minus_half[:, :], -0.5).then_inc(consts, 1)
            pool.memset(zero[:, :], 0.0).then_inc(consts, 1)
            pool.wait_ge(consts, 3)
            pool.affine_select(out=ident[:, :], in_=ident[:, :], compare_op=ALU.not_equal, fill=1.0,
                               base=0, pattern=[[-1, P]], channel_multiplier=1).then_inc(consts, 1)
            pool.wait_ge(consts, 4)

            def remainder(lo, full, hi):
                return nc.gpsimd.tensor_tensor(lo, full, hi.bitcast(F32), ALU.subtract)

            def norm_power(p):
                pool.wait_ge(var_ready, p + 1)
                nc.gpsimd.tensor_tensor(rstd0[:, :], var_eps[:, :], minus_half[0:QW, :], ALU.pow).then_inc(rstd0_ready, 1)

            def ctx_remainder(n, d):
                pool.wait_ge(ctx_hi_done, n * DC + d + 1)
                remainder(ctx_lo[:, d, :], ctx_raw[:, d % 2, :], ctx_hi[:, d, :]).then_inc(ctx_lo_done, 1)

            def split_remainder(n, i):
                pool.wait_ge(hi_done, n * SPLITS + i + 1)
                if i < 2:
                    remainder(q_lo[:, 2 * i:2 * i + 2, :].rearrange("p c q -> p (c q)"), fresh[:, :],
                              q_hi[:, 2 * i:2 * i + 2, :].rearrange("p c q -> p (c q)")).then_inc(lo_done, 1)
                else:
                    c, half = divmod(i - 2, 2)
                    at, w = half * HALF_K[0], HALF_K[half]
                    remainder(k_lo[:, c, at:at + w], fresh[:, 0:w], k_hi[:, c, at:at + w]).then_inc(lo_done, 1)

            def spread_reciprocals(b, c):
                pool.wait_ge(rec_done, b * DC + c + 1)
                pool.wait_ge(pv_done, PRE["pv_done"] + b * DC + c)
                nc.gpsimd.tensor_tensor(rec_x[:, :, :].rearrange("p t (h w) -> p (t h) w", w=DH),
                                        rec[:, :, :].rearrange("p t h -> p (t h)").unsqueeze(2).broadcast_to([QW, QT * HC, DH]),
                                        zero[0:QW, :].unsqueeze(2).broadcast_to([QW, QT * HC, DH]), ALU.add)\
                    .then_inc(rec_x_done, 1)

            norm_power(0)
            pool.wait_ge(w_hi, 1)
            remainder(wk_lo[:, :, :], v_sb[:, 0:DC, :], wk_hi[:, :, :]).then_inc(w_lo, 1)
            ctx_remainder(0, 0)
            ctx_remainder(0, 1)
            split_remainder(0, 0)
            ctx_remainder(0, 2)
            ctx_remainder(0, 3)
            split_remainder(0, 1)
            for i in range(2, SPLITS):
                split_remainder(0, i)
                c = i - 3
                if c == 0:
                    pool.wait_ge(w_hi, 2)
                if 0 <= c < DC:
                    remainder(wv_lo[:, c, :], wv_tmp[:, c, :], wv_hi[:, c, :]).then_inc(w_lo, 1)

            def batch(b, first, last):
                n = b + 1
                if not first:
                    norm_power(2 * b)
                if not last:
                    norm_power(2 * b + 1)
                spread_reciprocals(b, 0)
                if not last:
                    for d in range(DC):
                        ctx_remainder(n, d)
                    split_remainder(n, 0)
                    split_remainder(n, 1)
                spread_reciprocals(b, 1)
                if not last:
                    for i in range(2, 5):
                        split_remainder(n, i)
                spread_reciprocals(b, 2)
                pool.wait_ge(res_loaded, b * 16 + 16)
                pool.wait_ge(bo_ready, 1)
                nc.gpsimd.tensor_tensor(x_res[:, :, :], x_res[:, :, :],
                                        bo_t[0:QW, :].unsqueeze(1).broadcast_to([QW, QT, D]), ALU.add).then_inc(res_ready, 1)
                if not last:
                    for i in range(5, SPLITS - 1):
                        split_remainder(n, i)
                spread_reciprocals(b, 3)
                if not last:
                    split_remainder(n, SPLITS - 1)

            batch(0, True, False)
            with pool.Fori(1, B - 1) as b:
                batch(b, False, False)
            batch(B - 1, False, True)
            norm_power(2 * B - 1)

        @block.scalar
        def _(act):
            act.wait_ge(energy_out, 16)
            act.dma_start(gate_b[0:B, :], energy_dram).then_inc(energy_in, 16)
            act.wait_ge(gate_ready, 1)
            act.dma_start(gate_dram, gate_b[0:B, :]).then_inc(gate_out, 16)
            act.wait_ge(gate_out, 16)
            act.dma_start(gate_b[:, :], gate_dram[0:1, :].broadcast_to([P, S])).then_inc(gate_loaded, 16)

            def store_cols(m, k):
                act.wait_ge(proj_read, PRE["proj_read"] + k + 1)
                act.dma_start(xn_cols[bass.ds(m, 1), :, :, :].rearrange("a p c q -> p (a c) q"), out_t[:, :, :])\
                    .then_inc(cols_stored, 16)

            def exponentials(b, h):
                for t in range(QT):
                    act.wait_ge(maxed[t], b * H + h + 1)
                    act.wait_ge(flipped, PRE["flipped"] + b * 3 * H + 3 * (h - 1))
                    act.activation(probs[0:QW, h % 2, t, :], score[t][0:QW, 0:S], ACT.Exp,
                                   bias=neg_max[:, h % 2, t:t + 1], accum_out=row_sum[:, t, h:h + 1]).then_inc(exped[t], 1)

            def copy_flipped(b, h, pieces=range(3)):
                for p in pieces:
                    if not by_vector(h, p):
                        act.wait_ge(flipped, PRE["flipped"] + b * 3 * H + 3 * h + p + 1)
                        act.activation(probs_t[0:KW, h % HC, 2 * p:2 * p + 2, :].rearrange("k a q -> k (a q)"),
                                       flip[(3 * h + p) % 2][0:KW, 0:2 * L], ACT.Relu).then_inc(copied_act, 1)

            def copy_values(n, kt):
                act.wait_ge(proj_done, item(n, VALUES[kt]) + 1)
                act.activation(v_sb[0:KW, kt, :], proj[0:KW, :], ACT.Copy).then_inc(proj_read, 1)

            def split_high(n, i, first):
                act.wait_ge(proj_read, PRE["proj_read"] + item(n, Q0 + i) + 1)
                if i < 2:
                    if not first:
                        act.wait_ge(q_stored, n * 16 * 2 * DC)
                    act.activation(q_hi[:, 2 * i:2 * i + 2, :].rearrange("p c q -> p (c q)"), fresh[:, :], ACT.Copy)\
                        .then_inc(hi_done, 1)
                else:
                    c, half = divmod(i - 2, 2)
                    at, w = half * HALF_K[0], HALF_K[half]
                    if not first:
                        act.wait_ge(k_stacked[c % 2], K_SET * (2 * n + c // 2 - 1))
                    act.activation(k_hi[:, c, at:at + w], fresh[:, 0:w], ACT.Copy).then_inc(hi_done, 1)

            for i in range(SPLITS):
                split_high(0, i, True)
                if i == 4:
                    act.wait_ge(tabs_in, TABS)
                    act.activation(tanh_g[:, :], g_col[:, :], ACT.Tanh).then_inc(tanh_ready, 1)
            copy_values(0, 0)
            exponentials(0, 0)

            def batch(b, first, last):
                n = b + 1
                for h in range(H):
                    if h in ATTEND_HEADS:
                        exponentials(b, h)
                        copy_flipped(b, h - 1)
                    elif h:
                        copy_flipped(b, h - 1, (0, 1))
                        exponentials(b, h)
                    if h in VALUE_HEADS:
                        copy_values(b, h + 1)
                    if h and h not in ATTEND_HEADS:
                        copy_flipped(b, h - 1, (2,))
                    if h == LOGIT_HEAD and not first:
                        store_cols(b - 1, item(b, YT[1]))
                    if not last and h in SPLIT_HEADS:
                        split_high(n, SPLIT_HEADS.index(h), False)
                copy_flipped(b, H - 1)
                if not last:
                    split_high(n, SPLITS - 1, False)
                    exponentials(n, 0)
                    copy_values(n, 0)

            batch(0, True, False)
            with act.Fori(1, B - 1) as b:
                batch(b, False, False)
            batch(B - 1, False, True)
            store_cols(B - 1, item(B, 0) + QT - 1)

        @block.vector
        def _(dve):
            links = [0]

            def link(ins, base=0):
                links[0] += 1
                ins.then_inc(dve_chain, 1)
                dve.wait_ge(dve_chain, base + links[0])

            free = {"exped": exped, "flipped": [flipped], "pv_done": [pv_done], "normed": [normed],
                    "rec_x_done": [rec_x_done], "proj_read": [proj_read], "lo_done": [lo_done],
                    "res_done": [res_done], "x1_stored": [x1_stored], "logits_stored": [logits_stored]}
            given = [(s, PRE[name]) for name, sems in free.items() for s in sems]
            for i, (s, count) in enumerate(given):
                nc.vector.memset(token[:, i:i + 1], 0.0).then_inc(s, count)

            def norm_statistics(rows, p, base):
                nc.vector.bn_stats(stats[:, 0, :], rows[:, 0, :])
                link(nc.vector.bn_stats(stats[:, 1, :], rows[:, 1, :]), base)
                nc.vector.memset(token[:, 15:16], 0.0)
                nc.vector.bn_aggr(moments[:, 0, :], stats[:, 0, :])
                link(nc.vector.bn_aggr(moments[:, 1, :], stats[:, 1, :]), base)
                nc.vector.tensor_scalar(var_eps[:, :], moments[:, :, 1], EPS, None, ALU.add).then_inc(var_ready, 1)

            def norm_factor(p, base):
                dve.wait_ge(rstd0_ready, p + 1)
                link(nc.vector.tensor_tensor(newton[:, :], rstd0[:, :], rstd0[:, :], ALU.mult), base)
                link(nc.vector.tensor_tensor(newton[:, :], newton[:, :], var_eps[:, :], ALU.mult), base)
                link(nc.vector.tensor_scalar(newton[:, :], newton[:, :], -0.5, 1.5, ALU.mult, ALU.add), base)
                link(nc.vector.tensor_tensor(rstd[:, :], rstd0[:, :], newton[:, :], ALU.mult), base)

            def normalize(rows, done):
                for t in range(QT):
                    nc.vector.tensor_scalar(rows[:, t, :], rows[:, t, :], moments[:, t, 0:1], rstd[:, t:t + 1],
                                            ALU.subtract, ALU.mult).then_inc(done, 1)

            def input_statistics(n, p, base):
                dve.wait_ge(x_loaded, n * 16 + 16)
                norm_statistics(x_in, p, base)

            def normalize_input(p, base):
                norm_factor(p, base)
                normalize(x_in, xn_ready)

            def result_statistics(m, p, base):
                dve.wait_ge(res_done, PRE["res_done"] + m * QT + QT)
                norm_statistics(x_res, p, base)

            def normalize_result(m, p, base):
                norm_factor(p, base)
                dve.wait_ge(x1_stored, PRE["x1_stored"] + m * 16 + 16)
                normalize(x_res, xn2_ready)

            def copy_result(k, t):
                dve.wait_ge(proj_done, k + 1)
                nc.vector.tensor_copy(out_t[:, :, t * QW:(t + 1) * QW],
                                      proj[:, 0:DC * QW].rearrange("p (c q) -> p c q", c=DC)).then_inc(proj_read, 1)

            def copy_logits(k, m):
                dve.wait_ge(proj_done, k + 1)
                dve.wait_ge(logits_stored, PRE["logits_stored"] + m * 16)
                nc.vector.tensor_copy(logit_sb[:, :, :].rearrange("p t e -> p (t e)"), proj[0:QW, 0:QT * E_R])\
                    .then_inc(proj_read, 1)

            def ctx_high(n, d, first):
                ring = d % 2
                dve.wait_ge(raw_in[ring], 16 * (2 * n + d // 2 + 1))
                if not first:
                    dve.wait_ge(proj_done, item(n, 0))
                nc.vector.tensor_copy(ctx_hi[:, d, :], ctx_raw[:, ring, :]).then_inc(ctx_hi_done, 1)

            def copy_xt(n, t):
                dve.wait_ge(proj_done, item(n, XT0 + t) + 1)
                nc.vector.tensor_copy(xn_t[:, :, t * QW:(t + 1) * QW],
                                      proj[:, 0:DC * QW].rearrange("p (c q) -> p c q", c=DC)).then_inc(proj_read, 1)

            def read_split(n, i):
                dve.wait_ge(proj_done, item(n, Q0 + i) + 1)
                dve.wait_ge(lo_done, PRE["lo_done"] + n * SPLITS + i)
                if i < 2:
                    for k in range(2):
                        c = 2 * i + k
                        ins = nc.vector.tensor_scalar(fresh[:, k * L:(k + 1) * L], proj[:, k * L:(k + 1) * L],
                                                      bq_col[:, c:c + 1], None, ALU.add)
                    ins.then_inc(proj_read, 1)
                else:
                    c, half = divmod(i - 2, 2)
                    at, w = half * HALF_K[0], HALF_K[half]
                    if i == 2:
                        dve.wait_ge(gate_loaded, n * 16 + 16)
                    nc.vector.scalar_tensor_tensor(fresh[:, 0:w], proj[:, 0:w], bk_col[:, c:c + 1],
                                                   gate_b[:, at:at + w], ALU.add, ALU.mult).then_inc(proj_read, 1)

            def maxima(b, h):
                for t in range(QT):
                    dve.wait_ge(scored[t], b * H + h + 1)
                    nc.vector.tensor_reduce(neg_max[:, h % 2, t:t + 1], score[t][0:QW, 0:S], axis=AX.X, op=ALU.max,
                                            negate=True).then_inc(maxed[t], 1)

            def copy_flipped(b, h):
                for p in range(3):
                    if by_vector(h, p):
                        dve.wait_ge(flipped, PRE["flipped"] + b * 3 * H + 3 * h + p + 1)
                        nc.vector.tensor_scalar(probs_t[0:KW, h % HC, 2 * p:2 * p + 2, :].rearrange("k a q -> k (a q)"),
                                                flip[(3 * h + p) % 2][0:KW, 0:2 * L], 0.0, None, ALU.max)\
                            .then_inc(copied_dve, 1)

            def reciprocals(b, c, base):
                for t in range(QT):
                    dve.wait_ge(exped[t], PRE["exped"] + b * H + (c + 1) * HC)
                dve.wait_ge(rec_x_done, PRE["rec_x_done"] + b * DC + c)
                link(nc.vector.reciprocal(rec[:, :, :], row_sum[:, :, c * HC:(c + 1) * HC]), base)
                nc.vector.tensor_scalar(rec[:, :, :], rec[:, :, :], 0.0, None, ALU.max).then_inc(rec_done, 1)

            def normalize_output(b, c, first, base):
                dve.wait_ge(pv_done, PRE["pv_done"] + b * DC + c + 1)
                if c == 0 and not first:
                    dve.wait_ge(cols_stored, b * 16)
                link(nc.vector.tensor_copy(out_t[:, c, :], pv[:, 0:L]), base)
                nc.vector.tensor_tensor(out_t[:, c, :], out_t[:, c, :], pv[:, L:2 * L], ALU.mult).then_inc(normed, 1)

            input_statistics(0, 0, 0)
            dve.wait_ge(ctxb_in, 16)
            nc.vector.tensor_reduce(out_t[0:B * KT, 0, 0:KW],
                                    flat_t[0:B * KT, 0:KW * NF].rearrange("p (t f) -> p t f", f=NF),
                                    axis=AX.X, op=ALU.add, apply_absolute_value=True).then_inc(energy_summed, 1)
            normalize_input(0, 0)
            dve.wait_ge(wk_in, 16)
            nc.vector.tensor_copy(wk_hi[:, :, :], v_sb[:, 0:DC, :]).then_inc(w_hi, 1)
            ctx_high(0, 0, True)
            ctx_high(0, 1, True)
            for t in range(QT):
                copy_xt(0, t)
            dve.wait_ge(energy_in, 16)
            link(nc.vector.tensor_reduce(e_max[:, :], gate_b[0:B, :], axis=AX.X, op=ALU.max))
            link(nc.vector.tensor_scalar(e_max[:, :], e_max[:, :], 1.0 / NF, 1e-8, ALU.mult, ALU.add))
            link(nc.vector.reciprocal(e_rec[:, :], e_max[:, :]))
            link(nc.vector.tensor_scalar(gate_b[0:B, :], gate_b[0:B, :], 1.0 / NF, e_rec[:, :], ALU.mult, ALU.mult))
            link(nc.vector.tensor_scalar(gate_b[0:B, :], gate_b[0:B, :], THRESHOLD, 1.0 - GATE_LOW, ALU.is_gt, ALU.mult))
            nc.vector.tensor_scalar(gate_b[0:B, :], gate_b[0:B, :], GATE_LOW, SCORE_SCALE, ALU.add, ALU.mult)\
                .then_inc(gate_ready, 1)
            dve.wait_ge(bias_in, 32)
            read_split(0, 0)
            ctx_high(0, 2, True)
            ctx_high(0, 3, True)
            read_split(0, 1)
            for i in range(2, SPLITS):
                read_split(0, i)
                if i == 3:
                    dve.wait_ge(wv_in, 16)
                    nc.vector.tensor_copy(wv_hi[:, :, :], wv_tmp).then_inc(w_hi, 1)
                if i == 6:
                    dve.wait_ge(tabs_in, TABS)
                    dve.wait_ge(bvwo_done, 1)
                    dve.wait_ge(tanh_ready, 1)
                    link(nc.vector.tensor_tensor(bo_t[:, :], pv[:, :], bo_t[:, :], ALU.add))
                    nc.vector.tensor_scalar(bo_t[:, :], bo_t[:, :], tanh_g[:, :], None, ALU.mult).then_inc(bo_ready, 1)
            maxima(0, 0)
            setup_links = links[0]

            def batch(b, first, last):
                n = b + 1
                base = setup_links if first else setup_links + b * BATCH_LINKS - NORM_LINKS
                links[0] = 0
                for h in range(H):
                    if h and h % HC == 0:
                        reciprocals(b, h // HC - 1, base)
                    if h:
                        maxima(b, h)
                    if h == XT_HEAD and not last:
                        ctx_high(n, 0, False)
                        ctx_high(n, 1, False)
                    if h in ATTEND_HEADS:
                        normalize_output(b, ATTEND_HEADS.index(h), first, base)
                    if h == XT_HEAD and not last:
                        copy_xt(n, 0)
                    if h:
                        copy_flipped(b, h - 1)
                    if h == 0 and not first:
                        result_statistics(b - 1, 2 * b, base)
                    if h == 1 and not first:
                        normalize_result(b - 1, 2 * b, base)
                    if not last:
                        if h == 2:
                            input_statistics(n, 2 * b + 1, base)
                        if h == 3:
                            normalize_input(2 * b + 1, base)
                        if h == XT_HEAD:
                            copy_xt(n, 1)
                        if h == XT_HEAD + 1:
                            ctx_high(n, 2, False)
                            ctx_high(n, 3, False)
                        if h in SPLIT_HEADS:
                            read_split(n, SPLIT_HEADS.index(h))
                    if h in RESULT_HEADS and not first:
                        t = RESULT_HEADS.index(h)
                        copy_result(item(b, YT[t]), t)
                    if h == LOGIT_HEAD and not first:
                        copy_logits(item(b, LOGITS), b - 1)
                reciprocals(b, DC - 1, base)
                copy_flipped(b, H - 1)
                if not last:
                    read_split(n, SPLITS - 1)
                normalize_output(b, DC - 1, first, base)
                if not last:
                    maxima(n, 0)
                dve.wait_ge(res_ready, b + 1)
                for t in range(QT):
                    dve.wait_ge(out_done, b * QT + t + 1)
                    nc.vector.scalar_tensor_tensor(x_res[:, t, :], flip[t][0:QW, :], tanh_g[0:QW, :], x_res[:, t, :],
                                                   ALU.mult, ALU.add).then_inc(res_done, 1)
                return links[0]

            batch(0, True, False)
            with dve.Fori(1, B - 1) as b:
                assert batch(b, False, False) == BATCH_LINKS
            batch(B - 1, False, True)
            base = setup_links + B * BATCH_LINKS - 2 * NORM_LINKS
            links[0] = 0
            result_statistics(B - 1, 2 * B - 1, base)
            normalize_result(B - 1, 2 * B - 1, base)
            for t in range(QT):
                copy_result(item(B, 0) + t, t)
            copy_logits(item(B, 0) + QT, B - 1)

        @block.tensor
        def _(pe):
            pe.wait_ge(consts, 4)

            def take_proj(k):
                pe.wait_ge(proj_read, PRE["proj_read"] + k)

            def transpose_x(n, t):
                take_proj(item(n, XT0 + t))
                pe.wait_ge(xn_ready, n * QT + t + 1)
                for c in range(DC):
                    ins = nc.tensor.transpose(proj[:, c * QW:(c + 1) * QW], x_in[:, t, c * P:(c + 1) * P],
                                              ident[0:QW, 0:QW])
                ins.then_inc(proj_done, 1)

            def transpose_result(k, m, t):
                take_proj(k)
                pe.wait_ge(xn2_ready, m * QT + t + 1)
                for c in range(DC):
                    ins = nc.tensor.transpose(proj[:, c * QW:(c + 1) * QW], x_res[:, t, c * P:(c + 1) * P],
                                              ident[0:QW, 0:QW])
                ins.then_inc(proj_done, 1)

            def route(k):
                take_proj(k)
                for t in range(QT):
                    for c in range(DC):
                        ins = nc.tensor.matmul(proj[0:QW, t * E_R:(t + 1) * E_R], out_t[:, c, t * QW:(t + 1) * QW],
                                               rw_sb[:, c, :], start=(c == 0), stop=(c == DC - 1))
                ins.then_inc(proj_done, 1)

            def project_q(n, i):
                take_proj(item(n, Q0 + i))
                for k in range(2):
                    c = 2 * i + k
                    for d in range(DC):
                        ins = nc.tensor.matmul(proj[:, k * L:(k + 1) * L], wq_sb[:, d, c * P:(c + 1) * P], xn_t[:, d, :],
                                               start=(d == 0), stop=(d == DC - 1))
                ins.then_inc(proj_done, 1)

            def project_k(n, i):
                c, half = divmod(i, 2)
                at, w = half * HALF_K[0], HALF_K[half]
                take_proj(item(n, K0 + i))
                if i == 0:
                    pe.wait_ge(ctx_lo_done, n * DC + DC)
                for d in range(DC):
                    for k, (wp, xp) in enumerate(((wk_hi, ctx_hi), (wk_hi, ctx_lo), (wk_lo, ctx_hi))):
                        ins = nc.tensor.matmul(proj[:, 0:w], wp[:, d, c * P:(c + 1) * P], xp[:, d, at:at + w],
                                               start=(d == 0 and k == 0), stop=(d == DC - 1 and k == 2))
                ins.then_inc(proj_done, 1)

            def split_item(n, i):
                if i < 2:
                    project_q(n, i)
                else:
                    project_k(n, i - 2)

            def project_v(n, kt):
                take_proj(item(n, VALUES[kt]))
                for d in range(DC):
                    for k, (xp, wp) in enumerate(((ctx_hi, wv_hi), (ctx_hi, wv_lo), (ctx_lo, wv_hi))):
                        ins = nc.tensor.matmul(proj[0:KW, :], xp[:, d, kt * KW:(kt + 1) * KW], wp[:, d, :],
                                               start=(d == 0 and k == 0), stop=(d == DC - 1 and k == 2))
                ins.then_inc(proj_done, 1)

            def scores(b, h):
                c = h // HC
                if h % HC == 0:
                    pe.wait_ge(k_stacked[c % 2], K_SET * (2 * b + c // 2 + 1))
                    pe.wait_ge(q_stacked[c % 2], Q_SET * (2 * b + c // 2 + 1))
                slot = h % (2 * HC)
                for t in range(QT):
                    pe.wait_ge(exped[t], PRE["exped"] + b * H + h)
                    at = 0
                    for w in HALF_N:
                        ins = nc.tensor.matmul(score[t][0:QW, at:at + w], q_stack[:, slot, t * QW:(t + 1) * QW],
                                               k_stack[:, slot, at:at + w], start=True, stop=True)
                        at += w
                    ins.then_inc(scored[t], 1)

            def wait_copied(b, h, p):
                vector = by_vector(h, p)
                done, each = (copied_dve, DVE_CHUNK) if vector else (copied_act, ACT_CHUNK)
                pe.wait_ge(done, b * DC * each + copied_before(h, p, vector))

            def flip_probs(b, h, pieces):
                if pieces[0] == 0:
                    for t in range(QT):
                        pe.wait_ge(exped[t], PRE["exped"] + b * H + h + 1)
                for p in pieces:
                    g = 3 * h + p
                    if g < 2:
                        pe.wait_ge(res_done, PRE["res_done"] + (b - 1) * QT + g + 1)
                    else:
                        wait_copied(b, (g - 2) // 3, (g - 2) % 3)
                    for k in range(2):
                        for t in range(QT):
                            kt = 2 * p + k
                            ins = nc.tensor.transpose(flip[g % 2][0:KW, k * L + t * QW:k * L + (t + 1) * QW],
                                                      probs[0:QW, h % 2, t, kt * KW:(kt + 1) * KW], ident[0:QW, 0:QW])
                    ins.then_inc(flipped, 1)

            def attend(b, c):
                pe.wait_ge(normed, PRE["normed"] + b * DC + c)
                pe.wait_ge(rec_x_done, PRE["rec_x_done"] + b * DC + c + 1)
                for t in range(QT):
                    nc.tensor.matmul(pv[:, L + t * QW:L + (t + 1) * QW], rec_x[:, t, :], ident[0:QW, 0:QW],
                                     start=True, stop=True)
                if c == 0:
                    pe.wait_ge(proj_read, PRE["proj_read"] + item(b, ITEMS))
                h = c * HC + HC - 1
                pe.wait_ge(copied_act, b * DC * ACT_CHUNK + copied_before(h, 2, False))
                pe.wait_ge(copied_dve, b * DC * DVE_CHUNK + copied_before(h, 2, True))
                for kt in range(KT):
                    for j in range(HC):
                        at = (c * HC + j) * DH
                        ins = nc.tensor.matmul(pv[j * DH:(j + 1) * DH, 0:L], v_sb[0:KW, kt, at:at + DH],
                                               probs_t[0:KW, j, kt, :], start=(kt == 0), stop=(kt == KT - 1))
                ins.then_inc(pv_done, 1)

            def project_out(b, t):
                pe.wait_ge(normed, PRE["normed"] + b * DC + DC)
                for c in range(DC):
                    ins = nc.tensor.matmul(flip[t][0:QW, :], out_t[:, c, t * QW:(t + 1) * QW], wo_sb[:, c, :],
                                           start=(c == 0), stop=(c == DC - 1))
                ins.then_inc(out_done, 1)

            for t in range(QT):
                transpose_x(0, t)
            pe.wait_ge(wq_in, 16)
            for i in range(2):
                project_q(0, i)
            pe.wait_ge(w_lo, 1)
            for i in range(2 * DC):
                project_k(0, i)
                if i == 0:
                    pe.wait_ge(tabs_in, TABS)
                if i < DC:
                    ins = nc.tensor.matmul(pv[:, :], bv_col[:, i:i + 1].broadcast_to([P, P]), wo_sb[:, i, :],
                                           start=(i == 0), stop=(i == DC - 1))
                    if i == DC - 1:
                        ins.then_inc(bvwo_done, 1)
            pe.wait_ge(w_lo, 1 + DC)
            project_v(0, 0)
            scores(0, 0)

            def batch(b, first, last):
                n = b + 1
                for h in range(H):
                    if h:
                        scores(b, h)
                        if h in ATTEND_HEADS:
                            attend(b, ATTEND_HEADS.index(h))
                        if h == XT_HEAD and not last:
                            transpose_x(n, 0)
                        flip_probs(b, h - 1, (0, 1))
                    if h in VALUE_HEADS:
                        project_v(b, h + 1)
                    elif not last:
                        if h == XT_HEAD:
                            transpose_x(n, 1)
                        elif h in SPLIT_HEADS:
                            split_item(n, SPLIT_HEADS.index(h))
                    if h:
                        flip_probs(b, h - 1, (2,))
                    if h in RESULT_HEADS and not first:
                        t = RESULT_HEADS.index(h)
                        transpose_result(item(b, YT[t]), b - 1, t)
                    if h == LOGIT_HEAD and not first:
                        route(item(b, LOGITS))
                flip_probs(b, H - 1, (0,))
                if not last:
                    split_item(n, SPLITS - 1)
                flip_probs(b, H - 1, (1, 2))
                attend(b, DC - 1)
                if not last:
                    scores(n, 0)
                    project_v(n, 0)
                for t in range(QT):
                    project_out(b, t)

            batch(0, True, False)
            with pe.Fori(1, B - 1) as b:
                batch(b, False, False)
            batch(B - 1, False, True)
            for t in range(QT):
                transpose_result(item(B, 0) + t, B - 1, t)
            route(item(B, 0) + QT)


TOP, MID = 2, 128
MID_S = 512
GATE_UP = 2 * MID
NTK = B * QT
GT = 4
GROUPS, GTOK = NTK // GT, GT * QW
BATCHES = GT // QT
SLOT_TILES = TOP * T // P + E_R
ASTEP = 4
MAX_TILES = T // P


def experts_phase(nc, x1, xn_rows, xn_cols, logits, g_ffn, w_gu, w_d, ws_gu, ws_d, out):
    y_slots = nc.dram_tensor("y_slots", (SLOT_TILES * P, D), F32, kind="Internal").ap()

    outer = ExitStack()
    with outer:
        def sb(name, shape, dt=F32):
            return outer.enter_context(nc.sbuf_tensor(name, shape, dt))

        shared = {
            "gu_hi": sb("sgu_hi", [P, DC, 2 * MID_S], F32R), "gu_lo": sb("sgu_lo", [P, DC, 2 * MID_S], F32R),
            "d_hi": sb("sd_hi", [P, DC, D], F32R), "d_lo": sb("sd_lo", [P, DC, D], F32R),
        }
        tanh_g2 = sb("tanh_g2", [P, 1])
        weight = sb("weight", [QW, TOP, NTK])
        slot_i = sb("slot_i", [QW, TOP, NTK], I32)
        inner = ExitStack()
        with inner:
            def sbi(name, shape, dt=F32):
                return inner.enter_context(nc.sbuf_tensor(name, shape, dt))

            gu_sb = sbi("gu_sb", [P, E_R, DC, GATE_UP])
            d_sb = sbi("d_sb", [P, E_R, D])
            ident2 = sbi("ident2", [P, P])
            slot_token = sbi("slot_token", [P, SLOT_TILES], I32)
            tile_expert = sbi("tile_expert", [P, SLOT_TILES], I32)
            prev_expert = sbi("prev_expert", [P, SLOT_TILES], I32)
            routed_in = inner.enter_context(nc.semaphore("routed_in"))
            assign_slots(nc, logits, g_ffn, w_gu, w_d, ws_gu, ws_d, shared, gu_sb, d_sb, ident2, routed_in,
                         tanh_g2, weight, slot_i, slot_token, tile_expert, prev_expert)
            routed_experts(nc, xn_rows, y_slots, gu_sb, d_sb, ident2, slot_token, tile_expert, prev_expert, routed_in)
        shared_and_combine(nc, x1, xn_cols, y_slots, shared, tanh_g2, weight, slot_i, out)


def assign_slots(nc, logits, g_ffn, w_gu, w_d, ws_gu, ws_d, shared, gu_sb, d_sb, ident2, routed_in,
                 tanh_g2, weight, slot_i, slot_token, tile_expert, prev_expert):
    es = ExitStack()
    with es:
        def sb(name, shape, dt=F32):
            return es.enter_context(nc.sbuf_tensor(name, shape, dt))

        def sem(name):
            return es.enter_context(nc.semaphore(name))

        PAD_T, PAD_E = NTK // 2, E_R // 2
        CHUNK = 8
        CHUNKS = TOP * NTK // CHUNK
        g_col2 = sb("g_col2", [P, 1])
        logit = sb("logit", [QW, NTK, E_R])
        sgu_raw = sb("sgu_raw", [P, DC, 2 * MID_S])
        sd_raw = sb("sd_raw", [P, DC, D])
        before = sb("before", [QW, P])
        ones = sb("ones", [QW, P])
        rev = sb("rev", [QW, E_R])
        slot_iota = sb("slot_iota", [QW, P])
        tile_iota = sb("tile_iota", [P, SLOT_TILES])
        fill = sb("fill", [P, MAX_TILES])
        slot_iota_h = sb("slot_iota_h", [QW, P], BF16)
        tile_iota_h = sb("tile_iota_h", [QW, SLOT_TILES], BF16)
        token_tile = sb("token_tile", [QW, NTK])
        token_row = sb("token_row", [QW, 1])
        token_tile_h = sb("token_tile_h", [QW, NTK], BF16)
        probs2 = sb("probs2", [QW, NTK, E_R])
        key = sb("key", [QW, NTK, E_R])
        picked = sb("picked", [QW, TOP, NTK, E_R])
        any_pick = sb("any_pick", [QW, NTK, E_R])
        slot_e = sb("slot_e", [QW, NTK, E_R])
        top = sb("top", [QW, NTK])
        denom = sb("denom", [QW, NTK])
        top_p = sb("top_p", [QW, TOP, NTK])
        run_t = [sb(f"run_t{i}", [P, PAD_T + NTK, E_R]) for i in range(2)]
        run_e = [sb(f"run_e{i}", [P, PAD_E + E_R]) for i in range(2)]
        expert_f = sb("expert_f", [P, SLOT_TILES])
        slot_f = sb("slot_f", [QW, TOP, NTK])
        part_i = sb("part_i", [QW, 2, TOP, NTK], I32)
        part_h = sb("part_h", [QW, 2, TOP, NTK], BF16)
        row_hot = sb("row_hot", [QW, 2, CHUNK, P], BF16)
        in_tile = sb("in_tile", [QW, 2, CHUNK, SLOT_TILES], BF16)
        tile_hot = sb("tile_hot", [P, 2, CHUNK, 2, SLOT_TILES], BF16)
        table_low = sb("table_low", [P, SLOT_TILES])
        counts = es.enter_context(nc.psum_tensor("counts", [P, NTK * E_R], F32))
        earlier = es.enter_context(nc.psum_tensor("earlier", [P, NTK * E_R], F32))
        table = es.enter_context(nc.psum_tensor("table", [P, 512], F32))

        logits_in = sem("logits_in")
        gate_in = sem("gate_in")
        tanh2 = sem("tanh2")
        shared_in = sem("shared_in")
        shared_hi = sem("shared_hi")
        split_done = sem("split_done")
        consts3 = sem("consts3")
        chain3 = sem("chain3")
        shifted = sem("shifted")
        exped2 = sem("exped2")
        picks_ready = sem("picks_ready")
        counted = sem("counted")
        tokens_ready = sem("tokens_ready")
        in_tile_ready = sem("in_tile_ready")
        row_ready = sem("row_ready")
        by_tile_ready = sem("by_tile_ready")
        by_row_ready = sem("by_row_ready")
        hot_used = sem("hot_used")
        CONSTS = 15

        def chunk_of(ap, n):
            k, t = divmod(n * CHUNK, NTK)
            return ap[:, k, t:t + CHUNK]

        def against(ap, width):
            return ap.unsqueeze(2).broadcast_to([QW, CHUNK, width])

        block = es.enter_context(nc.Block())

        @block.sync
        def _(sp):
            sp.dma_start(logit[:, :, :], logits).then_inc(logits_in, 16)
            sp.dma_start(g_col2[:, :], g_ffn.rearrange("(a n) -> a n", a=1).broadcast_to([P, 1])).then_inc(gate_in, 16)
            sp.dma_start(sgu_raw[:, :, :], ws_gu).then_inc(shared_in, 16)
            sp.dma_start(sd_raw[:, :, :], ws_d.rearrange("(c p) n -> p c n", p=P)).then_inc(shared_in, 16)
            sp.dma_start(gu_sb[:, :, :, :].rearrange("p e c m -> p (e c m)"), w_gu).then_inc(routed_in, 16)
            sp.dma_start(d_sb[:, :, :], w_d.rearrange("e m n -> m e n")).then_inc(routed_in, 16)

        @block.gpsimd
        def _(pool):
            def iota(dst, pattern, base=0, step=0):
                pool.iota(dst, pattern=pattern, base=base, channel_multiplier=step,
                          allow_small_or_imprecise_dtypes=True).then_inc(consts3, 1)

            pool.memset(ones[:, :], 1.0).then_inc(consts3, 1)
            pool.memset(before[:, :], 1.0).then_inc(consts3, 1)
            iota(rev[:, :], [[-1, E_R]], base=E_R)
            iota(slot_iota[:, :], [[1, P]])
            iota(tile_iota[:, :], [[1, SLOT_TILES]])
            iota(fill[:, :], [[P, MAX_TILES]])
            iota(token_tile[:, :], [[1, NTK]])
            iota(token_row[:, :], [[0, 1]], step=1)
            for i in range(2):
                pool.memset(run_t[i][:, 0:PAD_T, :], 0.0).then_inc(consts3, 1)
            for i in range(2):
                pool.memset(run_e[i][:, 0:PAD_E], 0.0).then_inc(consts3, 1)
            pool.memset(ident2[:, :], 0.0).then_inc(consts3, 1)
            pool.wait_ge(consts3, CONSTS - 2)
            pool.affine_select(out=before[:, :], in_=before[:, :], compare_op=ALU.is_gt, fill=0.0,
                               base=0, pattern=[[1, P]], channel_multiplier=-1).then_inc(consts3, 1)
            pool.affine_select(out=ident2[:, :], in_=ident2[:, :], compare_op=ALU.not_equal, fill=1.0,
                               base=0, pattern=[[-1, P]], channel_multiplier=1).then_inc(consts3, 1)
            for n, (lo, raw, hi) in enumerate(((shared["gu_lo"], sgu_raw, shared["gu_hi"]),
                                               (shared["d_lo"], sd_raw, shared["d_hi"]))):
                pool.wait_ge(shared_hi, n + 1)
                nc.gpsimd.tensor_tensor(lo[:, :, :], raw[:, :, :], hi[:, :, :].bitcast(F32), ALU.subtract)\
                    .then_inc(split_done, 1)
            pool.wait_ge(split_done, 2)
            pool.wait_ge(tokens_ready, 1)
            for n in range(CHUNKS):
                pool.wait_ge(in_tile_ready, n + 1)
                nc.gpsimd.tensor_tensor(tile_hot[0:QW, n % 2, :, 0, :], in_tile[:, n % 2, :, :],
                                        against(chunk_of(token_tile_h[:, :].unsqueeze(1).broadcast_to([QW, TOP, NTK]), n),
                                                SLOT_TILES), ALU.mult).then_inc(by_tile_ready, 1)

        @block.scalar
        def _(act):
            act.wait_ge(gate_in, 16)
            act.activation(tanh_g2[:, :], g_col2[:, :], ACT.Tanh).then_inc(tanh2, 1)
            act.wait_ge(shifted, 1)
            act.activation(probs2[:, :, :], probs2[:, :, :], ACT.Exp).then_inc(exped2, 1)
            act.wait_ge(shared_in, 32)
            act.activation(shared["gu_hi"][:, :, :], sgu_raw[:, :, :], ACT.Copy).then_inc(shared_hi, 1)
            act.activation(shared["d_hi"][:, :, :], sd_raw[:, :, :], ACT.Copy).then_inc(shared_hi, 1)
            act.wait_ge(consts3, CONSTS)
            for n in range(CHUNKS):
                act.wait_ge(in_tile_ready, n + 1)
                act.activation(tile_hot[0:QW, n % 2, :, 1, :], in_tile[:, n % 2, :, :], ACT.Copy, scale=token_row[:, :])\
                    .then_inc(by_row_ready, 1)

        @block.vector
        def _(dve):
            links = [0]

            def link(ins):
                links[0] += 1
                ins.then_inc(chain3, 1)
                dve.wait_ge(chain3, links[0])

            def by_expert(ap):
                return ap.unsqueeze(2).broadcast_to([QW, NTK, E_R])

            def by_token(ap):
                return ap.unsqueeze(1).broadcast_to([QW, NTK, E_R])

            dve.wait_ge(logits_in, 16)
            link(nc.vector.tensor_reduce(top[:, :], logit[:, :, :], axis=AX.X, op=ALU.max))
            nc.vector.tensor_tensor(probs2[:, :, :], logit[:, :, :], by_expert(top[:, :]), ALU.subtract).then_inc(shifted, 1)
            dve.wait_ge(exped2, 1)
            link(nc.vector.tensor_reduce(top[:, :], probs2[:, :, :], axis=AX.X, op=ALU.add))
            link(nc.vector.reciprocal(denom[:, :], top[:, :]))
            link(nc.vector.tensor_tensor(probs2[:, :, :], probs2[:, :, :], by_expert(denom[:, :]), ALU.mult))
            dve.wait_ge(consts3, CONSTS)
            nc.vector.tensor_copy(slot_iota_h[:, :], slot_iota[:, :])
            nc.vector.tensor_copy(tile_iota_h[:, :], tile_iota[0:QW, :])
            nc.vector.tensor_copy(token_tile_h[:, :], token_tile[:, :]).then_inc(tokens_ready, 1)
            for k in range(TOP):
                link(nc.vector.tensor_reduce(top_p[:, k, :], probs2[:, :, :], axis=AX.X, op=ALU.max))
                link(nc.vector.tensor_tensor(key[:, :, :], probs2[:, :, :], by_expert(top_p[:, k, :]), ALU.is_equal))
                link(nc.vector.tensor_tensor(key[:, :, :], key[:, :, :], by_token(rev[:, :]), ALU.mult))
                link(nc.vector.tensor_reduce(top[:, :], key[:, :, :], axis=AX.X, op=ALU.max))
                link(nc.vector.tensor_tensor(picked[:, k, :, :], by_token(rev[:, :]), by_expert(top[:, :]), ALU.is_equal))
                if k == 0:
                    link(nc.vector.scalar_tensor_tensor(probs2[:, :, :], picked[:, 0, :, :], -2.0, probs2[:, :, :],
                                                        ALU.mult, ALU.add))
            nc.vector.tensor_tensor(any_pick[:, :, :], picked[:, 0, :, :], picked[:, 1, :, :], ALU.add)\
                .then_inc(picks_ready, 1)
            link(nc.vector.tensor_tensor(denom[:, :], top_p[:, 0, :], top_p[:, 1, :], ALU.add))
            link(nc.vector.tensor_scalar(denom[:, :], denom[:, :], 1e-9, None, ALU.add))
            link(nc.vector.reciprocal(denom[:, :], denom[:, :]))
            link(nc.vector.tensor_tensor(weight[:, :, :], top_p[:, :, :],
                                         denom[:, :].unsqueeze(1).broadcast_to([QW, TOP, NTK]), ALU.mult))
            dve.wait_ge(tanh2, 1)
            link(nc.vector.tensor_scalar(weight[:, :, :], weight[:, :, :], tanh_g2[0:QW, :], None, ALU.mult))

            dve.wait_ge(counted, 1)
            link(nc.vector.tensor_copy(run_t[0][:, PAD_T:, :], counts[:, :].rearrange("p (t e) -> p t e", e=E_R)))
            at, shift = 0, 1
            while shift < NTK:
                link(nc.vector.tensor_tensor(run_t[1 - at][:, PAD_T:, :], run_t[at][:, PAD_T:, :],
                                             run_t[at][:, PAD_T - shift:PAD_T + NTK - shift, :], ALU.add))
                at, shift = 1 - at, 2 * shift
            tiles_before = run_t[at][0:QW, PAD_T - 1:PAD_T + NTK - 1, :]
            count = run_t[at][:, PAD_T + NTK - 1, :]
            unused = tile_hot[:, :, :, :, :].rearrange("p r a k q -> p (r a k q)").bitcast(F32)
            full = unused[:, 0:E_R * MAX_TILES].rearrange("p (e q) -> p e q", e=E_R)
            link(nc.vector.tensor_tensor(full, count.unsqueeze(2).broadcast_to([P, E_R, MAX_TILES]),
                                         fill[:, :].unsqueeze(1).broadcast_to([P, E_R, MAX_TILES]), ALU.is_gt))
            link(nc.vector.tensor_reduce(run_e[0][:, PAD_E:], full, axis=AX.X, op=ALU.add))
            at, shift = 0, 1
            while shift < E_R:
                link(nc.vector.tensor_tensor(run_e[1 - at][:, PAD_E:], run_e[at][:, PAD_E:],
                                             run_e[at][:, PAD_E - shift:PAD_E + E_R - shift], ALU.add))
                at, shift = 1 - at, 2 * shift
            ends = run_e[at][:, PAD_E:]
            starts = run_e[at][0:QW, PAD_E - 1:PAD_E + E_R - 1]

            dve.wait_ge(counted, 2)
            link(nc.vector.tensor_tensor(slot_e[:, :, :], earlier[0:QW, :].rearrange("p (t e) -> p t e", e=E_R),
                                         tiles_before, ALU.add))
            link(nc.vector.scalar_tensor_tensor(slot_e[:, :, :], by_token(starts), float(P), slot_e[:, :, :],
                                                ALU.mult, ALU.add))
            for k in range(TOP):
                link(nc.vector.tensor_tensor(key[:, :, :], picked[:, k, :, :], slot_e[:, :, :], ALU.mult))
                link(nc.vector.tensor_reduce(slot_f[:, k, :], key[:, :, :], axis=AX.X, op=ALU.add))
            link(nc.vector.tensor_copy(slot_i[:, :, :], slot_f[:, :, :]))
            nc.vector.tensor_scalar(part_i[:, 0, :, :], slot_i[:, :, :], P - 1, None, ALU.bitwise_and)
            link(nc.vector.tensor_scalar(part_i[:, 1, :, :], slot_i[:, :, :], P.bit_length() - 1, None,
                                         ALU.logical_shift_right))
            link(nc.vector.tensor_copy(part_h[:, :, :, :], part_i[:, :, :, :]))

            passed = unused[:, 0:SLOT_TILES * E_R].rearrange("p (q e) -> p q e", e=E_R)
            link(nc.vector.tensor_tensor(passed, ends.unsqueeze(1).broadcast_to([P, SLOT_TILES, E_R]),
                                         tile_iota[:, :].unsqueeze(2).broadcast_to([P, SLOT_TILES, E_R]), ALU.is_le))
            link(nc.vector.tensor_reduce(expert_f[:, :], passed, axis=AX.X, op=ALU.add))
            link(nc.vector.tensor_scalar(expert_f[:, :], expert_f[:, :], float(E_R - 1), None, ALU.min))
            nc.vector.memset(prev_expert[:, 0:1], 0)
            nc.vector.tensor_copy(prev_expert[:, 1:], expert_f[:, 0:SLOT_TILES - 1])
            link(nc.vector.tensor_copy(tile_expert[:, :], expert_f[:, :]))

            for n in range(CHUNKS):
                ring = n % 2
                if n >= 2:
                    dve.wait_ge(hot_used, n - 1)
                nc.vector.tensor_tensor(in_tile[:, ring, :, :],
                                        tile_iota_h[:, :].unsqueeze(1).broadcast_to([QW, CHUNK, SLOT_TILES]),
                                        against(chunk_of(part_h[:, 1, :, :], n), SLOT_TILES), ALU.is_equal)\
                    .then_inc(in_tile_ready, 1)
                nc.vector.tensor_tensor(row_hot[:, ring, :, :], slot_iota_h[:, :].unsqueeze(1).broadcast_to([QW, CHUNK, P]),
                                        against(chunk_of(part_h[:, 0, :, :], n), P), ALU.is_equal).then_inc(row_ready, 1)

            dve.wait_ge(hot_used, CHUNKS)
            link(nc.vector.tensor_copy(table_low[:, :], table[:, SLOT_TILES:2 * SLOT_TILES]))
            link(nc.vector.scalar_tensor_tensor(slot_token[:, :], table[:, 0:SLOT_TILES], float(QW), table_low[:, :],
                                                ALU.mult, ALU.add))

        @block.tensor
        def _(pe):
            pe.wait_ge(consts3, CONSTS)
            pe.wait_ge(picks_ready, 1)
            flat = any_pick[:, :, :].rearrange("p t e -> p (t e)")
            nc.tensor.matmul(counts[:, :], ones[:, :], flat, start=True, stop=True).then_inc(counted, 1)
            nc.tensor.matmul(earlier[:, :], before[:, :], flat, start=True, stop=True).then_inc(counted, 1)
            for n in range(CHUNKS):
                for ready in (row_ready, by_tile_ready, by_row_ready):
                    pe.wait_ge(ready, n + 1)
                for a in range(CHUNK):
                    ins = nc.tensor.matmul(table[:, 0:2 * SLOT_TILES], row_hot[:, n % 2, a, :],
                                           tile_hot[0:QW, n % 2, a, :, :].rearrange("p k q -> p (k q)"),
                                           start=(n == 0 and a == 0), stop=(n == CHUNKS - 1 and a == CHUNK - 1))
                ins.then_inc(hot_used, 1)


def routed_experts(nc, xn_rows, y_slots, gu_sb, d_sb, ident2, slot_token, tile_expert, prev_expert, routed_in):
    es = ExitStack()
    with es:
        def sb(name, shape, dt=F32):
            return es.enter_context(nc.sbuf_tensor(name, shape, dt))

        def ps(name):
            return es.enter_context(nc.psum_tensor(name, [P, 512], F32))

        def sem(name):
            return es.enter_context(nc.semaphore(name))

        STEPS = SLOT_TILES // ASTEP
        gather_at = sb("gather_at", [P, ASTEP], I32)
        xg = sb("xg", [P, ASTEP, D])
        xg_t = sb("xg_t", [P, 2, DC, P])
        silu_g = sb("silu_g", [P, 2, MID])
        hid2 = sb("hid2", [P, 2, MID])
        hid_t2 = sb("hid_t2", [P, 2, P])
        y_sb = sb("y_sb", [P, ASTEP, D])
        spare = sb("spare", [P, 8])
        gu_ps = [ps(f"gu_ps{i}") for i in range(2)]
        turn_x = [ps(f"turn_x{i}") for i in range(2)]
        turn_h = ps("turn_h")
        y_bank = [ps(f"y_bank{i}") for i in range(2)]

        spare_set = sem("spare_set")
        index_ready = sem("index_ready")
        gathered = [sem(f"gathered{k}") for k in range(ASTEP)]
        x_turned = sem("x_turned")
        xg_t_ready = sem("xg_t_ready")
        gu_done = sem("gu_done")
        silu2_done = sem("silu2_done")
        hid2_done = sem("hid2_done")
        h_turned = sem("h_turned")
        hid_t_ready = sem("hid_t_ready")
        y_done2 = sem("y_done2")
        y_copied = sem("y_copied")
        y_stored = [sem(f"y_stored{k}") for k in range(ASTEP)]

        block = es.enter_context(nc.Block())

        def loop(engine, step):
            step(0, True, False)
            with engine.Fori(1, STEPS - 1) as i:
                step(i, False, False)
            step(STEPS - 1, False, True)

        @block.gpsimd
        def _(pool):
            pool.memset(spare[:, :], 0.0).then_inc(spare_set, 1)
            pool.wait_ge(spare_set, 1)

            def take_waits(n):
                nc.gpsimd.tensor_tensor(spare[:, n:n + 1], spare[:, 7:8], spare[:, 7:8], ALU.add).then_inc(spare_set, 1)

            def step(i, first, last):
                if not first:
                    for k in range(ASTEP):
                        pool.wait_ge(gathered[k], 16 * i)
                    pool.wait_ge(spare_set, 1 + (i - 1) * (ASTEP + 2))
                    take_waits(ASTEP)
                nc.gpsimd.tensor_copy(gather_at[:, :], slot_token[:, bass.ds(i * ASTEP, ASTEP)]).then_inc(index_ready, 1)
                pool.wait_ge(index_ready, i + 1)
                if not first:
                    take_waits(ASTEP + 1)
                for k in range(ASTEP):
                    if not first:
                        pool.wait_ge(x_turned, (i - 1) * ASTEP + k + 1)
                        take_waits(k)
                    nc.gpsimd.indirect_dma_start(xg[:, k, :], None, xn_rows,
                                                 bass.IndirectOffsetOnAxis(ap=gather_at[:, k:k + 1], axis=0))\
                        .then_inc(gathered[k], 16)

            step(0, True, False)
            with pool.Fori(1, STEPS) as i:
                step(i, False, False)

        @block.sync
        def _(sp):
            with sp.Fori(0, STEPS) as i:
                for k in range(ASTEP):
                    sp.wait_ge(y_copied, i * ASTEP + k + 1)
                    sp.dma_start(y_slots[bass.ds((i * ASTEP + k) * P, P), :], y_sb[:, k, :]).then_inc(y_stored[k], 16)
            for k in range(ASTEP):
                sp.wait_ge(y_stored[k], 16 * STEPS)

        @block.scalar
        def _(act):
            def copy_y(q, k, i, first):
                act.wait_ge(y_done2, q + 1)
                if not first:
                    act.wait_ge(y_stored[k], 16 * i)
                act.activation(y_sb[:, k, :], y_bank[k % 2][:, :], ACT.Copy).then_inc(y_copied, 1)

            def step(i, first, last):
                for k in range(ASTEP):
                    q = i * ASTEP + k
                    act.wait_ge(gu_done, q + 1)
                    if not (first and k < 2):
                        act.wait_ge(hid2_done, q - 1)
                    act.activation(silu_g[:, k % 2, :], gu_ps[k % 2][:, 0:MID], ACT.Silu).then_inc(silu2_done, 1)
                    if k:
                        copy_y(q - 1, k - 1, i, first)
                    elif not first:
                        copy_y(q - 1, ASTEP - 1, i - 1, isinstance(i, int) and i == 1)
                if last:
                    copy_y(SLOT_TILES - 1, ASTEP - 1, i, False)

            step(0, True, False)
            step(1, False, False)
            with act.Fori(2, STEPS - 1) as i:
                step(i, False, False)
            step(STEPS - 1, False, True)

        @block.vector
        def _(dve):
            def copy_x(q, k, early):
                dve.wait_ge(x_turned, q + 1)
                if not early:
                    dve.wait_ge(gu_done, q - 1)
                nc.vector.tensor_copy(xg_t[:, k % 2, :, :].rearrange("p c q -> p (c q)"), turn_x[k % 2][:, :])\
                    .then_inc(xg_t_ready, 1)

            def copy_h(q, k, early):
                dve.wait_ge(h_turned, q + 1)
                if not early:
                    dve.wait_ge(y_done2, q - 1)
                nc.vector.tensor_copy(hid_t2[:, k % 2, :], turn_h[:, 0:P]).then_inc(hid_t_ready, 1)

            def step(i, first, last):
                for k in range(ASTEP):
                    q = i * ASTEP + k
                    if not (first and k == 0):
                        copy_h(q - 1, (k - 1) % 2, first and k < 3)
                    if not (last and k == ASTEP - 1):
                        copy_x(q + 1, k + 1, first and k < 1)
                    dve.wait_ge(silu2_done, q + 1)
                    if not (first and k < 2):
                        dve.wait_ge(h_turned, q - 1)
                    nc.vector.tensor_tensor(hid2[:, k % 2, :], silu_g[:, k % 2, :], gu_ps[k % 2][:, MID:GATE_UP], ALU.mult)\
                        .then_inc(hid2_done, 1)

            copy_x(0, 0, True)
            loop(dve, step)
            copy_h(SLOT_TILES - 1, ASTEP - 1, False)

        @block.tensor
        def _(pe):
            def turn(q, k, i, early):
                pe.wait_ge(gathered[k], 16 * i + 16)
                if not early:
                    pe.wait_ge(xg_t_ready, q - 1)
                for c in range(DC):
                    ins = nc.tensor.transpose(turn_x[k % 2][:, c * P:(c + 1) * P], xg[:, k, c * P:(c + 1) * P], ident2[:, :])
                ins.then_inc(x_turned, 1)

            def turn_hidden(q, k, early):
                pe.wait_ge(hid2_done, q + 1)
                if not early:
                    pe.wait_ge(hid_t_ready, q)
                nc.tensor.transpose(turn_h[:, 0:P], hid2[:, k % 2, :], ident2[:, :]).then_inc(h_turned, 1)

            def gate_up(q, k, expert, chunks):
                for c in chunks:
                    ins = nc.tensor.matmul(gu_ps[k % 2][:, 0:GATE_UP], xg_t[:, k % 2, c, :],
                                           gu_sb[:, bass.ds(expert, 1), c, :].rearrange("p a m -> p (a m)"),
                                           start=(c == 0), stop=(c == DC - 1))
                if c == DC - 1:
                    ins.then_inc(gu_done, 1)

            def down(q, k, expert, early):
                pe.wait_ge(hid_t_ready, q + 1)
                if not early:
                    pe.wait_ge(y_copied, q - 1)
                nc.tensor.matmul(y_bank[k % 2][:, :], hid_t2[:, k % 2, :],
                                 d_sb[:, bass.ds(expert, 1), :].rearrange("p a n -> p (a n)"),
                                 start=True, stop=True).then_inc(y_done2, 1)

            def expert_of(table, q):
                return pe.value_load(table[0:1, bass.ds(q, 1)], min_val=0, max_val=E_R - 1)

            def step(i, first, last):
                expert = expert_of(tile_expert, i * ASTEP)
                for k in range(ASTEP):
                    q = i * ASTEP + k
                    pe.wait_ge(xg_t_ready, q + 1)
                    if not (first and k < 2):
                        pe.wait_ge(hid2_done, q - 1)
                    gate_up(q, k, expert, (0, 1))
                    if not (first and k == 0):
                        turn_hidden(q - 1, (k - 1) % ASTEP, first and k == 1)
                    if k == 0 and not first:
                        before = expert_of(prev_expert, q)
                    gate_up(q, k, expert, (2, 3))
                    after = expert_of(tile_expert, q + 1) if k < ASTEP - 1 else None
                    if k < ASTEP - 1:
                        turn(q + 1, k + 1, i, first and k == 0)
                    elif not last:
                        turn(q + 1, 0, i + 1, False)
                    if not (first and k == 0):
                        down(q - 1, (k - 1) % ASTEP, before, first and k < 3)
                    before, expert = expert, after
                if last:
                    turn_hidden(SLOT_TILES - 1, ASTEP - 1, False)
                    down(SLOT_TILES - 1, ASTEP - 1, before, False)

            pe.wait_ge(routed_in, 32)
            turn(0, 0, 0, True)
            loop(pe, step)


def shared_and_combine(nc, x1, xn_cols, y_slots, shared, tanh_g2, weight, slot_i, out):
    es = ExitStack()
    with es:
        def sb(name, shape, dt=F32):
            return es.enter_context(nc.sbuf_tensor(name, shape, dt))

        def ps(name):
            return es.enter_context(nc.psum_tensor(name, [P, 512], F32))

        def sem(name):
            return es.enter_context(nc.semaphore(name))

        SC = MID_S // P
        xc = sb("xc", [P, DC, GTOK])
        xc_hi = sb("xc_hi", [P, DC, GTOK], F32R)
        xc_lo = sb("xc_lo", [P, DC, GTOK], F32R)
        silu_s = sb("silu_s", [P, 2, GTOK])
        hid_s = sb("hid_s", [P, 2, GTOK])
        hid_hi = sb("hid_hi", [P, SC, GTOK], F32R)
        hid_lo = sb("hid_lo", [P, SC, GTOK], F32R)
        total = sb("total", [QW, GT, D])
        routed = sb("routed", [QW, GT, TOP, D])
        gather_at2 = sb("gather_at2", [QW, TOP, GT], I32)
        spare2 = sb("spare2", [P, 8])
        free2 = sb("free2", [P, 4])
        gate_bank = [ps(f"gate_bank{i}") for i in range(2)]
        up_bank = [ps(f"up_bank{i}") for i in range(2)]
        down_bank = [ps(f"down_bank{t}") for t in range(GT)]

        xc_in = sem("xc_in")
        xc_ready = sem("xc_ready")
        chain4 = sem("chain4")
        gate_done2 = sem("gate_done2")
        up_done2 = sem("up_done2")
        silu_done3 = sem("silu_done3")
        hid_done3 = sem("hid_done3")
        parts_ready = sem("parts_ready")
        down_done = sem("down_done")
        total_in = sem("total_in")
        spare_set2 = sem("spare_set2")
        index_ready2 = sem("index_ready2")
        routed_got = [sem(f"routed_got{t}") for t in range(GT)]
        bank_read = sem("bank_read")
        routed_used = sem("routed_used")
        out_stored = sem("out_stored")
        PRE4 = {"hid_done3": 2, "down_done": 1, "bank_read": GT}

        block = es.enter_context(nc.Block())

        def loop(engine, step):
            with engine.Fori(0, GROUPS - 1) as g:
                step(g, False)
            step(GROUPS - 1, True)

        @block.sync
        def _(sp):
            def load_cols(g):
                for k in range(BATCHES):
                    sp.dma_start(xc[:, :, k * L:(k + 1) * L],
                                 xn_cols[bass.ds(g * BATCHES + k, 1), :, :, :].rearrange("a p c q -> p (a c) q"))\
                        .then_inc(xc_in, 16)

            def load_total(g):
                sp.dma_start(total[:, :, :], x1[bass.ds(g * GTOK, GTOK), :].rearrange("(t p) d -> p t d", p=QW))\
                    .then_inc(total_in, 16)

            load_cols(0)
            load_total(0)

            def step(g, last):
                if not last:
                    sp.wait_ge(xc_ready, g + 1)
                    load_cols(g + 1)
                for t in range(GT):
                    sp.wait_ge(bank_read, PRE4["bank_read"] + GT * g + t + 1)
                    sp.dma_start(out[bass.ds(g * GTOK + t * QW, QW), :], total[:, t, :]).then_inc(out_stored, 16)
                if not last:
                    sp.wait_ge(out_stored, 16 * (GT * g + GT))
                    load_total(g + 1)

            loop(sp, step)
            sp.wait_ge(out_stored, 16 * GT * GROUPS)

        @block.gpsimd
        def _(pool):
            pool.memset(spare2[:, :], 0.0).then_inc(spare_set2, 1)
            pool.wait_ge(spare_set2, 1)

            def take_waits(n):
                nc.gpsimd.tensor_tensor(spare2[:, n:n + 1], spare2[:, 7:8], spare2[:, 7:8], ALU.add).then_inc(spare_set2, 1)

            def step(g, first):
                if not first:
                    for t in range(GT):
                        pool.wait_ge(routed_got[t], 32 * g)
                    pool.wait_ge(spare_set2, 1 + (g - 1) * (GT + 2))
                    take_waits(GT)
                nc.gpsimd.tensor_copy(gather_at2[:, :, :], slot_i[:, :, bass.ds(g * GT, GT)]).then_inc(index_ready2, 1)
                pool.wait_ge(index_ready2, g + 1)
                if not first:
                    take_waits(GT + 1)
                for t in range(GT):
                    if not first:
                        pool.wait_ge(routed_used, GT * (g - 1) + t + 1)
                        take_waits(t)
                    for k in range(TOP):
                        nc.gpsimd.indirect_dma_start(routed[:, t, k, :], None, y_slots,
                                                     bass.IndirectOffsetOnAxis(ap=gather_at2[:, k, t:t + 1], axis=0))\
                            .then_inc(routed_got[t], 16)

            step(0, True)
            with pool.Fori(1, GROUPS) as g:
                step(g, False)

        @block.scalar
        def _(act):
            def step(g, last):
                for j in range(SC):
                    act.wait_ge(gate_done2, SC * g + j + 1)
                    act.wait_ge(hid_done3, PRE4["hid_done3"] + SC * g + j - 1)
                    act.activation(silu_s[:, j % 2, :], gate_bank[j % 2][:, 0:GTOK], ACT.Silu).then_inc(silu_done3, 1)

            loop(act, step)

        @block.vector
        def _(dve):
            links = [0]

            def link(ins, base):
                links[0] += 1
                ins.then_inc(chain4, 1)
                dve.wait_ge(chain4, base + links[0])

            for n, (s, name) in enumerate(((hid_done3, "hid_done3"), (down_done, "down_done"), (bank_read, "bank_read"))):
                nc.vector.memset(free2[:, n:n + 1], 0.0).then_inc(s, PRE4[name])

            def split_cols(n, base):
                dve.wait_ge(xc_in, 16 * BATCHES * (n + 1))
                link(nc.vector.tensor_copy(xc_hi[:, :, :], xc[:, :, :]), base)
                nc.vector.tensor_tensor(xc_lo[:, :, :], xc[:, :, :], xc_hi[:, :, :].bitcast(F32), ALU.subtract)\
                    .then_inc(xc_ready, 1)

            split_cols(0, 0)
            FIRST, LINKS = links[0], SC + 2

            def step(g, last):
                base = FIRST + g * LINKS
                links[0] = 0
                for j in range(SC):
                    dve.wait_ge(silu_done3, SC * g + j + 1)
                    dve.wait_ge(up_done2, SC * g + j + 1)
                    nc.vector.tensor_tensor(hid_s[:, j % 2, :], silu_s[:, j % 2, :], up_bank[j % 2][:, 0:GTOK], ALU.mult)\
                        .then_inc(hid_done3, 1)
                    dve.wait_ge(hid_done3, PRE4["hid_done3"] + SC * g + j + 1)
                    dve.wait_ge(down_done, PRE4["down_done"] + GT * g)
                    link(nc.vector.tensor_copy(hid_hi[:, j, :], hid_s[:, j % 2, :]), base)
                    nc.vector.tensor_tensor(hid_lo[:, j, :], hid_s[:, j % 2, :], hid_hi[:, j, :].bitcast(F32), ALU.subtract)\
                        .then_inc(parts_ready, 1)
                if not last:
                    split_cols(g + 1, base)
                dve.wait_ge(total_in, 16 * g + 16)
                for k in range(TOP):
                    for t in range(GT):
                        dve.wait_ge(routed_got[t], 32 * g + 32)
                        ins = nc.vector.scalar_tensor_tensor(total[:, t, :], routed[:, t, k, :],
                                                             weight[:, k, bass.ds(g * GT + t, 1)], total[:, t, :],
                                                             ALU.mult, ALU.add)
                        if k == TOP - 1:
                            ins.then_inc(routed_used, 1)
                    if k < TOP - 1:
                        link(ins, base)
                for t in range(GT):
                    dve.wait_ge(routed_used, GT * g + t + 1)
                    dve.wait_ge(down_done, PRE4["down_done"] + GT * g + t + 1)
                    nc.vector.scalar_tensor_tensor(total[:, t, :], down_bank[t][0:QW, :], tanh_g2[0:QW, :], total[:, t, :],
                                                   ALU.mult, ALU.add).then_inc(bank_read, 1)
                return links[0]

            with dve.Fori(0, GROUPS - 1) as g:
                assert step(g, False) == LINKS
            step(GROUPS - 1, True)

        @block.tensor
        def _(pe):
            def step(g, last):
                pe.wait_ge(xc_ready, g + 1)
                for j in range(SC):
                    pe.wait_ge(hid_done3, PRE4["hid_done3"] + SC * g + j - 1)
                    for bank, done, at in ((gate_bank, gate_done2, j * P), (up_bank, up_done2, MID_S + j * P)):
                        for d in range(DC):
                            for n, (wp, xp) in enumerate(((shared["gu_hi"], xc_hi), (shared["gu_hi"], xc_lo),
                                                          (shared["gu_lo"], xc_hi))):
                                ins = nc.tensor.matmul(bank[j % 2][:, 0:GTOK], wp[:, d, at:at + P], xp[:, d, :],
                                                       start=(d == 0 and n == 0), stop=(d == DC - 1 and n == 2))
                        ins.then_inc(done, 1)
                for j in range(SC):
                    pe.wait_ge(parts_ready, SC * g + j + 1)
                    for t in range(GT):
                        if j == 0:
                            pe.wait_ge(bank_read, PRE4["bank_read"] + GT * (g - 1) + t + 1)
                        for n, (hp, wp) in enumerate(((hid_hi, "d_hi"), (hid_hi, "d_lo"), (hid_lo, "d_hi"))):
                            ins = nc.tensor.matmul(down_bank[t][0:QW, :], hp[:, j, t * QW:(t + 1) * QW], shared[wp][:, j, :],
                                                   start=(j == 0 and n == 0), stop=(j == SC - 1 and n == 2))
                        if j == SC - 1:
                            ins.then_inc(down_done, 1)

            loop(pe, step)


def kernel(**inputs):
    import numpy as np
    import concourse.bacc as bacc
    from concourse.bass_utils import run_bass_kernel_spmd as run

    a = {k: np.asarray(v) for k, v in inputs.items()}
    laid = {
        "x": a["x"],
        "ctx_t": a["ctx_1024"].transpose(0, 2, 1).reshape(B, DC, P, S).transpose(0, 2, 1, 3),
        "ctxb": a["ctxb_2048x32"],
        "g_xattn": a["g_xattn"],
        "wq": a["L0_xattn_Wq"], "bq": a["L0_xattn_bq"].reshape(DC, P).T,
        "wk": a["L0_xattn_Wk"], "bk": a["L0_xattn_bk"].reshape(DC, P).T,
        "wv": a["L0_xattn_Wv"], "bv": a["L0_xattn_bv"].reshape(DC, P).T,
        "wo": a["L0_xattn_Wo"], "bo": a["L0_xattn_bo"],
        "g_ffn": a["g_ffn"],
        "router_w": a["L0_ffn_router_w"],
        "w_gu": np.concatenate([a["L0_ffn_wg_r"], a["L0_ffn_wu_r"]], axis=2)
        .reshape(E_R, DC, P, 2 * MID).transpose(2, 0, 1, 3).reshape(P, -1),
        "w_d": a["L0_ffn_wd_r"],
        "ws_gu": np.stack([a["L0_ffn_wg_s"], a["L0_ffn_wu_s"]]).transpose(2, 0, 1, 3)
        .reshape(DC, P, 2 * MID_S).transpose(1, 0, 2),
        "ws_d": a["L0_ffn_wd_s"].reshape(MID_S, D),
    }
    nc = bacc.Bacc("TRN2", target_bir_lowering=False, num_devices=1)
    arrays, dram = {}, {}
    for name, value in laid.items():
        arrays[f"in_{name}"] = np.ascontiguousarray(value)
        dram[name] = nc.dram_tensor(f"in_{name}", value.shape, mybir.dt.from_np(value.dtype), kind="ExternalInput").ap()
    out = nc.dram_tensor("out", (T, D), F32, kind="ExternalOutput").ap()
    program(nc, out=out, **dram)
    result = run(nc, [arrays], core_ids=[0])
    return result.results[0]["out"].reshape(B, L, D)


def program(nc, x, ctx_t, ctxb, g_xattn, wq, bq, wk, bk, wv, bv, wo, bo,
            g_ffn, router_w, w_gu, w_d, ws_gu, ws_d, out):
    x1 = nc.dram_tensor("x1", (T, D), F32, kind="Internal").ap()
    xn_rows = nc.dram_tensor("xn_rows", (T, D), F32, kind="Internal").ap()
    xn_cols = nc.dram_tensor("xn_cols", (B, P, DC, L), F32, kind="Internal").ap()
    logits = nc.dram_tensor("logits", (QW, B * QT, E_R), F32, kind="Internal").ap()
    attention_phase(nc, x, ctx_t, ctxb, g_xattn, wq, bq, wk, bk, wv, bv, wo, bo, router_w, x1, xn_rows, xn_cols, logits)
    experts_phase(nc, x1, xn_rows, xn_cols, logits, g_ffn, w_gu, w_d, ws_gu, ws_d, out)
```
